# Optimizing a Trainium2 kernel written in Bass

```python
import numpy as np
import jax
import jax.numpy as jnp

def _softmax(x, axis=-1):
    return jax.nn.softmax(x, axis=axis)

def _gelu(x):
    return jax.nn.gelu(x, approximate=True)

def _silu(x):
    return jax.nn.silu(x)

def _sigmoid(x):
    return jax.nn.sigmoid(x)

def _layernorm(x, axis=-1, eps=1e-05):
    m = jnp.mean(x, axis=axis, keepdims=True)
    v = jnp.var(x, axis=axis, keepdims=True)
    return (x - m) / jnp.sqrt(v + eps)

def _scatter_add(tgt, idx, src, axis=0):
    return tgt.at[idx].add(src)

def _segment_sum(src, seg, n):
    return jax.ops.segment_sum(src, seg, n)
kernel_name = 'mk_gnn_ffn_d1_gnn_r8_1f9429'

def setup_inputs(seed: int=0):
    np.random.seed(seed)
    _w = jnp.asarray

    def _rec_inputs():
        import jax
        import jax.numpy as jnp
        _gk = jax.random.key(seed)
        x = -8.776e-05 + 1 * jax.random.normal(jax.random.fold_in(_gk, 1), (2500, 256), jnp.float32)
        _s = jax.random.randint(jax.random.fold_in(_gk, 2), (20000,), 0, 2500, jnp.int32)
        _d = jax.random.randint(jax.random.fold_in(_gk, 3), (20000,), 0, 2500, jnp.int32)
        _loop = jnp.arange(2500, dtype=jnp.int32)
        src = jnp.concatenate([_s, _d, _loop])
        dst = jnp.concatenate([_d, _s, _loop])
        _o = jnp.argsort(dst, stable=True)
        src = src[_o]
        dst = dst[_o]
        return (x, src, dst)
    x, src, dst = _rec_inputs()

    def _L0_gnn_setup():
        import jax, jax.numpy as jnp
        import numpy as np
        N = 2500
        E = 40000
        IN = 256
        H = 4
        C = 64
        D = H * C
        LN_EPS = 1e-05
        key = jax.random.key(seed)
        ks = jax.random.split(key, 8)
        w = lambda k, sh: jax.random.normal(k, sh, jnp.float32) * 0.05
        return {'x': jax.random.normal(ks[0], (N, IN), jnp.float32), 'edge_index': jax.random.randint(ks[1], (2, E), 0, N, dtype=jnp.int32), 'Wq': w(ks[2], (IN, D)), 'bq': jnp.zeros((D,), jnp.float32), 'Wk': w(ks[3], (IN, D)), 'bk': jnp.zeros((D,), jnp.float32), 'Wv': w(ks[4], (IN, D)), 'bv': jnp.zeros((D,), jnp.float32), 'Wskip': w(ks[5], (IN, D)), 'bskip': jnp.zeros((D,), jnp.float32), 'gamma': jnp.ones((D,), jnp.float32), 'beta_ln': jnp.zeros((D,), jnp.float32)}
    _L0_gnn_all = _L0_gnn_setup()
    _L0_gnn_in = {k: v for k, v in _L0_gnn_all.items() if k in ('Wq', 'bq', 'Wk', 'bk', 'Wv', 'bv', 'Wskip', 'bskip', 'gamma', 'beta_ln')}
    del _L0_gnn_all

    def _L0_ffn_setup():
        import jax, jax.numpy as jnp
        import numpy as np
        B, N, D = (16, 512, 256)
        NUM_EXPERTS, TOP_K, HEADS = (4, 2, 4)
        N_EDGES = 131072
        LN_EPS = 1e-05

        def _layernorm(x, g, b):
            mu = x.mean(-1, keepdims=True)
            var = ((x - mu) ** 2).mean(-1, keepdims=True)
            return (x - mu) * jax.lax.rsqrt(var + LN_EPS) * g + b

        def _forward(x, edge_index, W_gat, att_src, att_dst, b_gat, ln_gamma, ln_beta, W1, b1, W2, b2):
            Bc, Nc, Dc = x.shape
            M = Bc * Nc
            x_flat = x.reshape(M, Dc)
            h = (x_flat @ W_gat).reshape(M, HEADS, NUM_EXPERTS)
            loops = jnp.arange(M, dtype=edge_index.dtype)
            src = jnp.concatenate([edge_index[0], loops])
            dst = jnp.concatenate([edge_index[1], loops])
            a_src = (h * att_src).sum(-1)
            a_dst = (h * att_dst).sum(-1)
            e = jax.nn.leaky_relu(a_src[src] + a_dst[dst], negative_slope=0.2)
            e_max = jax.ops.segment_max(e, dst, num_segments=M)
            ee = jnp.exp(e - e_max[dst])
            denom = jax.ops.segment_sum(ee, dst, num_segments=M)
            alpha = ee / (denom[dst] + 1e-16)
            msg = h[src] * alpha[:, :, None]
            agg = jax.ops.segment_sum(msg, dst, num_segments=M).reshape(M, HEADS * NUM_EXPERTS) + b_gat
            scores = _layernorm(agg, ln_gamma, ln_beta).reshape(M, HEADS, NUM_EXPERTS).mean(1)
            scores = scores.reshape(Bc, Nc, NUM_EXPERTS)
            topk_s, topk_i = jax.lax.top_k(scores, TOP_K)
            w = jax.nn.softmax(topk_s, axis=-1)
            out = jnp.zeros_like(x)
            for ei in range(NUM_EXPERTS):
                g = jnp.where(topk_i == ei, w, 0.0).sum(-1)
                hh = jax.nn.gelu(x @ W1[ei] + b1[ei], approximate=False)
                out = out + g[..., None] * (hh @ W2[ei] + b2[ei])
            return out
        key = jax.random.key(seed)
        ks = jax.random.split(key, 8)
        s = 0.05
        return {'x': jax.random.normal(ks[0], (B, N, D), jnp.float32), 'W_gat': jax.random.normal(ks[1], (D, HEADS * NUM_EXPERTS), jnp.float32) * s, 'att_src': jax.random.normal(ks[2], (HEADS, NUM_EXPERTS), jnp.float32) * s, 'att_dst': jax.random.normal(ks[3], (HEADS, NUM_EXPERTS), jnp.float32) * s, 'b_gat': jnp.zeros((HEADS * NUM_EXPERTS,), jnp.float32), 'ln_gamma': jnp.ones((HEADS * NUM_EXPERTS,), jnp.float32), 'ln_beta': jnp.zeros((HEADS * NUM_EXPERTS,), jnp.float32), 'W1': jax.random.normal(ks[4], (NUM_EXPERTS, D, 2 * D), jnp.float32) * s, 'b1': jnp.zeros((NUM_EXPERTS, 2 * D), jnp.float32), 'W2': jax.random.normal(ks[5], (NUM_EXPERTS, 2 * D, D), jnp.float32) * s, 'b2': jnp.zeros((NUM_EXPERTS, D), jnp.float32), 'edge_index': jax.random.randint(ks[6], (2, N_EDGES), 0, B * N, jnp.int32)}
    _L0_ffn_all = _L0_ffn_setup()
    _L0_ffn_in = {k: v for k, v in _L0_ffn_all.items() if k in ('W_gat', 'att_src', 'att_dst', 'b_gat', 'ln_gamma', 'ln_beta', 'W1', 'b1', 'W2', 'b2', 'edge_index')}
    del _L0_ffn_all
    return {'x': x, 'src': src, 'dst': dst, 'L0_gnn_Wq': _L0_gnn_in['Wq'], 'L0_gnn_bq': _L0_gnn_in['bq'], 'L0_gnn_Wk': _L0_gnn_in['Wk'], 'L0_gnn_bk': _L0_gnn_in['bk'], 'L0_gnn_Wv': _L0_gnn_in['Wv'], 'L0_gnn_bv': _L0_gnn_in['bv'], 'L0_gnn_Wskip': _L0_gnn_in['Wskip'], 'L0_gnn_bskip': _L0_gnn_in['bskip'], 'L0_gnn_gamma': _L0_gnn_in['gamma'], 'L0_gnn_beta_ln': _L0_gnn_in['beta_ln'], 'L0_ffn_W_gat': _L0_ffn_in['W_gat'], 'L0_ffn_att_src': _L0_ffn_in['att_src'], 'L0_ffn_att_dst': _L0_ffn_in['att_dst'], 'L0_ffn_b_gat': _L0_ffn_in['b_gat'], 'L0_ffn_ln_gamma': _L0_ffn_in['ln_gamma'], 'L0_ffn_ln_beta': _L0_ffn_in['ln_beta'], 'L0_ffn_W1': _L0_ffn_in['W1'], 'L0_ffn_b1': _L0_ffn_in['b1'], 'L0_ffn_W2': _L0_ffn_in['W2'], 'L0_ffn_b2': _L0_ffn_in['b2'], 'L0_ffn_edge_index': _L0_ffn_in['edge_index']}

def reference(x, src, dst, L0_gnn_Wq, L0_gnn_bq, L0_gnn_Wk, L0_gnn_bk, L0_gnn_Wv, L0_gnn_bv, L0_gnn_Wskip, L0_gnn_bskip, L0_gnn_gamma, L0_gnn_beta_ln, L0_ffn_W_gat, L0_ffn_att_src, L0_ffn_att_dst, L0_ffn_b_gat, L0_ffn_ln_gamma, L0_ffn_ln_beta, L0_ffn_W1, L0_ffn_b1, L0_ffn_W2, L0_ffn_b2, L0_ffn_edge_index):
    import jax
    import jax.numpy as jnp

    def _L0_gnn_ref(x, edge_index, Wq, bq, Wk, bk, Wv, bv, Wskip, bskip, gamma, beta_ln):
        import jax, jax.numpy as jnp
        import numpy as np
        N = 2500
        E = 40000
        IN = 256
        H = 4
        C = 64
        D = H * C
        LN_EPS = 1e-05
        src = edge_index[0]
        dst = edge_index[1]
        q = (x @ Wq + bq).reshape(N, H, C)
        k = (x @ Wk + bk).reshape(N, H, C)
        v = (x @ Wv + bv).reshape(N, H, C)
        scale = 1.0 / jnp.sqrt(jnp.float32(C))
        alpha = jnp.einsum('ehc,ehc->eh', q[dst], k[src]) * scale
        m = jax.ops.segment_max(alpha, dst, num_segments=N)
        m = jnp.where(jnp.isfinite(m), m, 0.0)
        a = jnp.exp(alpha - m[dst])
        denom = jax.ops.segment_sum(a, dst, num_segments=N)
        a = a / (denom[dst] + 1e-16)
        msg = a[:, :, None] * v[src]
        agg = jax.ops.segment_sum(msg, dst, num_segments=N)
        out = agg.reshape(N, D) + (x @ Wskip + bskip)
        out = jax.nn.gelu(out, approximate=False)
        mu = jnp.mean(out, axis=-1, keepdims=True)
        var = jnp.var(out, axis=-1, keepdims=True)
        out = (out - mu) * jax.lax.rsqrt(var + LN_EPS) * gamma + beta_ln
        return out

    def _L0_ffn_ref(x, W_gat, att_src, att_dst, b_gat, ln_gamma, ln_beta, W1, b1, W2, b2, edge_index):
        import jax, jax.numpy as jnp
        import numpy as np
        B, N, D = (16, 512, 256)
        NUM_EXPERTS, TOP_K, HEADS = (4, 2, 4)
        N_EDGES = 131072
        LN_EPS = 1e-05

        def _layernorm(x, g, b):
            mu = x.mean(-1, keepdims=True)
            var = ((x - mu) ** 2).mean(-1, keepdims=True)
            return (x - mu) * jax.lax.rsqrt(var + LN_EPS) * g + b

        def _forward(x, edge_index, W_gat, att_src, att_dst, b_gat, ln_gamma, ln_beta, W1, b1, W2, b2):
            Bc, Nc, Dc = x.shape
            M = Bc * Nc
            x_flat = x.reshape(M, Dc)
            h = (x_flat @ W_gat).reshape(M, HEADS, NUM_EXPERTS)
            loops = jnp.arange(M, dtype=edge_index.dtype)
            src = jnp.concatenate([edge_index[0], loops])
            dst = jnp.concatenate([edge_index[1], loops])
            a_src = (h * att_src).sum(-1)
            a_dst = (h * att_dst).sum(-1)
            e = jax.nn.leaky_relu(a_src[src] + a_dst[dst], negative_slope=0.2)
            e_max = jax.ops.segment_max(e, dst, num_segments=M)
            ee = jnp.exp(e - e_max[dst])
            denom = jax.ops.segment_sum(ee, dst, num_segments=M)
            alpha = ee / (denom[dst] + 1e-16)
            msg = h[src] * alpha[:, :, None]
            agg = jax.ops.segment_sum(msg, dst, num_segments=M).reshape(M, HEADS * NUM_EXPERTS) + b_gat
            scores = _layernorm(agg, ln_gamma, ln_beta).reshape(M, HEADS, NUM_EXPERTS).mean(1)
            scores = scores.reshape(Bc, Nc, NUM_EXPERTS)
            topk_s, topk_i = jax.lax.top_k(scores, TOP_K)
            w = jax.nn.softmax(topk_s, axis=-1)
            out = jnp.zeros_like(x)
            for ei in range(NUM_EXPERTS):
                g = jnp.where(topk_i == ei, w, 0.0).sum(-1)
                hh = jax.nn.gelu(x @ W1[ei] + b1[ei], approximate=False)
                out = out + g[..., None] * (hh @ W2[ei] + b2[ei])
            return out
        return _forward(x, edge_index, W_gat, att_src, att_dst, b_gat, ln_gamma, ln_beta, W1, b1, W2, b2)
    edge_index = jnp.stack([src, dst])
    x = x + _L0_gnn_ref(_layernorm(x, axis=-1), edge_index, L0_gnn_Wq, L0_gnn_bq, L0_gnn_Wk, L0_gnn_bk, L0_gnn_Wv, L0_gnn_bv, L0_gnn_Wskip, L0_gnn_bskip, L0_gnn_gamma, L0_gnn_beta_ln)
    x = x + _L0_ffn_ref(_layernorm(x, axis=-1)[None], L0_ffn_W_gat, L0_ffn_att_src, L0_ffn_att_dst, L0_ffn_b_gat, L0_ffn_ln_gamma, L0_ffn_ln_beta, L0_ffn_W1, L0_ffn_b1, L0_ffn_W2, L0_ffn_b2, L0_ffn_edge_index)[0]
    return x

_drawn_inputs = setup_inputs


def setup_inputs(seed=0):
    import zlib

    import numpy as np

    out = dict(_drawn_inputs(seed))
    spreads = {'L0_gnn_bq': (0.0, 0.383),
     'L0_gnn_bk': (0.0, 0.8),
     'L0_gnn_bv': (0.0, 0.1),
     'L0_gnn_bskip': (0.0, 0.1),
     'L0_gnn_gamma': (1.0, 0.2),
     'L0_gnn_beta_ln': (0.0, 0.1),
     'L0_ffn_b_gat': (0.0, 0.1),
     'L0_ffn_ln_gamma': (1.0, 0.2),
     'L0_ffn_ln_beta': (0.0, 0.1),
     'L0_ffn_b1': (0.0, 0.1),
     'L0_ffn_b2': (0.0, 0.1)}
    factors = {'L0_ffn_att_src': 2.897, 'L0_ffn_att_dst': 4.455}
    for name, (base, spread) in spreads.items():
        noise = np.random.default_rng([zlib.crc32(name.encode()), seed]).standard_normal(out[name].shape)
        drawn = base * np.exp(spread * noise) if base else spread * noise
        out[name] = jnp.asarray(drawn.astype(out[name].dtype))
    for name, factor in factors.items():
        out[name] = (out[name] * factor).astype(out[name].dtype)
    return out
```

```python
from contextlib import ExitStack

import concourse.bass as bass
from concourse import mybir
from concourse.alu_op_type import AluOpType as ALU

F32 = mybir.dt.float32
BF16 = mybir.dt.bfloat16
I32 = mybir.dt.int32
U32 = mybir.dt.uint32
ACT = mybir.ActivationFunctionType
AX_X = mybir.AxisListType.X
ds = bass.ds

N = 2500
D = 256
H = 4
C = D // H
T = 125
NT = N // T
SEG = 500
NSEG = N // SEG
TPS = SEG // T
KC = D // 128
NEXP = 4
F = 512
FC = F // 128
LN_EPS = 1e-5
NEG = -1e30
NEG_FLOOR = -1e20
QSCALE = C ** -0.5

W = 4
PA, PB = 125, 128
EA, EB = 42500, 131072
LA, LB = W * PA, W * PB
GA, GB = EA // LA, EB // LB
EARLIER = 4096.0
DUMMY = N * N
ROWS = N + 1

BATCH = 5
STEPS = GA // BATCH
B_EARLY = (STEPS - 1) * BATCH
B_TILE0 = BATCH
B_TILE = (GB - B_EARLY - B_TILE0) // (NT - 1)
assert GA % BATCH == 0 and B_EARLY + B_TILE0 + B_TILE * (NT - 1) == GB
SLOTS = 2 * BATCH
assert B_TILE < SLOTS
SEG_ORDER = [1, 2, 3, 4, 0]


def build(nc, x, src_a, dst_a, Wq, bq, Wk, bk, Wv, bv, Wskip, bskip, gamma, beta, Wgat, att_src, att_dst,
          b_gat, g_gamma, g_beta, W1, b1, W2, b2, edge_index, out):
    ctx = ExitStack()
    with ctx:
        def sb(name, shape, dt=F32):
            return ctx.enter_context(nc.sbuf_tensor(name, shape, dt))

        def sem(name):
            return ctx.enter_context(nc.semaphore(name))

        table_a = nc.dram_tensor("table_a", [ROWS * N, 1], F32).ap()
        table_b = nc.dram_tensor("table_b", [ROWS * N, 1], F32).ap()
        keys_a = nc.dram_tensor("keys_a", [EA], F32).ap()
        keys_b = nc.dram_tensor("keys_b", [EB], F32).ap()
        s_rows = nc.dram_tensor("s_rows", [H, NT, T], F32).ap()

        ident = sb("ident", [128, 128])
        ones_row = sb("ones_row", [1, 128])
        slot_a = sb("slot_a", [128, W])
        slot_b = sb("slot_b", [128, W])
        order_a = sb("order_a", [128, W, LB], BF16)
        order_b = sb("order_b", [128, W, LB], BF16)
        eps = sb("eps", [128, 1])
        tiny = sb("tiny", [128, 1])
        KA = sb("KA", [128, GA * W])
        KB = sb("KB", [128, GB * W])
        keyrow = sb("keyrow", [128, SLOTS, LB])
        weight = sb("weight", [128, SLOTS, W])
        cell = sb("cell", [128, SLOTS, W], U32)
        shift = sb("shift", [128, W])
        moved = sb("moved", [128, W])
        X = sb("X", [128, NT, D])
        QK = sb("QK", [128, 2 * KC * N])
        VS = sb("VS", [128, 2 * NT * D])
        qT = QK[:, 0:KC * N].rearrange("p (k n) -> p k n", k=KC)
        kT = QK[:, KC * N:2 * KC * N].rearrange("p (k n) -> p k n", k=KC)
        S_all = QK[:, 0:H * N].rearrange("p (h n) -> p h n", h=H)
        V = VS[:, 0:NT * D].rearrange("p (t d) -> p t d", t=NT)
        SK = VS[:, NT * D:2 * NT * D].rearrange("p (t d) -> p t d", t=NT)
        w1_sb = VS[:, 0:NEXP * KC * F].rearrange("p (e k f) -> p e k f", e=NEXP, k=KC)
        b2_sb = VS[:, 2 * NT * D - NEXP * D:2 * NT * D].rearrange("p (e d) -> p e d", e=NEXP)
        w2_sb = VS[:, NEXP * KC * F:NEXP * KC * F + NEXP * FC * D].rearrange("p (e k d) -> p e k d", e=NEXP, k=FC)
        bvs = sb("bvs", [1, 2 * D])
        bqk = sb("bqk", [128, 2, KC])
        wg_sb = sb("wg_sb", [128, KC, 16])
        rows_ln = sb("rows_ln", [128, 2, D])
        att = sb("att", [128, 2, 16])
        gat_rows = sb("gat_rows", [128, 3, 16])
        b1_sb = sb("b1_sb", [128, NEXP, FC])
        counts = sb("counts", [128, N])
        mask = sb("mask", [128, N], BF16)
        lnc = sb("lnc", [128, N])
        L = [sb(f"L{i}", [128, N]) for i in range(2)]
        PT = sb("PT", [128, 4, SEG])
        qz = sb("qz", [128, H, T])
        oT = sb("oT", [128, H, T])
        y = sb("y", [128, D])
        z = sb("z", [128, D])
        xn = sb("xn", [128, D])
        xt = sb("xt", [128, KC, T])
        hid = sb("hid", [128, 2, FC, 128])
        HV = sb("HV", [128, NT, 16])
        prod = sb("prod", [128, 2, 16])
        s_all = sb("s_all", [128, H, NT])
        t_all = sb("t_all", [128, NT, H])
        stats = sb("stats", [128, 6])
        mv = sb("mv", [128, NT, 2])
        rs = sb("rs", [128, NT])
        nmr = sb("nmr", [128, NT])
        sm = sb("sm", [128, 8])
        mx = sb("mx", [128, H])
        nm = sb("nm", [128, H])
        den = sb("den", [128, H])
        rden = sb("rden", [128, H])
        agg = sb("agg", [128, NT, 16])
        gate = sb("gate", [128, NT, NEXP])
        sT = sb("sT", [80, T])

        S = ctx.enter_context(nc.psum_tensor("S", [128, NSEG, 512], F32))
        TP = [ctx.enter_context(nc.psum_tensor(f"TP{i}", [128, 512], F32)) for i in range(2)]
        O = ctx.enter_context(nc.psum_tensor("O", [128, 512], F32))

        wqk = L[0][:, 1024:2048].rearrange("p (w k n) -> p w k n", w=2, k=KC)
        wvs = L[1][:, 1024:2048].rearrange("p (k n) -> p k n", k=KC)
        ints = [L[0][:, 0:1024].bitcast(I32), L[1][:, 0:1024].bitcast(I32)]
        rowkey = [counts[:, 0:1024], lnc[:, 0:1024]]
        rowtmp = [counts[:, 1024:2048], lnc[:, 1024:2048]]
        dummyrow = mask[:, 0:2048].bitcast(F32)
        out_of_range = QK[:, 1024:2048]
        equal = hid[:].rearrange("p a f n -> p (a f n)").bitcast(BF16).rearrange("p (c n) -> p c n", c=W)
        spare_rows = keyrow[:].rearrange("p s n -> p (s n)")
        LB4 = [L[0], L[1], spare_rows[:, 0:N], spare_rows[:, N:2 * N]]
        zeros = PT[:, :, :].rearrange("p a b -> p (a b)")

        const_ready = sem("const_ready")
        zeros_ready = sem("zeros_ready")
        ea_loaded = sem("ea_loaded")
        eb_loaded = sem("eb_loaded")
        x_loaded = sem("x_loaded")
        w_loaded = sem("w_loaded")
        zero_a = sem("zero_a")
        zero_b = sem("zero_b")
        keystep = sem("keystep")
        rowkeys_ready = sem("rowkeys_ready")
        keycols_done = sem("keycols_done")
        keycols_ready = sem("keycols_ready")
        keys_stored_a = sem("keys_stored_a")
        keys_stored_b = sem("keys_stored_b")
        row_a = [sem(f"row_a{j}") for j in range(BATCH)]
        row_b = [sem(f"row_b{j}") for j in range(BATCH)]
        row_t = [sem(f"row_t{j}") for j in range(B_TILE)]
        step_a = sem("step_a")
        step_b = sem("step_b")
        cells_a = sem("cells_a")
        cells_b = sem("cells_b")
        scattered_a = sem("scattered_a")
        scattered_b = sem("scattered_b")
        vstep = sem("vstep")
        rs_ready = sem("rs_ready")
        dev_ready = sem("dev_ready")
        xn_ready = sem("xn_ready")
        xn_turned = sem("xn_turned")
        xt_ready = sem("xt_ready")
        proj_done = sem("proj_done")
        proj_kept = sem("proj_kept")
        qz_zeroed = sem("qz_zeroed")

        block = ctx.enter_context(nc.Block())
        def attention_sems(g):
            names = ["counts_loaded", "mask_ready", "ln_ready", "lnc_ready", "vs", "qk_done", "masked",
                     "nm_ready", "exp_done", "turned", "kept", "av_done", "o_kept", "qz_ready",
                     "epi1", "y_ready", "gelu_done", "var_ready", "dev_done", "xn2_ready", "epi2", "xt2_ready",
                     "epi3", "h_kept", "agg_read", "summed", "x2_ready"]
            return {n: sem(f"{n}_{g}") for n in names}

        a = attention_sems("a")
        b = attention_sems("b")
        s_turned = sem("s_turned")
        s_kept = sem("s_kept")
        s_stored = sem("s_stored")
        s_loaded = sem("s_loaded")
        w1_loaded = sem("w1_loaded")
        gstep = sem("gstep")
        gvar = sem("gvar")
        gdev = sem("gdev")
        gmax = sem("gmax")
        gexp = sem("gexp")
        gate_ready = sem("gate_ready")
        e_xn = sem("e_xn")
        e_turned = sem("e_turned")
        e_xt = sem("e_xt")
        e_hid = sem("e_hid")
        e_act = sem("e_act")
        e_out = sem("e_out")
        e_step = sem("e_step")
        stored = sem("stored")

        CONSTANTS = 13

        passed = sem("passed")

        def wait_apart(eng, s, value):
            eng.wait_ge(s, value)
            if not isinstance(value, int):
                eng.sem_inc(passed, 1)

        @block.sync
        def _(sp):
            sp.dma_start(ints[0][0:GA, 0:LA], dst_a.rearrange("(q f) -> q f", q=GA)).then_inc(ea_loaded, 16)
            sp.dma_start(ints[0][0:GA, 512:512 + LA], src_a.rearrange("(q f) -> q f", q=GA)).then_inc(ea_loaded, 16)
            edges_b = edge_index.rearrange("two (q f) -> two q f", q=128)
            sp.dma_start(ints[1][:, :], edges_b[1]).then_inc(eb_loaded, 16)
            sp.dma_start(QK[:, 0:1024].bitcast(I32), edges_b[0]).then_inc(eb_loaded, 16)
            sp.dma_start(X[0:T], x.rearrange("(t p) d -> p t d", p=T)).then_inc(x_loaded, 16)

            def weights(dst, src_ap, slow=False):
                sp.dma_start(dst, src_ap, allow_slow_non_contiguous=slow).then_inc(w_loaded, 16)

            def spread(row, p):
                return row.rearrange("(a n) -> a n", a=1).broadcast_to([p, row.shape[0]])

            weights(wqk[:, 0], Wq.rearrange("(k p) n -> p k n", p=128))
            weights(wqk[:, 1], Wk.rearrange("(k p) n -> p k n", p=128))
            weights(wvs[:, :, 0:D], Wv.rearrange("(k p) n -> p k n", p=128))
            weights(wvs[:, :, D:2 * D], Wskip.rearrange("(k p) n -> p k n", p=128))
            weights(bvs[:, 0:D], bv.rearrange("(a n) -> a n", a=1))
            weights(bvs[:, D:2 * D], bskip.rearrange("(a n) -> a n", a=1))
            weights(bqk[:, 0], bq.rearrange("(k p) -> p k", p=128), True)
            weights(bqk[:, 1], bk.rearrange("(k p) -> p k", p=128), True)
            weights(wg_sb[:], Wgat.rearrange("(k p) n -> p k n", p=128))
            weights(rows_ln[:, 0], spread(gamma, 128))
            weights(rows_ln[:, 1], spread(beta, 128))
            weights(att[:, 0], spread(att_src.rearrange("h e -> (h e)"), 128))
            weights(att[:, 1], spread(att_dst.rearrange("h e -> (h e)"), 128))
            weights(gat_rows[:, 0], spread(b_gat, 128))
            weights(gat_rows[:, 1], spread(g_gamma, 128))
            weights(gat_rows[:, 2], spread(g_beta, 128))
            for e in range(NEXP):
                weights(b1_sb[:, e], b1[e].rearrange("(k p) -> p k", p=128), True)

            sp.wait_ge(zeros_ready, 1)
            def clear(table, done):
                view = table[0:N * N, :].rearrange("(p r n) o -> p r (n o)", p=T, n=2000)
                sp.dma_start(view, zeros[0:T, 0:2000].rearrange("p (o n) -> p o n", o=1)
                             .broadcast_to([T, N * N // T // 2000, 2000])).then_inc(done, 16)
                sp.dma_start(table[N * N:N * ROWS, :].rearrange("(p n) o -> p (n o)", p=T),
                             zeros[0:T, 0:N // T]).then_inc(done, 16)
            clear(table_a, zero_a)
            sp.wait_ge(rowkeys_ready, 1)
            sp.dma_start(keys_a.rearrange("(q f) -> q f", q=GA), rowkey[0][0:GA, 0:LA]).then_inc(keys_stored_a, 16)
            sp.wait_ge(rowkeys_ready, 2)
            sp.dma_start(keys_b.rearrange("(q f) -> q f", q=128), rowkey[1]).then_inc(keys_stored_b, 16)
            sp.wait_ge(keys_stored_a, 16)

            def load_row(keys, g, slot, P, Lg, done):
                row = keys[ds(g * Lg, Lg)].rearrange("(a n) -> a n", a=1).broadcast_to([P, Lg])
                sp.dma_start(keyrow[0:P, slot, 0:Lg], row).then_inc(done, 16)

            for j in range(BATCH):
                load_row(keys_a, j, j, PA, LA, row_a[j])
            sp.wait_ge(zero_a, 32)
            clear(table_b, zero_b)
            sp.wait_ge(keys_stored_b, 16)
            for j in range(BATCH):
                sp.wait_ge(cells_a, j + 1)
                load_row(keys_a, BATCH + j, j, PA, LA, row_a[j])
                load_row(keys_b, j, BATCH + j, PB, LB, row_b[j])
            with sp.Fori(1, STEPS - 1) as i:
                for j in range(BATCH):
                    sp.wait_ge(cells_a, i * BATCH + j + 1)
                    load_row(keys_a, (i + 1) * BATCH + j, j, PA, LA, row_a[j])
                    sp.wait_ge(cells_b, (i - 1) * BATCH + j + 1)
                    load_row(keys_b, i * BATCH + j, BATCH + j, PB, LB, row_b[j])
            for j in range(BATCH):
                sp.wait_ge(cells_b, B_EARLY - BATCH + j + 1)
                load_row(keys_b, B_EARLY + j, BATCH + j, PB, LB, row_b[j])
            sp.wait_ge(scattered_a, 16 * W * GA)

            def load_counts(table, t, sems, user):
                if user is not None:
                    sp.wait_ge(sems["lnc_ready"], user)
                sp.dma_start(counts[0:T, :], table[ds(t * T * N, T * N), :].rearrange("(p n) o -> p (n o)", p=T))\
                  .then_inc(sems["counts_loaded"], 16)

            load_counts(table_a, 0, a, None)

            def tile_a(t, last):
                for j in range(B_TILE):
                    sp.wait_ge(cells_b, B_EARLY + B_TILE0 + B_TILE * (t - 1) - B_TILE + j + 1)
                    load_row(keys_b, B_EARLY + B_TILE0 + B_TILE * (t - 1) + j, j, PB, LB, row_t[j])
                    if j == 3 and not last:
                        load_counts(table_a, t + 1, a, t + 1)

            sp.wait_ge(cells_a, GA)
            load_counts(table_a, 1, a, 1)
            with sp.Fori(1, NT - 1) as t:
                tile_a(t, False)
            tile_a(NT - 1, True)
            sp.wait_ge(scattered_b, 16 * W * GB)
            sp.wait_ge(a["lnc_ready"], NT)
            load_counts(table_b, 0, b, None)
            sp.wait_ge(s_kept, 1)
            sp.dma_start(s_rows.rearrange("h t p -> (h t) p"), sT[0:H * NT, :]).then_inc(s_stored, 16)
            sp.wait_ge(s_stored, 16)
            sp.wait_ge(a["qk_done"], H * NT)
            sp.dma_start(S_all[0:T], s_rows.rearrange("h t p -> h (t p)").rearrange("(a h) n -> a h n", a=1)
                         .broadcast_to([T, H, N])).then_inc(s_loaded, 16)
            sp.wait_ge(a["av_done"], NSEG * H * NT)
            sp.wait_ge(a["y_ready"], NT)
            sp.dma_start(w1_sb, W1.rearrange("e (k p) f -> p e k f", p=128)).then_inc(w1_loaded, 16)
            sp.dma_start(w2_sb, W2.rearrange("e (k p) d -> p e k d", p=128)).then_inc(w1_loaded, 16)
            sp.dma_start(b2_sb.rearrange("p e d -> p (e d)"), spread(b2.rearrange("e d -> (e d)"), 128)).then_inc(w1_loaded, 16)
            load_counts(table_b, 1, b, 1)
            with sp.Fori(1, NT - 1) as t:
                load_counts(table_b, t + 1, b, t + 1)
            with sp.Fori(0, NT) as t:
                sp.wait_ge(e_step, 2 * NEXP * (t + 1))
                sp.dma_start(out[ds(t * T, T), :], y[0:T, :]).then_inc(stored, 16)
            sp.wait_ge(stored, 16 * NT)

        @block.gpsimd
        def _(pool):
            pool.memset(zeros, 0.0).then_inc(zeros_ready, 1)
            pool.iota(dummyrow[:, 0:512], pattern=[[1, 512]], base=DUMMY, channel_multiplier=0,
                      allow_small_or_imprecise_dtypes=True).then_inc(const_ready, 1)
            pool.iota(dummyrow[:, 512:1024], pattern=[[1, 512]], base=DUMMY, channel_multiplier=0,
                      allow_small_or_imprecise_dtypes=True).then_inc(const_ready, 1)
            pool.memset(ident[:], 0.0).then_inc(const_ready, 1)
            pool.memset(order_a[:], 1.0).then_inc(const_ready, 1)
            pool.memset(order_b[:], 1.0).then_inc(const_ready, 1)
            pool.iota(slot_a[:], pattern=[[PA, W]], base=DUMMY, channel_multiplier=1,
                      allow_small_or_imprecise_dtypes=True).then_inc(const_ready, 1)
            pool.iota(slot_b[:], pattern=[[PB, W]], base=DUMMY, channel_multiplier=1,
                      allow_small_or_imprecise_dtypes=True).then_inc(const_ready, 1)
            pool.memset(eps[:], LN_EPS).then_inc(const_ready, 1)
            pool.memset(tiny[:], 1e-18).then_inc(const_ready, 1)
            pool.memset(ones_row[:], 1.0).then_inc(const_ready, 1)
            pool.memset(qz[:], 0.0).then_inc(qz_zeroed, 1)
            pool.wait_ge(const_ready, 10)
            pool.affine_select(out=ident[:], in_=ident[:], compare_op=ALU.not_equal, fill=1.0, base=0,
                               pattern=[[-1, 128]], channel_multiplier=1).then_inc(const_ready, 1)
            for m, P in ((order_a, PA), (order_b, PB)):
                pool.affine_select(out=m[:], in_=m[:], compare_op=ALU.is_ge, fill=EARLIER, base=0,
                                   pattern=[[-P, W], [1, LB]], channel_multiplier=-1).then_inc(const_ready, 1)

            def scatter(table, g, slot, P, cells, landed, landed_base):
                pool.wait_ge(cells, g + 1)
                if landed_base is not None:
                    wait_apart(pool, landed, landed_base)
                for c in range(W):
                    pool.indirect_dma_start(
                        table, bass.IndirectOffsetOnAxis(ap=cell[0:P, slot, c:c + 1], axis=0),
                        weight[0:P, slot, c:c + 1], None, bounds_check=ROWS * N - 1, oob_is_err=True,
                        compute_op=ALU.add).then_inc(landed, 16)

            pool.wait_ge(zero_a, 32)
            for j in range(BATCH):
                scatter(table_a, j, j, PA, cells_a, scattered_a, 16 * W * j if j else None)
            pool.wait_ge(zero_b, 32)
            for j in range(BATCH):
                scatter(table_a, BATCH + j, j, PA, cells_a, scattered_a, 16 * W * (BATCH + j))
                scatter(table_b, j, BATCH + j, PB, cells_b, scattered_b, 16 * W * j if j else None)
            with pool.Fori(1, STEPS - 1) as i:
                for j in range(BATCH):
                    scatter(table_a, (i + 1) * BATCH + j, j, PA, cells_a, scattered_a, 16 * W * ((i + 1) * BATCH + j))
                    scatter(table_b, i * BATCH + j, BATCH + j, PB, cells_b, scattered_b, 16 * W * (i * BATCH + j))
            for j in range(BATCH):
                scatter(table_b, B_EARLY + j, BATCH + j, PB, cells_b, scattered_b, 16 * W * (B_EARLY + j))
            with pool.Fori(0, NT - 1) as t:
                for j in range(B_TILE):
                    g = B_EARLY + B_TILE0 + B_TILE * t + j
                    scatter(table_b, g, j, PB, cells_b, scattered_b, 16 * W * g)

        def turn_and_sum(pe, sems, tiles, v, vpar, h, src_tile, M, first, o_free):
            pe.wait_ge(sems["exp_done"], v + 1)
            n = NSEG * v

            def turn(s):
                if not (first and s < 2):
                    pe.wait_ge(sems["kept"], n + s - 1)
                for j in range(TPS):
                    last = pe.transpose(TP[(vpar * NSEG + s) % 2][0:T, j * T:(j + 1) * T],
                                        tiles[vpar % len(tiles)][0:T, (TPS * s + j) * T:(TPS * s + j + 1) * T],
                                        ident[0:T, 0:T])
                last.then_inc(sems["turned"], 1)

            def sums(s):
                pe.wait_ge(sems["kept"], n + s + 1)
                if s == 0 and o_free is not None:
                    pe.wait_ge(sems["o_kept"], o_free)
                for j in range(TPS):
                    k = TPS * s + j
                    last = pe.matmul(O[0:M, h * T:(h + 1) * T], src_tile(k, h),
                                     PT[0:T, (vpar * NSEG + s) % 4, j * T:(j + 1) * T],
                                     start=(k == 0), stop=(k == NT - 1))
                last.then_inc(sems["av_done"], 1)

            turn(0)
            turn(1)
            for s in range(NSEG):
                sums(s)
                if s + 2 < NSEG:
                    turn(s + 2)

        def keep_turned(act, sems, v, vpar, first, segs=range(NSEG)):
            for s in segs:
                n = NSEG * v + s
                act.wait_ge(sems["turned"], n + 1)
                if not (first and s < 4):
                    act.wait_ge(sems["av_done"], n - 3)
                act.activation(PT[0:T, (vpar * NSEG + s) % 4, :], TP[(vpar * NSEG + s) % 2][0:T, 0:SEG],
                               ACT.Copy).then_inc(sems["kept"], 1)

        def exps(act, sems, tiles, u, h):
            act.wait_ge(sems["nm_ready"], u + 1)
            act.activation(tiles[h % len(tiles)][0:T, :], tiles[h % len(tiles)][0:T, :], ACT.Exp, bias=nm[0:T, h:h + 1],
                           accum_out=den[0:T, h:h + 1]).then_inc(sems["exp_done"], 1)

        @block.tensor
        def _(pe):
            pe.wait_ge(const_ready, CONSTANTS)
            pe.wait_ge(rowkeys_ready, 1)
            for c in range(W):
                last = pe.transpose(S[0:PA, 0, c * GA:(c + 1) * GA], rowkey[0][0:GA, c * PA:(c + 1) * PA],
                                    ident[0:GA, 0:GA])
            last.then_inc(keycols_done, 1)
            pe.wait_ge(rowkeys_ready, 2)
            for c in range(8):
                last = pe.transpose(S[:, 1 + c // 4, (c % 4) * 128:(c % 4 + 1) * 128],
                                    rowkey[1][:, c * 128:(c + 1) * 128], ident[:])
            last.then_inc(keycols_done, 1)

            def project(t, first):
                pe.wait_ge(xn_ready, t + 1)
                if not first:
                    pe.wait_ge(xt_ready, t)
                for k in range(KC):
                    last = pe.transpose(TP[0][:, k * T:(k + 1) * T], xn[0:T, k * 128:(k + 1) * 128],
                                        ident[0:T, 0:T])
                last.then_inc(xn_turned, 1)
                pe.wait_ge(xt_ready, t + 1)
                if not first:
                    pe.wait_ge(proj_kept, 2 * t)
                for w in range(2):
                    for m in range(KC):
                        for k in range(KC):
                            last = pe.matmul(S[:, 3, (w * KC + m) * T:(w * KC + m + 1) * T],
                                             wqk[:, w, k, m * 128:(m + 1) * 128], xt[:, k, :],
                                             start=(k == 0), stop=(k == KC - 1))
                last.then_inc(proj_done, 1)
                for k in range(KC):
                    pe.matmul(S[0:T, 4, :], xt[:, k, :], wvs[:, k, :], start=(k == 0), stop=False)
                pe.matmul(S[0:T, 4, :], ones_row[:, 0:T], bvs[:, :], start=False, stop=True).then_inc(proj_done, 1)

            pe.wait_ge(w_loaded, 16 * 20)
            project(0, True)
            with pe.Fori(1, NT) as t:
                project(t, False)

            def logits(t, h, wait_masked, lent):
                u = H * t + h
                pe.wait_ge(a["qz_ready"], u + 1)
                if wait_masked:
                    pe.wait_ge(a["masked"], u)
                for n, s in enumerate(SEG_ORDER):
                    if s == 0 and lent is not None:
                        pe.wait_ge(*lent)
                    last = pe.matmul(S[0:T, s, 0:SEG], qz[:, h, :], kT[:, h // 2, s * SEG:(s + 1) * SEG],
                                     start=True, stop=True)
                last.then_inc(a["qk_done"], 1)

            values_a = lambda k, h: V[0:T, k, h * C:(h + 1) * C]

            def epi1(t):
                wait_apart(pe, a["o_kept"], H * t + H)
                for h in range(H):
                    last = pe.transpose(S[0:T, 0, h * C:(h + 1) * C], oT[0:C, h, :], ident[0:C, 0:C])
                last.then_inc(a["epi1"], 1)

            def epi2(t):
                pe.wait_ge(a["xn2_ready"], t + 1)
                for k in range(KC):
                    last = pe.transpose(S[:, 0, k * T:(k + 1) * T], xn[0:T, k * 128:(k + 1) * 128],
                                        ident[0:T, 0:T])
                last.then_inc(a["epi2"], 1)

            def epi3(t):
                pe.wait_ge(a["xt2_ready"], t + 1)
                for k in range(KC):
                    last = pe.matmul(S[0:T, 0, 0:16], xt[:, k, :], wg_sb[:, k, :], start=(k == 0), stop=(k == KC - 1))
                last.then_inc(a["epi3"], 1)

            def tile_a(t, first, second):
                for h in range(H):
                    lent = None
                    if h >= 2 and not first:
                        pe.wait_ge(a["masked"], H * t + h)
                    if h == 0 and not first and not second:
                        lent = (a["h_kept"], t - 1)
                    if h == 2 and not first:
                        epi1(t - 1)
                        lent = (a["y_ready"], t)
                    if h == 3 and not first:
                        epi2(t - 1)
                        lent = (a["xt2_ready"], t)
                    logits(t, h, not (first and h == 0), lent)
                    if not (first and h == 0):
                        v = H * t + h - 1
                        turn_and_sum(pe, a, L, v, h + 3, (h + 3) % 4, values_a, C, first and h == 1,
                                     None if first or (second and h == 0) else v - 3)
                if not first:
                    pe.wait_ge(a["masked"], H * t + H)
                    epi3(t - 1)

            pe.wait_ge(proj_kept, 2 * NT)
            tile_a(0, True, False)
            tile_a(1, False, True)
            with pe.Fori(2, NT) as t:
                tile_a(t, False, False)
            turn_and_sum(pe, a, L, H * NT - 1, 3, 3, values_a, C, False, H * NT - 4)
            pe.wait_ge(a["h_kept"], NT - 1)
            epi1(NT - 1)
            epi2(NT - 1)
            epi3(NT - 1)
            pe.wait_ge(a["h_kept"], NT)
            pe.transpose(S[0:H * NT, 0, 0:T], s_all[0:T].rearrange("p h t -> p (h t)"), ident[0:T, 0:T]).then_inc(s_turned, 1)

            values_b = lambda k, h: HV[0:T, k, h * NEXP:(h + 1) * NEXP]

            def epi_b(t, first):
                if not first:
                    pe.wait_ge(b["agg_read"], t)
                wait_apart(pe, b["o_kept"], t + 1)
                for h in range(H):
                    last = pe.transpose(S[0:T, 1, h * NEXP:(h + 1) * NEXP], oT[0:NEXP, h, :], ident[0:NEXP, 0:NEXP])
                last.then_inc(b["epi1"], 1)

            def tile_b(t, first):
                for h in range(H):
                    turn_and_sum(pe, b, LB4, H * t + h, h, h, values_b, NEXP, first and h == 0,
                                 t if not first and h == 0 else None)
                epi_b(t, first)

            tile_b(0, True)
            with pe.Fori(1, NT) as t:
                tile_b(t, False)

            pe.wait_ge(w1_loaded, 48)
            pe.wait_ge(b["agg_read"], NT)

            def experts(t, first):
                pe.wait_ge(e_xn, t + 1)
                for k in range(KC):
                    last = pe.transpose(TP[0][:, k * T:(k + 1) * T], xn[0:T, k * 128:(k + 1) * 128],
                                        ident[0:T, 0:T])
                last.then_inc(e_turned, 1)
                pe.wait_ge(e_xt, t + 1)

                def hidden(e):
                    if not (first and e < 2):
                        pe.wait_ge(e_act, NEXP * t + e - 1)
                    for f in range(FC):
                        for k in range(KC):
                            last = pe.matmul(S[:, 1 + e % 2, f * T:(f + 1) * T], w1_sb[:, e, k, f * 128:(f + 1) * 128],
                                             xt[:, k, :], start=(k == 0), stop=(k == KC - 1))
                    last.then_inc(e_hid, 1)

                def output(e):
                    pe.wait_ge(e_act, NEXP * t + e + 1)
                    if not (first and e < 2):
                        pe.wait_ge(e_step, 2 * (NEXP * t + e - 2) + 1)
                    for f in range(FC):
                        last = pe.matmul(S[0:T, 3 + e % 2, 0:D], hid[:, e % 2, f, 0:T], w2_sb[:, e, f, :],
                                         start=(f == 0), stop=(f == FC - 1))
                    last.then_inc(e_out, 1)

                hidden(0)
                for e in range(NEXP):
                    if e + 1 < NEXP:
                        hidden(e + 1)
                    output(e)

            experts(0, True)
            with pe.Fori(1, NT) as t:
                experts(t, False)

        @block.scalar
        def _(act):
            act.wait_ge(keycols_done, 1)
            act.activation(KA[0:PA].rearrange("p (q c) -> p c q", c=W),
                           S[0:PA, 0, 0:W * GA].rearrange("p (c q) -> p c q", c=W), ACT.Copy).then_inc(keycols_ready, 1)
            act.wait_ge(keycols_done, 2)
            kb = KB[:].rearrange("p (q c) -> p c q", c=8)
            for i in range(2):
                act.activation(kb[:, 4 * i:4 * i + 4, :], S[:, 1 + i, :].rearrange("p (c q) -> p c q", c=4),
                               ACT.Copy).then_inc(keycols_ready, 1)
            act.wait_ge(const_ready, CONSTANTS)
            act.wait_ge(rs_ready, 1)
            act.activation(rs[0:T], mv[0:T, :, 1], ACT.Sqrt, bias=eps[0:T]).then_inc(dev_ready, 1)
            act.wait_ge(rs_ready, 2)
            act.wait_ge(w_loaded, 16 * 20)

            def project(t, first):
                if not first:
                    act.wait_ge(xn_turned, t)
                act.activation(xn[0:T], X[0:T, ds(t, 1), :].rearrange("p a d -> p (a d)"), ACT.Identity,
                               bias=nmr[0:T, ds(t, 1)], scale=rs[0:T, ds(t, 1)]).then_inc(xn_ready, 1)
                act.wait_ge(xn_turned, t + 1)
                if not first:
                    act.wait_ge(proj_done, 2 * t)
                act.activation(xt[:], TP[0][:, 0:KC * T].rearrange("p (k n) -> p k n", k=KC), ACT.Copy).then_inc(xt_ready, 1)
                act.wait_ge(proj_done, 2 * t + 1)
                for w, dst_ap, sc in ((0, qT, 1.0), (1, kT, 1.0)):
                    for m in range(KC):
                        last = act.activation(dst_ap[:, m, ds(t * T, T)], S[:, 3, (w * KC + m) * T:(w * KC + m + 1) * T],
                                              ACT.Identity, bias=bqk[:, w, m:m + 1], scale=sc)
                last.then_inc(proj_kept, 1)
                act.wait_ge(proj_done, 2 * t + 2)
                act.activation(VS[0:T].rearrange("p (w t d) -> p w t d", w=2, t=NT)[:, :, ds(t, 1), :]
                               .rearrange("p w t d -> p w (t d)"),
                               S[0:T, 4, :].rearrange("p (w d) -> p w d", w=2), ACT.Copy).then_inc(proj_kept, 1)

            project(0, True)
            with act.Fori(1, NT) as t:
                project(t, False)

            def copy_q(t, h, wait):
                r = (h % 2) * C
                if wait:
                    act.wait_ge(a["qk_done"], H * (t - 1) + h + 1)
                act.activation(qz[r:r + C, h, :], qT[r:r + C, h // 2, ds(t * T, T)], ACT.Copy, scale=QSCALE)\
                   .then_inc(a["qz_ready"], 1)

            def keep_sums(v, h, wait):
                act.wait_ge(a["av_done"], NSEG * (v + 1))
                if wait is not None:
                    act.wait_ge(a["epi1"], wait)
                act.activation(oT[0:C, h, :], O[0:C, h * T:(h + 1) * T], ACT.Copy).then_inc(a["o_kept"], 1)

            def logs(sems, t):
                act.wait_ge(sems["mask_ready"], t + 1)
                act.activation(counts[0:T], counts[0:T], ACT.Ln, bias=tiny[0:T]).then_inc(sems["ln_ready"], 1)

            def turn_copy(t):
                act.wait_ge(a["epi2"], t + 1)
                act.activation(xt[:], S[:, 0, 0:KC * T].rearrange("p (k n) -> p k n", k=KC), ACT.Copy)\
                   .then_inc(a["xt2_ready"], 1)

            def gelu_of(t):
                act.wait_ge(a["y_ready"], t + 1)
                act.activation(y[0:T], y[0:T], ACT.Gelu).then_inc(a["gelu_done"], 1)
                for i in range(2):
                    act.wait_ge(a["var_ready"], 2 * t + 1 + i)
                    act.activation(sm[0:T, 2 + 4 * i:3 + 4 * i], sm[0:T, 1 + 4 * i:2 + 4 * i], ACT.Sqrt, bias=eps[0:T])\
                       .then_inc(a["dev_done"], 1)

            def tile_a(t, first, last):
                for h in range(H):
                    if h == 3 and not first:
                        turn_copy(t - 1)
                    if not (first and h == 0):
                        keep_turned(act, a, H * t + h - 1, h + 3, first and h == 1)
                    exps(act, a, L, H * t + h, h)
                    if not (first and h == 0):
                        second = isinstance(t, int) and t == 1 and h == 0
                        keep_sums(H * t + h - 1, (h + 3) % 4,
                                  None if first or second else (t if h else t - 1))
                    if not last:
                        copy_q(t + 1, h, True)
                    if h == 2 and not last:
                        logs(a, t + 1)
                    if h == 2 and not first:
                        gelu_of(t - 1)

            act.wait_ge(qz_zeroed, 1)
            act.wait_ge(proj_kept, 2 * NT)
            for h in range(H):
                copy_q(0, h, False)
            logs(a, 0)
            tile_a(0, True, False)
            tile_a(1, False, False)
            with act.Fori(2, NT - 1) as t:
                tile_a(t, False, False)
            tile_a(NT - 1, False, True)
            keep_turned(act, a, H * NT - 1, 3, False)
            keep_sums(H * NT - 1, 3, NT - 1)
            gelu_of(NT - 1)
            turn_copy(NT - 1)
            act.wait_ge(s_turned, 1)
            act.activation(sT[0:H * NT, :], S[0:H * NT, 0, 0:T], ACT.Copy).then_inc(s_kept, 1)

            def keep_sums_b(t, first):
                act.wait_ge(b["av_done"], NSEG * H * (t + 1))
                if not first:
                    act.wait_ge(b["epi1"], t)
                act.activation(oT[0:NEXP], O[0:NEXP, 0:SEG].rearrange("p (h n) -> p h n", h=H), ACT.Copy)\
                   .then_inc(b["o_kept"], 1)

            def tile_b(t, first, last):
                for h in range(H):
                    if not (first and h == 0):
                        keep_turned(act, b, H * t + h - 1, h + 3, first and h == 1, range(0, 2))
                    exps(act, b, LB4, H * t + h, h)
                    if not (first and h == 0):
                        keep_turned(act, b, H * t + h - 1, h + 3, first and h == 1, range(2, NSEG))
                    if h == 0 and not first:
                        keep_sums_b(t - 1, isinstance(t, int) and t == 1)
                    if h == 2 and not last:
                        logs(b, t + 1)

            act.wait_ge(a["epi1"], NT)
            logs(b, 0)
            tile_b(0, True, False)
            tile_b(1, False, False)
            with act.Fori(2, NT - 1) as t:
                tile_b(t, False, False)
            tile_b(NT - 1, False, True)
            keep_turned(act, b, H * NT - 1, 3, False)
            keep_sums_b(NT - 1, False)

            act.wait_ge(gvar, 1)
            act.activation(nmr[0:T], nmr[0:T], ACT.Sqrt, bias=eps[0:T]).then_inc(gdev, 1)
            act.wait_ge(gmax, 1)
            act.activation(gate[0:T], gate[0:T], ACT.Exp).then_inc(gexp, 1)

            def experts(t, first):
                act.wait_ge(e_turned, t + 1)
                if not first:
                    act.wait_ge(e_hid, NEXP * t)
                act.activation(xt[:], TP[0][:, 0:KC * T].rearrange("p (k n) -> p k n", k=KC), ACT.Copy).then_inc(e_xt, 1)
                for e in range(NEXP):
                    act.wait_ge(e_hid, NEXP * t + e + 1)
                    if not (first and e < 2):
                        act.wait_ge(e_out, NEXP * t + e - 1)
                    for f in range(FC):
                        last = act.activation(hid[:, e % 2, f, 0:T], S[:, 1 + e % 2, f * T:(f + 1) * T], ACT.Gelu,
                                              bias=b1_sb[:, e, f:f + 1])
                    last.then_inc(e_act, 1)

            experts(0, True)
            with act.Fori(1, NT) as t:
                experts(t, False)

        @block.vector
        def _(v):
            steps = {}

            def step(ins, s=vstep):
                steps[id(s)] = steps.get(id(s), 0) + 1
                ins.then_inc(s, 1)
                v.wait_ge(s, steps[id(s)])

            v.wait_ge(const_ready, CONSTANTS)

            def make_keys(i, dst_i, src_i, P, width):
                key, tmp = rowkey[i][0:P, 0:width], rowtmp[i][0:P, 0:width]
                step(v.tensor_scalar(tmp, dst_i, float(N), None, ALU.min), keystep)
                step(v.tensor_scalar(key, src_i, float(N - 1), None, ALU.min), keystep)
                step(v.scalar_tensor_tensor(key, tmp, float(N), key, ALU.mult, ALU.add), keystep)
                spare = dummyrow[0:P, 0:width]
                outside = out_of_range[0:P, 0:width]
                step(v.tensor_scalar(outside, tmp, float(N), None, ALU.is_ge), keystep)
                step(v.tensor_tensor(tmp, spare, key, ALU.subtract), keystep)
                step(v.tensor_tensor(tmp, tmp, outside, ALU.mult), keystep)
                v.tensor_tensor(key, key, tmp, ALU.add).then_inc(rowkeys_ready, 1)
                v.wait_ge(rowkeys_ready, i + 1)

            v.wait_ge(ea_loaded, 32)
            make_keys(0, ints[0][0:GA, 0:LA], ints[0][0:GA, 512:512 + LA], GA, LA)
            v.wait_ge(eb_loaded, 32)
            make_keys(1, ints[1][:, :], QK[:, 0:1024].bitcast(I32), 128, 1024)

            def compare(g, slot, K, order, spare, P, Lg, loaded, loaded_by, stepper, done, landed, landed_by, before):
                v.wait_ge(loaded, loaded_by)
                if landed is not None:
                    v.wait_ge(landed, landed_by)
                if before is not None:
                    v.wait_ge(*before)
                for c in range(W):
                    last = v.scalar_tensor_tensor(equal[0:P, c, 0:Lg], keyrow[0:P, slot, 0:Lg], K[0:P, ds(g * W + c, 1)],
                                                  order[0:P, c, 0:Lg], ALU.is_equal, ALU.mult,
                                                  accum_out=weight[0:P, slot, c:c + 1])
                v.tensor_tensor(shift[0:P], spare[0:P], K[0:P, ds(g * W, W)], ALU.subtract).then_inc(stepper, 1)
                v.wait_ge(stepper, 2 * g + 1)
                v.scalar_tensor_tensor(moved[0:P], weight[0:P, slot, :], EARLIER, shift[0:P], ALU.is_ge, ALU.mult)\
                 .then_inc(stepper, 1)
                v.wait_ge(stepper, 2 * g + 2)
                v.tensor_tensor(cell[0:P, slot, :], moved[0:P], K[0:P, ds(g * W, W)], ALU.add).then_inc(done, 1)

            def compare_a(g, j, batch, first, before):
                compare(g, j, KA, order_a, slot_a, PA, LA, row_a[j], 16 * (batch + 1), step_a, cells_a,
                        None if first else scattered_a, 16 * W * (g - BATCH + 1), before)

            def compare_b(g, j, batch, first, before):
                compare(g, BATCH + j, KB, order_b, slot_b, PB, LB, row_b[j], 16 * (batch + 1), step_b, cells_b,
                        None if first else scattered_b, 16 * W * (g - BATCH + 1), before)

            v.wait_ge(keycols_ready, 1)
            for j in range(BATCH):
                compare_a(j, j, 0, True, (cells_a, j) if j else None)
            v.wait_ge(x_loaded, 16)
            for t in range(NT):
                step(v.bn_stats(stats[0:T], X[0:T, t, :]))
                if t < NT - 1:
                    step(v.bn_aggr(mv[0:T, t, :], stats[0:T]))
            v.bn_aggr(mv[0:T, NT - 1, :], stats[0:T]).then_inc(rs_ready, 1)
            v.wait_ge(dev_ready, 1)
            step(v.reciprocal(rs[0:T], rs[0:T]))
            step(v.tensor_tensor(nmr[0:T], mv[0:T, :, 0], rs[0:T], ALU.mult))
            v.tensor_scalar(nmr[0:T], nmr[0:T], -1.0, None, ALU.mult).then_inc(rs_ready, 1)
            v.wait_ge(keycols_ready, 3)
            for j in range(BATCH):
                compare_a(BATCH + j, j, 1, False, (cells_b, j) if j else (cells_a, BATCH))
                compare_b(j, j, 0, True, (cells_a, BATCH + j + 1))
            with v.Fori(1, STEPS - 1) as i:
                for j in range(BATCH):
                    compare_a((i + 1) * BATCH + j, j, i + 1, False, (cells_b, i * BATCH + j))
                    compare_b(i * BATCH + j, j, i, False, (cells_a, (i + 1) * BATCH + j + 1))

            def compare_early(j):
                compare_b(B_EARLY + j, j, STEPS - 1, False, (cells_b, B_EARLY + j))

            def compare_t(t, j):
                g = B_EARLY + B_TILE0 + B_TILE * (t - 1) + j
                compare(g, j, KB, order_b, slot_b, PB, LB, row_t[j], 16 * t, step_b, cells_b,
                        scattered_b, 16 * W * (g - B_TILE + 1), (cells_b, g))

            def mask_of(sems, t, first):
                v.wait_ge(sems["counts_loaded"], 16 * (t + 1))
                if not first:
                    v.wait_ge(sems["lnc_ready"], t)
                v.tensor_scalar(mask[0:T], counts[0:T], 0.0, NEG, ALU.is_equal, ALU.mult).then_inc(sems["mask_ready"], 1)

            def lnc_of(sems, t):
                v.wait_ge(sems["ln_ready"], t + 1)
                v.tensor_tensor(lnc[0:T], mask[0:T], counts[0:T], ALU.add).then_inc(sems["lnc_ready"], 1)

            def row_max(sems, u, t, tile_L, h, in0, warm, close_last):
                wait_apart(v, sems["lnc_ready"], t + 1)
                v.tensor_tensor_reduce(out=tile_L[0:T].rearrange("p (s n) -> p s n", s=NSEG), in0=in0,
                                       in1=lnc[0:T].rearrange("p (s n) -> p s n", s=NSEG), scale=1.0, scalar=NEG,
                                       op0=ALU.add, op1=ALU.max, accum_out=mx[0:T, h:h + 1]).then_inc(sems["masked"], 1)
                if close_last:
                    denominators(sems, t - 1)
                v.wait_ge(sems["masked"], u + 1)
                if warm:
                    v.wait_ge(sems["exp_done"], u - H + 1)
                v.tensor_scalar(nm[0:T, h:h + 1], mx[0:T, h:h + 1], NEG_FLOOR, -1.0, ALU.max, ALU.mult)\
                 .then_inc(sems["nm_ready"], 1)

            LINKS = 8

            def divide_a(t):
                v.wait_ge(a["epi1"], t + 1)
                skip = SK[0:T, ds(t, 1), :].rearrange("p a d -> p (a d)")
                for h in range(H):
                    last = v.scalar_tensor_tensor(y[0:T, h * C:(h + 1) * C], S[0:T, 0, h * C:(h + 1) * C],
                                                  rden[0:T, h:h + 1], skip[:, h * C:(h + 1) * C], ALU.mult, ALU.add)
                last.then_inc(a["y_ready"], 1)

            def finish_a(t):
                n = [0]

                def link(ins):
                    n[0] += 1
                    ins.then_inc(a["vs"], 1)
                    wait_apart(v, a["vs"], LINKS * t + n[0])

                v.wait_ge(a["gelu_done"], t + 1)
                link(v.bn_stats(stats[0:T], y[0:T]))
                v.bn_aggr(sm[0:T, 0:2], stats[0:T]).then_inc(a["var_ready"], 1)
                v.wait_ge(a["dev_done"], 2 * t + 1)
                link(v.reciprocal(sm[0:T, 3:4], sm[0:T, 2:3]))
                link(v.tensor_scalar(z[0:T], y[0:T], sm[0:T, 0:1], sm[0:T, 3:4], ALU.subtract, ALU.mult))
                link(v.tensor_tensor(z[0:T], z[0:T], rows_ln[0:T, 0], ALU.mult))
                link(v.tensor_tensor(z[0:T], z[0:T], rows_ln[0:T, 1], ALU.add))
                xrow = X[0:T, ds(t, 1), :].rearrange("p a d -> p (a d)")
                link(v.tensor_tensor(xrow, z[0:T], xrow, ALU.add))
                link(v.bn_stats(stats[0:T], xrow))
                v.bn_aggr(sm[0:T, 4:6], stats[0:T]).then_inc(a["var_ready"], 1)
                v.wait_ge(a["dev_done"], 2 * t + 2)
                link(v.reciprocal(sm[0:T, 7:8], sm[0:T, 6:7]))
                v.tensor_copy(rs[0:T, ds(t, 1)], sm[0:T, 7:8])
                v.tensor_copy(mv[0:T, ds(t, 1), 0:1].rearrange("p a b -> p (a b)"), sm[0:T, 4:5])
                v.tensor_scalar(xn[0:T], xrow, sm[0:T, 4:5], sm[0:T, 7:8], ALU.subtract, ALU.mult)\
                 .then_inc(a["xn2_ready"], 1)
                assert n[0] == LINKS

            def keep_h(t):
                v.wait_ge(a["epi3"], t + 1)
                hrow = HV[0:T, ds(t, 1), :].rearrange("p a d -> p (a d)")
                v.tensor_copy(hrow, S[0:T, 0, 0:16])
                for i in range(2):
                    last = v.tensor_tensor(prod[0:T, i], S[0:T, 0, 0:16], att[0:T, i], ALU.mult)
                last.then_inc(b["x2_ready"], 1)
                v.wait_ge(b["x2_ready"], t + 1)
                v.tensor_reduce(s_all[0:T, :, ds(t, 1)].rearrange("p h a -> p (h a)"),
                                prod[0:T, 0].rearrange("p (h e) -> p h e", h=H), AX_X, ALU.add)
                v.tensor_reduce(t_all[0:T, ds(t, 1), :].rearrange("p a h -> p (a h)"),
                                prod[0:T, 1].rearrange("p (h e) -> p h e", h=H), AX_X, ALU.add).then_inc(a["h_kept"], 1)

            def denominators(sems, t):
                v.wait_ge(sems["exp_done"], H * t + H)
                v.tensor_scalar(rden[0:T], den[0:T], 1e-16, None, ALU.add).then_inc(sems["summed"], 1)
                v.wait_ge(sems["summed"], 2 * t + 1)
                v.reciprocal(rden[0:T], rden[0:T]).then_inc(sems["summed"], 1)
                v.wait_ge(sems["summed"], 2 * t + 2)

            PLACES = {0: range(0, 2), 1: range(2, 4), 2: range(4, 6), 3: range(6, B_TILE)}

            def tile_a(t, first, last):
                for h in range(H):
                    u = H * t + h
                    if h == 2 and not first:
                        divide_a(t - 1)
                    v.wait_ge(a["qk_done"], u + 1)
                    if not (first and h < 2):
                        v.wait_ge(a["turned"], NSEG * (u - 1))
                    row_max(a, u, t, L[h % 2], h, S[0:T, :, 0:SEG], not first, h == 0 and not first)
                    if h == 2 and not last:
                        mask_of(a, t + 1, False)
                    if h == 2 and not first:
                        finish_a(t - 1)
                    if h == 3 and not last:
                        v.wait_ge(a["masked"], u + 1)
                        lnc_of(a, t + 1)
                    if first:
                        for j in ([0, 1], [2], [3], [4])[h]:
                            compare_early(j)
                    else:
                        for j in PLACES[h]:
                            compare_t(t, j)
                if not first:
                    keep_h(t - 1)

            mask_of(a, 0, True)
            lnc_of(a, 0)
            tile_a(0, True, False)
            with v.Fori(1, NT - 1) as t:
                tile_a(t, False, False)
            tile_a(NT - 1, False, True)
            denominators(a, NT - 1)
            divide_a(NT - 1)
            finish_a(NT - 1)
            keep_h(NT - 1)

            def diagonal(t):
                v.wait_ge(b["counts_loaded"], 16 * (t + 1))
                block_t = counts[0:T, ds(t * T, T)]
                v.tensor_tensor(block_t, block_t, ident[0:T, 0:T], ALU.add).then_inc(b["y_ready"], 1)
                v.wait_ge(b["y_ready"], t + 1)

            def read_sums(t):
                v.wait_ge(b["epi1"], t + 1)
                for h in range(H):
                    last = v.tensor_scalar(agg[0:T, ds(t, 1), h * NEXP:(h + 1) * NEXP].rearrange("p a e -> p (a e)"),
                                           S[0:T, 1, h * NEXP:(h + 1) * NEXP], rden[0:T, h:h + 1], None, ALU.mult)
                last.then_inc(b["agg_read"], 1)

            def tile_b(t, first, last):
                for h in range(H):
                    u = H * t + h
                    if not first:
                        v.wait_ge(b["turned"], NSEG * (u - H + 1))
                    e = LB4[h][0:T]
                    v.tensor_scalar(e, S_all[0:T, h, :], t_all[0:T, ds(t, 1), h:h + 1].rearrange("p a b -> p (a b)"),
                                    None, ALU.add).then_inc(b["vs"], 1)
                    v.wait_ge(b["vs"], 2 * u + 1)
                    v.scalar_tensor_tensor(e, e, 0.2, e, ALU.mult, ALU.max).then_inc(b["vs"], 1)
                    v.wait_ge(b["vs"], 2 * u + 2)
                    row_max(b, u, t, LB4[h], h, e.rearrange("p (s n) -> p s n", s=NSEG), not first, h == 0 and not first)
                    if h == 2 and not last:
                        diagonal(t + 1)
                        mask_of(b, t + 1, False)
                    if h == 3 and not last:
                        v.wait_ge(b["masked"], u + 1)
                        lnc_of(b, t + 1)
                    if h == 2 and not first:
                        read_sums(t - 1)

            v.wait_ge(s_loaded, 16)
            diagonal(0)
            mask_of(b, 0, True)
            lnc_of(b, 0)
            tile_b(0, True, False)
            with v.Fori(1, NT - 1) as t:
                tile_b(t, False, False)
            tile_b(NT - 1, False, True)
            denominators(b, NT - 1)
            read_sums(NT - 1)
            v.wait_ge(b["agg_read"], NT)

            def over_tiles(row16):
                return row16.rearrange("p (a n) -> p a n", a=1).broadcast_to([T, NT, 16])

            def over_cols(col, n):
                return col.rearrange("p (t a) -> p t a", a=1).broadcast_to([T, NT, n])

            G = agg[0:T]
            big = L[0][0:T, 0:NT * 16].rearrange("p (t n) -> p t n", t=NT)
            mean = L[0][0:T, 400:400 + NT]
            step(v.tensor_tensor(G, G, over_tiles(gat_rows[0:T, 0]), ALU.add), gstep)
            step(v.tensor_reduce(mean, G, AX_X, ALU.add), gstep)
            step(v.tensor_scalar(mean, mean, 1.0 / 16, None, ALU.mult), gstep)
            step(v.tensor_tensor(G, G, over_cols(mean, 16), ALU.subtract), gstep)
            step(v.tensor_tensor(big, G, G, ALU.mult), gstep)
            var = L[0][0:T, 500:500 + NT]
            step(v.tensor_reduce(var, big, AX_X, ALU.add), gstep)
            v.tensor_scalar(nmr[0:T], var, 1.0 / 16, None, ALU.mult).then_inc(gvar, 1)
            v.wait_ge(gdev, 1)
            step(v.reciprocal(var, nmr[0:T]), gstep)
            step(v.tensor_tensor(G, G, over_cols(var, 16), ALU.mult), gstep)
            step(v.tensor_tensor(G, G, over_tiles(gat_rows[0:T, 1]), ALU.mult), gstep)
            step(v.tensor_tensor(G, G, over_tiles(gat_rows[0:T, 2]), ALU.add), gstep)
            score = L[0][0:T, 700:700 + NT * NEXP].rearrange("p (t e) -> p t e", t=NT)
            step(v.tensor_reduce(score, G.rearrange("p t (h e) -> p t e h", h=H), AX_X, ALU.add), gstep)
            step(v.tensor_scalar(score, score, 1.0 / H, None, ALU.mult), gstep)
            rank = L[0][0:T, 800:800 + NT * NEXP].rearrange("p (t e) -> p t e", t=NT)
            beats = L[0][0:T, 900:900 + NT * NEXP].rearrange("p (t e) -> p t e", t=NT)
            step(v.memset(rank, 0.0), gstep)
            for e in range(NEXP):
                other = score[:, :, e:e + 1]
                step(v.tensor_tensor(beats, other.broadcast_to([T, NT, NEXP]), score, ALU.is_gt), gstep)
                step(v.tensor_tensor(rank, rank, beats, ALU.add), gstep)
                if e + 1 < NEXP:
                    n_after = NEXP - e - 1
                    step(v.tensor_tensor(beats[:, :, 0:n_after], other.broadcast_to([T, NT, n_after]),
                                         score[:, :, e + 1:], ALU.is_equal), gstep)
                    step(v.tensor_tensor(rank[:, :, e + 1:], rank[:, :, e + 1:], beats[:, :, 0:n_after], ALU.add), gstep)
            best = L[0][0:T, 1000:1000 + NT]
            step(v.tensor_reduce(best, score, AX_X, ALU.max), gstep)
            v.tensor_tensor(gate[0:T], score, over_cols(best, NEXP), ALU.subtract).then_inc(gmax, 1)
            v.wait_ge(gexp, 1)
            step(v.tensor_scalar(rank, rank, 2.0, None, ALU.is_lt), gstep)
            step(v.tensor_tensor(gate[0:T], gate[0:T], rank, ALU.mult), gstep)
            step(v.tensor_reduce(best, gate[0:T], AX_X, ALU.add), gstep)
            step(v.reciprocal(best, best), gstep)
            step(v.tensor_tensor(gate[0:T], gate[0:T], over_cols(best, NEXP), ALU.mult), gstep)

            def norm_again(t):
                xrow = X[0:T, ds(t, 1), :].rearrange("p a d -> p (a d)")
                v.tensor_scalar(xn[0:T], xrow, mv[0:T, ds(t, 1), 0:1].rearrange("p a b -> p (a b)"),
                                rs[0:T, ds(t, 1)], ALU.subtract, ALU.mult).then_inc(e_xn, 1)

            def experts(t, first, last):
                xrow = X[0:T, ds(t, 1), :].rearrange("p a d -> p (a d)")
                for e in range(NEXP):
                    n = 2 * (NEXP * t + e)
                    if e == 1 and not last:
                        v.wait_ge(e_turned, t + 1)
                        norm_again(t + 1)
                    v.wait_ge(e_out, NEXP * t + e + 1)
                    if not (first and e == 0):
                        v.wait_ge(e_step, n)
                    if e == 0 and not first:
                        v.wait_ge(stored, 16 * t)
                    v.tensor_tensor(z[0:T], S[0:T, 3 + e % 2, 0:D], b2_sb[0:T, e], ALU.add).then_inc(e_step, 1)
                    v.wait_ge(e_step, n + 1)
                    v.scalar_tensor_tensor(y[0:T], z[0:T], gate[0:T, ds(t, 1), e:e + 1].rearrange("p a b -> p (a b)"),
                                           xrow if e == 0 else y[0:T], ALU.mult, ALU.add).then_inc(e_step, 1)

            norm_again(0)
            experts(0, True, False)
            with v.Fori(1, NT - 1) as t:
                experts(t, False, False)
            experts(NT - 1, False, True)


_ORDER = ["x", "src", "dst", "L0_gnn_Wq", "L0_gnn_bq", "L0_gnn_Wk", "L0_gnn_bk", "L0_gnn_Wv", "L0_gnn_bv",
          "L0_gnn_Wskip", "L0_gnn_bskip", "L0_gnn_gamma", "L0_gnn_beta_ln", "L0_ffn_W_gat", "L0_ffn_att_src",
          "L0_ffn_att_dst", "L0_ffn_b_gat", "L0_ffn_ln_gamma", "L0_ffn_ln_beta", "L0_ffn_W1", "L0_ffn_b1",
          "L0_ffn_W2", "L0_ffn_b2", "L0_ffn_edge_index"]


def kernel(**inputs):
    import numpy as np
    import concourse.bacc as bacc
    from concourse.bass_utils import run_bass_kernel_spmd

    nc = bacc.Bacc("TRN2", target_bir_lowering=False, num_devices=1)
    arrays, args = {}, []
    for name in _ORDER:
        arr = np.ascontiguousarray(inputs[name])
        arrays[f"in_{name}"] = arr
        args.append(nc.dram_tensor(f"in_{name}", arr.shape, mybir.dt.from_np(arr.dtype), kind="ExternalInput").ap())
    out = nc.dram_tensor("out_0", (N, D), F32, kind="ExternalOutput").ap()
    build(nc, *args, out)
    r = run_bass_kernel_spmd(nc, [arrays], core_ids=[0])
    return r.results[0]["out_0"]
```

```python
from contextlib import ExitStack

import concourse.bass as bass
from concourse import mybir
from concourse.alu_op_type import AluOpType as ALU

F32 = mybir.dt.float32
BF16 = mybir.dt.bfloat16
I32 = mybir.dt.int32
U32 = mybir.dt.uint32
ACT = mybir.ActivationFunctionType
AX_X = mybir.AxisListType.X
ds = bass.ds

N = 2500
D = 256
H = 4
C = D // H
T = 125
NT = N // T
SEG = 500
NSEG = N // SEG
TPS = SEG // T
KC = D // 128
NEXP = 4
F = 512
FC = F // 128
LN_EPS = 1e-5
NEG = -1e30
NEG_FLOOR = -1e20
QSCALE = C ** -0.5

W = 2
PA, PB = 125, 128
EA, EB = 42500, 131072
LA, LB = W * PA, W * PB
GPA, GPB = 10, 8
CA, CB = W * GPA, W * GPB
NBA, NBB = EA // (LA * GPA), EB // (LB * GPB)
EARLIER = 4096.0
DUMMY = N * N
ROWS = N + 1
SLICES = 20
SLICE = -(-ROWS * N // (SLICES * 256))
CELLS = SLICES * 256 * SLICE
FULL = T // 16 * 16
RING_A, RING_B = 2, 3
B_EARLY = NBB - RING_B * NT
assert NBA % RING_A == 1 and RING_B <= B_EARLY <= RING_B + 1
SEG_ORDER = [1, 2, 3, 4, 0]


def build(nc, x, src_a, dst_a, Wq, bq, Wk, bk, Wv, bv, Wskip, bskip, gamma, beta, Wgat, att_src, att_dst,
          b_gat, g_gamma, g_beta, W1, b1, W2, b2, edge_index, out):
    ctx = ExitStack()
    with ctx:
        def sb(name, shape, dt=F32):
            return ctx.enter_context(nc.sbuf_tensor(name, shape, dt))

        def sem(name):
            return ctx.enter_context(nc.semaphore(name))

        tables_a = [nc.dram_tensor(f"table_a{i}", [CELLS, 1], F32).ap() for i in range(2)]
        tables_b = [nc.dram_tensor(f"table_b{i}", [CELLS, 1], F32).ap() for i in range(2)]
        keys_a = nc.dram_tensor("keys_a", [EA], F32).ap()
        keys_b = nc.dram_tensor("keys_b", [EB], F32).ap()
        s_rows = nc.dram_tensor("s_rows", [H, NT, T], F32).ap()

        ident = sb("ident", [128, 128])
        ones_row = sb("ones_row", [1, 128])
        spare_a = sb("spare_a", [128, CA])
        spare_b = sb("spare_b", [128, CB])
        order_a = sb("order_a", [128, W, LB], BF16)
        order_b = sb("order_b", [128, W, LB], BF16)
        eps = sb("eps", [128, 1])
        tiny = sb("tiny", [128, 1])
        KA = sb("KA", [128, NBA * CA])
        KB = sb("KB", [128, NBB * CB])
        keyrow_b = sb("keyrow_b", [128, RING_B, GPB * LB])
        weight_a = sb("weight_a", [128, RING_A, CA])
        weight_b = sb("weight_b", [128, RING_B, CB])
        cell_a = sb("cell_a", [128, RING_A, CA], U32)
        cell_b = sb("cell_b", [128, RING_B, CB], U32)
        shift = sb("shift", [128, CA])
        moved = sb("moved", [128, CA])
        X = sb("X", [128, NT, D])
        QK = sb("QK", [128, 2 * KC * N])
        VS = sb("VS", [128, 2 * NT * D])
        qT = QK[:, 0:KC * N].rearrange("p (k n) -> p k n", k=KC)
        kT = QK[:, KC * N:2 * KC * N].rearrange("p (k n) -> p k n", k=KC)
        S_all = QK[:, 0:H * N].rearrange("p (h n) -> p h n", h=H)
        V = VS[:, 0:NT * D].rearrange("p (t d) -> p t d", t=NT)
        SK = VS[:, NT * D:2 * NT * D].rearrange("p (t d) -> p t d", t=NT)
        w1_sb = VS[:, 0:NEXP * KC * F].rearrange("p (e k f) -> p e k f", e=NEXP, k=KC)
        b2_sb = VS[:, 2 * NT * D - NEXP * D:2 * NT * D].rearrange("p (e d) -> p e d", e=NEXP)
        w2_sb = VS[:, NEXP * KC * F:NEXP * KC * F + NEXP * FC * D].rearrange("p (e k d) -> p e k d", e=NEXP, k=FC)
        bvs = sb("bvs", [1, 2 * D])
        bqk = sb("bqk", [128, 2, KC])
        wg_sb = sb("wg_sb", [128, KC, 16])
        rows_ln = sb("rows_ln", [128, 2, D])
        att = sb("att", [128, 2, 16])
        gat_rows = sb("gat_rows", [128, 3, 16])
        b1_sb = sb("b1_sb", [128, NEXP, FC])
        counts = sb("counts", [128, N])
        mask = sb("mask", [128, N], BF16)
        lnc = sb("lnc", [128, N])
        L = [sb(f"L{i}", [128, N]) for i in range(2)]
        PT = sb("PT", [128, 4, SEG])
        qz = sb("qz", [128, H, T])
        oT = sb("oT", [128, H, T])
        y = sb("y", [128, D])
        z = sb("z", [128, D])
        xn = sb("xn", [128, D])
        xt = sb("xt", [128, KC, T])
        hid = sb("hid", [128, 2, FC, 128])
        HV = sb("HV", [128, NT, 16])
        prod = sb("prod", [128, 2, 16])
        s_all = sb("s_all", [128, H, NT])
        t_all = sb("t_all", [128, NT, H])
        stats = sb("stats", [128, 6])
        mv = sb("mv", [128, NT, 2])
        rs = sb("rs", [128, NT])
        nmr = sb("nmr", [128, NT])
        sm = sb("sm", [128, 8])
        mx = sb("mx", [128, H])
        nm = sb("nm", [128, H])
        den = sb("den", [128, H])
        rden = sb("rden", [128, H])
        agg = sb("agg", [128, NT, 16])
        gate = sb("gate", [128, NT, NEXP])
        sT = sb("sT", [80, T])

        S = ctx.enter_context(nc.psum_tensor("S", [128, NSEG, 512], F32))
        TP = [ctx.enter_context(nc.psum_tensor(f"TP{i}", [128, 512], F32)) for i in range(2)]
        O = ctx.enter_context(nc.psum_tensor("O", [128, 512], F32))

        wqk = L[0][:, 1024:2048].rearrange("p (w k n) -> p w k n", w=2, k=KC)
        wvs = L[1][:, 1024:2048].rearrange("p (k n) -> p k n", k=KC)
        ints = [L[0][:, 0:1024].bitcast(I32), L[1][:, 0:1024].bitcast(I32)]
        rowkey = [counts[:, 0:1024], lnc[:, 0:1024]]
        rowtmp = [counts[:, 1024:2048], lnc[:, 1024:2048]]
        dummyrow = mask[:, 0:2048].bitcast(F32)
        out_of_range = QK[:, 1024:2048]
        equal = hid[:].rearrange("p a f n -> p (a f n)").bitcast(BF16).rearrange("p (c n) -> p c n", c=4)
        keyrow_a = [counts, lnc]
        spare_rows = keyrow_b[:].rearrange("p s n -> p (s n)")
        LB4 = [L[0], L[1], spare_rows[:, 0:N], spare_rows[:, N:2 * N]]
        zeros = PT[:, :, :].rearrange("p a b -> p (a b)")

        QA = EA // 500

        const_ready = sem("const_ready")
        zeros_ready = sem("zeros_ready")
        ea_loaded = sem("ea_loaded")
        eb_loaded = sem("eb_loaded")
        x_loaded = sem("x_loaded")
        w_loaded = sem("w_loaded")
        zero_a = [[sem(f"zero_a{i}{j}") for j in range(2)] for i in range(2)]
        zero_b = [[sem(f"zero_b{i}{j}") for j in range(2)] for i in range(2)]
        keystep = sem("keystep")
        rowkeys_ready = sem("rowkeys_ready")
        keycols_done = sem("keycols_done")
        keycols_ready = sem("keycols_ready")
        keys_stored_a = sem("keys_stored_a")
        keys_stored_b = sem("keys_stored_b")
        row_a = [sem(f"row_a{j}") for j in range(RING_A)]
        row_b = [sem(f"row_b{j}") for j in range(RING_B)]
        step_a = sem("step_a")
        step_b = sem("step_b")
        cells_a = sem("cells_a")
        cells_b = sem("cells_b")
        landed_a = [sem(f"landed_a{i}") for i in range(2)]
        landed_b = [sem(f"landed_b{i}") for i in range(2)]
        vstep = sem("vstep")
        rs_ready = sem("rs_ready")
        dev_ready = sem("dev_ready")
        xn_ready = sem("xn_ready")
        xn_turned = sem("xn_turned")
        xt_ready = sem("xt_ready")
        proj_done = sem("proj_done")
        proj_kept = sem("proj_kept")
        qz_zeroed = sem("qz_zeroed")

        block = ctx.enter_context(nc.Block())
        def attention_sems(g):
            names = ["half_loaded", "counts_loaded", "mask_ready", "ln_ready", "lnc_ready", "vs", "qk_done", "masked",
                     "nm_ready", "exp_done", "turned", "kept", "av_done", "o_kept", "qz_ready",
                     "epi1", "y_ready", "gelu_done", "var_ready", "dev_done", "xn2_ready", "epi2", "xt2_ready",
                     "epi3", "h_kept", "agg_read", "summed", "x2_ready"]
            return {n: sem(f"{n}_{g}") for n in names}

        a = attention_sems("a")
        b = attention_sems("b")
        s_turned = sem("s_turned")
        s_kept = sem("s_kept")
        s_stored = sem("s_stored")
        s_loaded = sem("s_loaded")
        w1_loaded = sem("w1_loaded")
        gstep = sem("gstep")
        gvar = sem("gvar")
        gdev = sem("gdev")
        gmax = sem("gmax")
        gexp = sem("gexp")
        gate_ready = sem("gate_ready")
        e_xn = sem("e_xn")
        e_turned = sem("e_turned")
        e_xt = sem("e_xt")
        e_hid = sem("e_hid")
        e_act = sem("e_act")
        e_out = sem("e_out")
        e_step = sem("e_step")
        stored = sem("stored")

        CONSTANTS = 13

        passed = sem("passed")

        def wait_apart(eng, s, value):
            eng.wait_ge(s, value)
            if not isinstance(value, int):
                eng.sem_inc(passed, 1)

        def clear(eng, table, t, done):
            eng.dma_start(table[ds(t * 256 * SLICE, 256 * SLICE), :].rearrange("(p r n) o -> p r (n o)", p=128, r=2),
                          zeros[:, 0:SLICE].rearrange("p (o n) -> p o n", o=1).broadcast_to([128, 2, SLICE]))\
               .then_inc(done, 16)

        A_HALF, B_HALF = 16 * W * GPA // 2, 16 * W * GPB // 2
        A_FIRST = 4 * A_HALF
        LANDED_A = [A_FIRST + (NBA - 2) * A_HALF, (NBA - 2) * A_HALF]
        LANDED_B = NBB * B_HALF

        @block.sync
        def _(sp):
            sp.dma_start(ints[0][0:QA, 0:500], dst_a.rearrange("(q f) -> q f", q=QA)).then_inc(ea_loaded, 16)
            sp.dma_start(ints[0][0:QA, 512:1012], src_a.rearrange("(q f) -> q f", q=QA)).then_inc(ea_loaded, 16)
            edges_b = edge_index.rearrange("two (q f) -> two q f", q=128)
            sp.dma_start(ints[1][:, :], edges_b[1]).then_inc(eb_loaded, 16)
            sp.dma_start(QK[:, 0:1024].bitcast(I32), edges_b[0]).then_inc(eb_loaded, 16)
            sp.dma_start(X[0:T], x.rearrange("(t p) d -> p t d", p=T)).then_inc(x_loaded, 16)

            def weights(dst, src_ap, slow=False):
                sp.dma_start(dst, src_ap, allow_slow_non_contiguous=slow).then_inc(w_loaded, 16)

            def spread(row, p):
                return row.rearrange("(a n) -> a n", a=1).broadcast_to([p, row.shape[0]])

            weights(wqk[:, 0], Wq.rearrange("(k p) n -> p k n", p=128))
            weights(wqk[:, 1], Wk.rearrange("(k p) n -> p k n", p=128))
            weights(wvs[:, :, 0:D], Wv.rearrange("(k p) n -> p k n", p=128))
            weights(wvs[:, :, D:2 * D], Wskip.rearrange("(k p) n -> p k n", p=128))
            weights(bvs[:, 0:D], bv.rearrange("(a n) -> a n", a=1))
            weights(bvs[:, D:2 * D], bskip.rearrange("(a n) -> a n", a=1))
            weights(bqk[:, 0], bq.rearrange("(k p) -> p k", p=128), True)
            weights(bqk[:, 1], bk.rearrange("(k p) -> p k", p=128), True)
            weights(wg_sb[:], Wgat.rearrange("(k p) n -> p k n", p=128))
            weights(rows_ln[:, 0], spread(gamma, 128))
            weights(rows_ln[:, 1], spread(beta, 128))
            weights(att[:, 0], spread(att_src.rearrange("h e -> (h e)"), 128))
            weights(att[:, 1], spread(att_dst.rearrange("h e -> (h e)"), 128))
            weights(gat_rows[:, 0], spread(b_gat, 128))
            weights(gat_rows[:, 1], spread(g_gamma, 128))
            weights(gat_rows[:, 2], spread(g_beta, 128))
            for e in range(NEXP):
                weights(b1_sb[:, e], b1[e].rearrange("(k p) -> p k", p=128), True)

            sp.wait_ge(rowkeys_ready, 1)
            sp.dma_start(keys_a.rearrange("(q f) -> q f", q=QA), rowkey[0][0:QA, 0:500]).then_inc(keys_stored_a, 16)
            sp.wait_ge(rowkeys_ready, 2)
            sp.dma_start(keys_b.rearrange("(q f) -> q f", q=128), rowkey[1]).then_inc(keys_stored_b, 16)

            def load_rows(keys, batch, dst, P, n, done):
                row = keys[ds(batch * n, n)].rearrange("(a n) -> a n", a=1).broadcast_to([P, n])
                sp.dma_start(dst, row).then_inc(done, 16)

            def rows_a(batch, slot):
                load_rows(keys_a, batch, keyrow_a[slot][0:PA, :], PA, GPA * LA, row_a[slot])

            def rows_b(batch, slot):
                load_rows(keys_b, batch, keyrow_b[:, slot, :], PB, GPB * LB, row_b[slot])

            sp.wait_ge(keys_stored_a, 16)
            sp.wait_ge(keys_stored_b, 16)
            sp.wait_ge(keycols_done, 2)
            for j in range(RING_A):
                rows_a(j, j)
            for j in range(RING_B):
                rows_b(j, j)
            with sp.Fori(1, (NBA - 1) // RING_A) as i:
                for j in range(RING_A):
                    sp.wait_ge(cells_a, RING_A * (i - 1) + j + 1)
                    rows_a(RING_A * i + j, j)
            sp.wait_ge(cells_a, NBA - RING_A)
            rows_a(NBA - 1, 0)

            def load_counts(tables, t, sems, built):
                if built is not None:
                    sp.wait_ge(sems["lnc_ready"], built)
                for p0, p1 in ((0, FULL), (FULL, T)):
                    sp.dma_start(counts[p0:p1, :], tables[0][ds(t * T * N + p0 * N, (p1 - p0) * N), :]
                                 .rearrange("(p n) o -> p (n o)", n=N)).then_inc(sems["half_loaded"], 16)

            sp.wait_ge(landed_a[0], LANDED_A[0])
            sp.wait_ge(landed_a[1], LANDED_A[1])
            load_counts(tables_a, 0, a, None)
            load_counts(tables_a, 1, a, 1)

            def tile_a(t, first, last):
                if first:
                    for n in range(B_EARLY - RING_B):
                        sp.wait_ge(cells_b, n + 1)
                        rows_b(RING_B + n, n)
                for j in range(RING_B):
                    n = B_EARLY + RING_B * t + j
                    sp.wait_ge(cells_b, n - RING_B + 1)
                    rows_b(n, (B_EARLY + j) % RING_B)
                    if j == 1 and not first and not last:
                        load_counts(tables_a, t + 1, a, t + 1)

            tile_a(0, True, False)
            with sp.Fori(1, NT - 1) as t:
                tile_a(t, False, False)
            tile_a(NT - 1, False, True)
            sp.wait_ge(landed_b[0], LANDED_B)
            sp.wait_ge(landed_b[1], LANDED_B)
            sp.wait_ge(a["lnc_ready"], NT)
            load_counts(tables_b, 0, b, None)
            sp.wait_ge(s_kept, 1)
            sp.dma_start(s_rows.rearrange("h t p -> (h t) p"), sT[0:H * NT, :]).then_inc(s_stored, 16)
            sp.wait_ge(s_stored, 16)
            sp.wait_ge(a["qk_done"], H * NT)
            sp.dma_start(S_all[0:T], s_rows.rearrange("h t p -> h (t p)").rearrange("(a h) n -> a h n", a=1)
                         .broadcast_to([T, H, N])).then_inc(s_loaded, 16)
            sp.wait_ge(a["av_done"], NSEG * H * NT)
            sp.wait_ge(a["y_ready"], NT)
            sp.dma_start(w1_sb, W1.rearrange("e (k p) f -> p e k f", p=128)).then_inc(w1_loaded, 16)
            sp.dma_start(w2_sb, W2.rearrange("e (k p) d -> p e k d", p=128)).then_inc(w1_loaded, 16)
            sp.dma_start(b2_sb.rearrange("p e d -> p (e d)"), spread(b2.rearrange("e d -> (e d)"), 128)).then_inc(w1_loaded, 16)
            load_counts(tables_b, 1, b, 1)
            with sp.Fori(1, NT - 1) as t:
                load_counts(tables_b, t + 1, b, t + 1)
            with sp.Fori(0, NT) as t:
                sp.wait_ge(e_step, 2 * NEXP * (t + 1))
                sp.dma_start(out[ds(t * T, T), :], y[0:T, :]).then_inc(stored, 16)
            sp.wait_ge(stored, 16 * NT)

        @block.gpsimd
        def _(pool):
            pool.memset(zeros, 0.0).then_inc(zeros_ready, 1)
            pool.iota(dummyrow[:, 0:512], pattern=[[1, 512]], base=DUMMY, channel_multiplier=0,
                      allow_small_or_imprecise_dtypes=True).then_inc(const_ready, 1)
            pool.iota(dummyrow[:, 512:1024], pattern=[[1, 512]], base=DUMMY, channel_multiplier=0,
                      allow_small_or_imprecise_dtypes=True).then_inc(const_ready, 1)
            pool.memset(ident[:], 0.0).then_inc(const_ready, 1)
            pool.memset(order_a[:], 1.0).then_inc(const_ready, 1)
            pool.memset(order_b[:], 1.0).then_inc(const_ready, 1)
            pool.iota(spare_a[:].rearrange("p (g c) -> p g c", c=W), pattern=[[0, GPA], [PA, W]], base=DUMMY, channel_multiplier=1,
                      allow_small_or_imprecise_dtypes=True).then_inc(const_ready, 1)
            pool.iota(spare_b[:].rearrange("p (g c) -> p g c", c=W), pattern=[[0, GPB], [PB, W]], base=DUMMY, channel_multiplier=1,
                      allow_small_or_imprecise_dtypes=True).then_inc(const_ready, 1)
            pool.memset(eps[:], LN_EPS).then_inc(const_ready, 1)
            pool.memset(tiny[:], 1e-18).then_inc(const_ready, 1)
            pool.memset(ones_row[:], 1.0).then_inc(const_ready, 1)
            pool.memset(qz[:], 0.0).then_inc(qz_zeroed, 1)
            pool.wait_ge(const_ready, 10)
            pool.affine_select(out=ident[:], in_=ident[:], compare_op=ALU.not_equal, fill=1.0, base=0,
                               pattern=[[-1, 128]], channel_multiplier=1).then_inc(const_ready, 1)
            for m, P in ((order_a, PA), (order_b, PB)):
                pool.affine_select(out=m[:], in_=m[:], compare_op=ALU.is_ge, fill=EARLIER, base=0,
                                   pattern=[[-P, W], [1, LB]], channel_multiplier=-1).then_inc(const_ready, 1)

            def scatter(tables, P, slot_cells, slot_weights, groups, landed, before):
                for g in range(groups):
                    i = g % len(tables)
                    if before[i] is not None or g >= len(tables):
                        wait_apart(pool, landed[i], 16 * W * (g // len(tables)) + (0 if before[i] is None else before[i]))
                    for c in range(W * g, W * g + W):
                        pool.indirect_dma_start(
                            tables[i], bass.IndirectOffsetOnAxis(ap=slot_cells[0:P, c:c + 1], axis=0),
                            slot_weights[0:P, c:c + 1], None, bounds_check=ROWS * N - 1, oob_is_err=True,
                            compute_op=ALU.add).then_inc(landed[i], 16)

            def scatter_a(batch, slot, fresh):
                wait_apart(pool, cells_a, batch + 1)
                done = (batch - 2) * A_HALF
                scatter(tables_a, PA, cell_a[:, slot], weight_a[:, slot], GPA, landed_a,
                        [A_FIRST + done, None if fresh else done])

            def scatter_b(batch, slot, fresh=False):
                wait_apart(pool, cells_b, batch + 1)
                scatter(tables_b, PB, cell_b[:, slot], weight_b[:, slot], GPB, landed_b,
                        [None, None] if fresh else [batch * B_HALF] * 2)

            def add_counts(tables, t, sems):
                wait_apart(pool, sems["half_loaded"], 32 * (t + 1))
                rows = tables[1][ds(t * T * N, T * N), :].rearrange("(p n) o -> p (n o)", p=T)
                for n0, n1 in ((0, N // 2), (N // 2, N)):
                    pool.dma_start(counts[0:T, n0:n1], rows[:, n0:n1], accum_op=ALU.add).then_inc(sems["counts_loaded"], 16)

            for done in zero_a[0]:
                pool.wait_ge(done, 8 * SLICES)
            for n in range(2):
                wait_apart(pool, cells_a, n + 1)
                scatter(tables_a[0:1], PA, cell_a[:, n], weight_a[:, n], GPA, landed_a[0:1],
                        [n * 2 * A_HALF if n else None])
            for done in zero_a[1]:
                pool.wait_ge(done, 8 * SLICES)
            scatter_a(2, 0, True)
            with pool.Fori(2, (NBA + 1) // RING_A) as i:
                for j in range(RING_A):
                    scatter_a(RING_A * i - 1 + j, (1 + j) % RING_A, False)
            pool.wait_ge(zero_b[0][0], 16 * SLICES)
            for done in zero_b[1]:
                pool.wait_ge(done, 8 * SLICES)
            for n in range(B_EARLY):
                if n == 1:
                    pool.wait_ge(landed_a[0], LANDED_A[0])
                    pool.wait_ge(landed_a[1], LANDED_A[1])
                    add_counts(tables_a, 0, a)
                scatter_b(n, n % RING_B, n == 0)

            def beside_tile(t, last):
                if not last:
                    add_counts(tables_a, t + 1, a)
                for j in range(RING_B):
                    scatter_b(B_EARLY + RING_B * t + j, (B_EARLY + j) % RING_B)

            with pool.Fori(0, NT - 1) as t:
                beside_tile(t, False)
            beside_tile(NT - 1, True)
            with pool.Fori(0, NT) as t:
                add_counts(tables_b, t, b)

        def turn_and_sum(pe, sems, tiles, v, vpar, h, src_tile, M, first, o_free):
            pe.wait_ge(sems["exp_done"], v + 1)
            n = NSEG * v

            def turn(s):
                if not (first and s < 2):
                    pe.wait_ge(sems["kept"], n + s - 1)
                for j in range(TPS):
                    last = pe.transpose(TP[(vpar * NSEG + s) % 2][0:T, j * T:(j + 1) * T],
                                        tiles[vpar % len(tiles)][0:T, (TPS * s + j) * T:(TPS * s + j + 1) * T],
                                        ident[0:T, 0:T])
                last.then_inc(sems["turned"], 1)

            def sums(s):
                pe.wait_ge(sems["kept"], n + s + 1)
                if s == 0 and o_free is not None:
                    pe.wait_ge(sems["o_kept"], o_free)
                for j in range(TPS):
                    k = TPS * s + j
                    last = pe.matmul(O[0:M, h * T:(h + 1) * T], src_tile(k, h),
                                     PT[0:T, (vpar * NSEG + s) % 4, j * T:(j + 1) * T],
                                     start=(k == 0), stop=(k == NT - 1))
                last.then_inc(sems["av_done"], 1)

            turn(0)
            turn(1)
            for s in range(NSEG):
                sums(s)
                if s + 2 < NSEG:
                    turn(s + 2)

        def keep_turned(act, sems, v, vpar, first, segs=range(NSEG)):
            for s in segs:
                n = NSEG * v + s
                act.wait_ge(sems["turned"], n + 1)
                if not (first and s < 4):
                    act.wait_ge(sems["av_done"], n - 3)
                act.activation(PT[0:T, (vpar * NSEG + s) % 4, :], TP[(vpar * NSEG + s) % 2][0:T, 0:SEG],
                               ACT.Copy).then_inc(sems["kept"], 1)

        def exps(act, sems, tiles, u, h):
            act.wait_ge(sems["nm_ready"], u + 1)
            act.activation(tiles[h % len(tiles)][0:T, :], tiles[h % len(tiles)][0:T, :], ACT.Exp, bias=nm[0:T, h:h + 1],
                           accum_out=den[0:T, h:h + 1]).then_inc(sems["exp_done"], 1)

        @block.tensor
        def _(pe):
            pe.wait_ge(const_ready, CONSTANTS)
            pe.wait_ge(rowkeys_ready, 1)
            for c in range(4):
                last = pe.transpose(S[0:PA, 0, c * QA:(c + 1) * QA], rowkey[0][0:QA, c * PA:(c + 1) * PA],
                                    ident[0:QA, 0:QA])
            last.then_inc(keycols_done, 1)
            pe.wait_ge(rowkeys_ready, 2)
            for c in range(8):
                last = pe.transpose(S[:, 1 + c // 4, (c % 4) * 128:(c % 4 + 1) * 128],
                                    rowkey[1][:, c * 128:(c + 1) * 128], ident[:])
            last.then_inc(keycols_done, 1)

            def project(t, first):
                pe.wait_ge(xn_ready, t + 1)
                if not first:
                    pe.wait_ge(xt_ready, t)
                for k in range(KC):
                    last = pe.transpose(TP[0][:, k * T:(k + 1) * T], xn[0:T, k * 128:(k + 1) * 128],
                                        ident[0:T, 0:T])
                last.then_inc(xn_turned, 1)
                pe.wait_ge(xt_ready, t + 1)
                if not first:
                    pe.wait_ge(proj_kept, 2 * t)
                for w in range(2):
                    for m in range(KC):
                        for k in range(KC):
                            last = pe.matmul(S[:, 3, (w * KC + m) * T:(w * KC + m + 1) * T],
                                             wqk[:, w, k, m * 128:(m + 1) * 128], xt[:, k, :],
                                             start=(k == 0), stop=(k == KC - 1))
                last.then_inc(proj_done, 1)
                for k in range(KC):
                    pe.matmul(S[0:T, 4, :], xt[:, k, :], wvs[:, k, :], start=(k == 0), stop=False)
                pe.matmul(S[0:T, 4, :], ones_row[:, 0:T], bvs[:, :], start=False, stop=True).then_inc(proj_done, 1)

            pe.wait_ge(w_loaded, 16 * 20)
            project(0, True)
            with pe.Fori(1, NT) as t:
                project(t, False)

            def logits(t, h, wait_masked, lent):
                u = H * t + h
                pe.wait_ge(a["qz_ready"], u + 1)
                if wait_masked:
                    pe.wait_ge(a["masked"], u)
                for n, s in enumerate(SEG_ORDER):
                    if s == 0 and lent is not None:
                        pe.wait_ge(*lent)
                    last = pe.matmul(S[0:T, s, 0:SEG], qz[:, h, :], kT[:, h // 2, s * SEG:(s + 1) * SEG],
                                     start=True, stop=True)
                last.then_inc(a["qk_done"], 1)

            values_a = lambda k, h: V[0:T, k, h * C:(h + 1) * C]

            def epi1(t):
                wait_apart(pe, a["o_kept"], H * t + H)
                for h in range(H):
                    last = pe.transpose(S[0:T, 0, h * C:(h + 1) * C], oT[0:C, h, :], ident[0:C, 0:C])
                last.then_inc(a["epi1"], 1)

            def epi2(t):
                pe.wait_ge(a["xn2_ready"], t + 1)
                for k in range(KC):
                    last = pe.transpose(S[:, 0, k * T:(k + 1) * T], xn[0:T, k * 128:(k + 1) * 128],
                                        ident[0:T, 0:T])
                last.then_inc(a["epi2"], 1)

            def epi3(t):
                pe.wait_ge(a["xt2_ready"], t + 1)
                for k in range(KC):
                    last = pe.matmul(S[0:T, 0, 0:16], xt[:, k, :], wg_sb[:, k, :], start=(k == 0), stop=(k == KC - 1))
                last.then_inc(a["epi3"], 1)

            def tile_a(t, first, second):
                for h in range(H):
                    lent = None
                    if h in (1, 3) and not first:
                        pe.wait_ge(a["masked"], H * t + h)
                    if h == 0 and not first and not second:
                        lent = (a["h_kept"], t - 1)
                    if h == 1 and not first:
                        epi1(t - 1)
                        lent = (a["y_ready"], t)
                    if h == 3 and not first:
                        epi2(t - 1)
                        lent = (a["xt2_ready"], t)
                    logits(t, h, not (first and h == 0), lent)
                    if not (first and h == 0):
                        v = H * t + h - 1
                        turn_and_sum(pe, a, L, v, h + 3, (h + 3) % 4, values_a, C, first and h == 1,
                                     None if first or (second and h == 0) else v - 3)
                if not first:
                    pe.wait_ge(a["masked"], H * t + H)
                    epi3(t - 1)

            pe.wait_ge(proj_kept, 2 * NT)
            tile_a(0, True, False)
            tile_a(1, False, True)
            with pe.Fori(2, NT) as t:
                tile_a(t, False, False)
            turn_and_sum(pe, a, L, H * NT - 1, 3, 3, values_a, C, False, H * NT - 4)
            pe.wait_ge(a["h_kept"], NT - 1)
            epi1(NT - 1)
            epi2(NT - 1)
            epi3(NT - 1)
            pe.wait_ge(a["h_kept"], NT)
            pe.transpose(S[0:H * NT, 0, 0:T], s_all[0:T].rearrange("p h t -> p (h t)"), ident[0:T, 0:T]).then_inc(s_turned, 1)

            values_b = lambda k, h: HV[0:T, k, h * NEXP:(h + 1) * NEXP]

            def epi_b(t, first):
                if not first:
                    pe.wait_ge(b["agg_read"], t)
                wait_apart(pe, b["o_kept"], t + 1)
                for h in range(H):
                    last = pe.transpose(S[0:T, 1, h * NEXP:(h + 1) * NEXP], oT[0:NEXP, h, :], ident[0:NEXP, 0:NEXP])
                last.then_inc(b["epi1"], 1)

            def tile_b(t, first):
                for h in range(H):
                    turn_and_sum(pe, b, LB4, H * t + h, h, h, values_b, NEXP, first and h == 0,
                                 t if not first and h == 0 else None)
                epi_b(t, first)

            tile_b(0, True)
            with pe.Fori(1, NT) as t:
                tile_b(t, False)

            pe.wait_ge(w1_loaded, 48)
            pe.wait_ge(b["agg_read"], NT)

            def experts(t, first):
                pe.wait_ge(e_xn, t + 1)
                for k in range(KC):
                    last = pe.transpose(TP[0][:, k * T:(k + 1) * T], xn[0:T, k * 128:(k + 1) * 128],
                                        ident[0:T, 0:T])
                last.then_inc(e_turned, 1)
                pe.wait_ge(e_xt, t + 1)

                def hidden(e):
                    if not (first and e < 2):
                        pe.wait_ge(e_act, NEXP * t + e - 1)
                    for f in range(FC):
                        for k in range(KC):
                            last = pe.matmul(S[:, 1 + e % 2, f * T:(f + 1) * T], w1_sb[:, e, k, f * 128:(f + 1) * 128],
                                             xt[:, k, :], start=(k == 0), stop=(k == KC - 1))
                    last.then_inc(e_hid, 1)

                def output(e):
                    pe.wait_ge(e_act, NEXP * t + e + 1)
                    if not (first and e < 2):
                        pe.wait_ge(e_step, 2 * (NEXP * t + e - 2) + 1)
                    for f in range(FC):
                        last = pe.matmul(S[0:T, 3 + e % 2, 0:D], hid[:, e % 2, f, 0:T], w2_sb[:, e, f, :],
                                         start=(f == 0), stop=(f == FC - 1))
                    last.then_inc(e_out, 1)

                hidden(0)
                for e in range(NEXP):
                    if e + 1 < NEXP:
                        hidden(e + 1)
                    output(e)

            experts(0, True)
            with pe.Fori(1, NT) as t:
                experts(t, False)

        @block.scalar
        def _(act):
            def clear_paced(table, done, slices):
                for t in slices:
                    if t >= 2:
                        act.wait_ge(done[t % 2], 16 * (t // 2))
                    clear(act, table, t, done[t % 2])

            act.wait_ge(zeros_ready, 1)
            clear_paced(tables_a[0], zero_a[0], range(0, 6))
            act.wait_ge(keycols_done, 1)
            act.activation(KA[0:PA].rearrange("p (q c) -> p c q", c=4),
                           S[0:PA, 0, 0:4 * QA].rearrange("p (c q) -> p c q", c=4), ACT.Copy).then_inc(keycols_ready, 1)
            act.wait_ge(keycols_done, 2)
            kb = KB[:].rearrange("p (q c) -> p c q", c=8)
            for i in range(2):
                act.activation(kb[:, 4 * i:4 * i + 4, :], S[:, 1 + i, :].rearrange("p (c q) -> p c q", c=4),
                               ACT.Copy).then_inc(keycols_ready, 1)
            clear_paced(tables_a[0], zero_a[0], range(6, SLICES))
            clear_paced(tables_a[1], zero_a[1], range(0, SLICES))
            act.wait_ge(const_ready, CONSTANTS)
            act.wait_ge(rs_ready, 1)
            act.activation(rs[0:T], mv[0:T, :, 1], ACT.Sqrt, bias=eps[0:T]).then_inc(dev_ready, 1)
            act.wait_ge(rs_ready, 2)
            act.wait_ge(w_loaded, 16 * 20)

            def project(t, first):
                clear(act, tables_b[0], t, zero_b[0][0])
                if not first:
                    act.wait_ge(xn_turned, t)
                act.activation(xn[0:T], X[0:T, ds(t, 1), :].rearrange("p a d -> p (a d)"), ACT.Identity,
                               bias=nmr[0:T, ds(t, 1)], scale=rs[0:T, ds(t, 1)]).then_inc(xn_ready, 1)
                act.wait_ge(xn_turned, t + 1)
                if not first:
                    act.wait_ge(proj_done, 2 * t)
                act.activation(xt[:], TP[0][:, 0:KC * T].rearrange("p (k n) -> p k n", k=KC), ACT.Copy).then_inc(xt_ready, 1)
                act.wait_ge(proj_done, 2 * t + 1)
                for w, dst_ap, sc in ((0, qT, 1.0), (1, kT, 1.0)):
                    for m in range(KC):
                        last = act.activation(dst_ap[:, m, ds(t * T, T)], S[:, 3, (w * KC + m) * T:(w * KC + m + 1) * T],
                                              ACT.Identity, bias=bqk[:, w, m:m + 1], scale=sc)
                last.then_inc(proj_kept, 1)
                act.wait_ge(proj_done, 2 * t + 2)
                act.activation(VS[0:T].rearrange("p (w t d) -> p w t d", w=2, t=NT)[:, :, ds(t, 1), :]
                               .rearrange("p w t d -> p w (t d)"),
                               S[0:T, 4, :].rearrange("p (w d) -> p w d", w=2), ACT.Copy).then_inc(proj_kept, 1)

            project(0, True)
            with act.Fori(1, NT) as t:
                project(t, False)

            clear_paced(tables_b[1], zero_b[1], range(0, SLICES))

            def copy_q(t, h, wait):
                r = (h % 2) * C
                if wait:
                    act.wait_ge(a["qk_done"], H * (t - 1) + h + 1)
                act.activation(qz[r:r + C, h, :], qT[r:r + C, h // 2, ds(t * T, T)], ACT.Copy, scale=QSCALE)\
                   .then_inc(a["qz_ready"], 1)

            def keep_sums(v, h, wait):
                act.wait_ge(a["av_done"], NSEG * (v + 1))
                if wait is not None:
                    act.wait_ge(a["epi1"], wait)
                act.activation(oT[0:C, h, :], O[0:C, h * T:(h + 1) * T], ACT.Copy).then_inc(a["o_kept"], 1)

            def logs(sems, t):
                act.wait_ge(sems["mask_ready"], t + 1)
                act.activation(counts[0:T], counts[0:T], ACT.Ln, bias=tiny[0:T]).then_inc(sems["ln_ready"], 1)

            def turn_copy(t):
                act.wait_ge(a["epi2"], t + 1)
                act.activation(xt[:], S[:, 0, 0:KC * T].rearrange("p (k n) -> p k n", k=KC), ACT.Copy)\
                   .then_inc(a["xt2_ready"], 1)

            def gelu_of(t):
                act.wait_ge(a["y_ready"], t + 1)
                act.activation(y[0:T], y[0:T], ACT.Gelu).then_inc(a["gelu_done"], 1)
                for i in range(2):
                    act.wait_ge(a["var_ready"], 2 * t + 1 + i)
                    act.activation(sm[0:T, 2 + 4 * i:3 + 4 * i], sm[0:T, 1 + 4 * i:2 + 4 * i], ACT.Sqrt, bias=eps[0:T])\
                       .then_inc(a["dev_done"], 1)

            def tile_a(t, first, last):
                for h in range(H):
                    if h == 3 and not first:
                        turn_copy(t - 1)
                    if not (first and h == 0):
                        keep_turned(act, a, H * t + h - 1, h + 3, first and h == 1)
                    exps(act, a, L, H * t + h, h)
                    if not (first and h == 0):
                        second = isinstance(t, int) and t == 1 and h == 0
                        keep_sums(H * t + h - 1, (h + 3) % 4,
                                  None if first or second else (t if h else t - 1))
                    if not last:
                        copy_q(t + 1, h, True)
                    if h == 2 and not last:
                        logs(a, t + 1)
                    if h == 1 and not first:
                        gelu_of(t - 1)

            act.wait_ge(qz_zeroed, 1)
            act.wait_ge(proj_kept, 2 * NT)
            for h in range(H):
                copy_q(0, h, False)
            logs(a, 0)
            tile_a(0, True, False)
            tile_a(1, False, False)
            with act.Fori(2, NT - 1) as t:
                tile_a(t, False, False)
            tile_a(NT - 1, False, True)
            keep_turned(act, a, H * NT - 1, 3, False)
            keep_sums(H * NT - 1, 3, NT - 1)
            gelu_of(NT - 1)
            turn_copy(NT - 1)
            act.wait_ge(s_turned, 1)
            act.activation(sT[0:H * NT, :], S[0:H * NT, 0, 0:T], ACT.Copy).then_inc(s_kept, 1)

            def keep_sums_b(t, first):
                act.wait_ge(b["av_done"], NSEG * H * (t + 1))
                if not first:
                    act.wait_ge(b["epi1"], t)
                act.activation(oT[0:NEXP], O[0:NEXP, 0:SEG].rearrange("p (h n) -> p h n", h=H), ACT.Copy)\
                   .then_inc(b["o_kept"], 1)

            def tile_b(t, first, last):
                for h in range(H):
                    if not (first and h == 0):
                        keep_turned(act, b, H * t + h - 1, h + 3, first and h == 1, range(0, 2))
                    exps(act, b, LB4, H * t + h, h)
                    if not (first and h == 0):
                        keep_turned(act, b, H * t + h - 1, h + 3, first and h == 1, range(2, NSEG))
                    if h == 0 and not first:
                        keep_sums_b(t - 1, isinstance(t, int) and t == 1)
                    if h == 2 and not last:
                        logs(b, t + 1)

            act.wait_ge(a["epi1"], NT)
            logs(b, 0)
            tile_b(0, True, False)
            tile_b(1, False, False)
            with act.Fori(2, NT - 1) as t:
                tile_b(t, False, False)
            tile_b(NT - 1, False, True)
            keep_turned(act, b, H * NT - 1, 3, False)
            keep_sums_b(NT - 1, False)

            act.wait_ge(gvar, 1)
            act.activation(nmr[0:T], nmr[0:T], ACT.Sqrt, bias=eps[0:T]).then_inc(gdev, 1)
            act.wait_ge(gmax, 1)
            act.activation(gate[0:T], gate[0:T], ACT.Exp).then_inc(gexp, 1)

            def experts(t, first):
                act.wait_ge(e_turned, t + 1)
                if not first:
                    act.wait_ge(e_hid, NEXP * t)
                act.activation(xt[:], TP[0][:, 0:KC * T].rearrange("p (k n) -> p k n", k=KC), ACT.Copy).then_inc(e_xt, 1)
                for e in range(NEXP):
                    act.wait_ge(e_hid, NEXP * t + e + 1)
                    if not (first and e < 2):
                        act.wait_ge(e_out, NEXP * t + e - 1)
                    for f in range(FC):
                        last = act.activation(hid[:, e % 2, f, 0:T], S[:, 1 + e % 2, f * T:(f + 1) * T], ACT.Gelu,
                                              bias=b1_sb[:, e, f:f + 1])
                    last.then_inc(e_act, 1)

            experts(0, True)
            with act.Fori(1, NT) as t:
                experts(t, False)

        @block.vector
        def _(v):
            steps = {}

            def step(ins, s=vstep):
                steps[id(s)] = steps.get(id(s), 0) + 1
                ins.then_inc(s, 1)
                v.wait_ge(s, steps[id(s)])

            v.wait_ge(const_ready, CONSTANTS)

            def make_keys(i, dst_i, src_i, P, width):
                key, tmp = rowkey[i][0:P, 0:width], rowtmp[i][0:P, 0:width]
                step(v.tensor_scalar(tmp, dst_i, float(N), None, ALU.min), keystep)
                step(v.tensor_scalar(key, src_i, float(N - 1), None, ALU.min), keystep)
                step(v.scalar_tensor_tensor(key, tmp, float(N), key, ALU.mult, ALU.add), keystep)
                spare = dummyrow[0:P, 0:width]
                outside = out_of_range[0:P, 0:width]
                step(v.tensor_scalar(outside, tmp, float(N), None, ALU.is_ge), keystep)
                step(v.tensor_tensor(tmp, spare, key, ALU.subtract), keystep)
                step(v.tensor_tensor(tmp, tmp, outside, ALU.mult), keystep)
                v.tensor_tensor(key, key, tmp, ALU.add).then_inc(rowkeys_ready, 1)
                v.wait_ge(rowkeys_ready, i + 1)

            v.wait_ge(ea_loaded, 32)
            make_keys(0, ints[0][0:QA, 0:500], ints[0][0:QA, 512:1012], QA, 500)
            v.wait_ge(eb_loaded, 32)
            make_keys(1, ints[1][:, :], QK[:, 0:1024].bitcast(I32), 128, 1024)

            def compare(batch, rows, K, order, spare, P, groups, loaded, loaded_by, stepper, cells, weights, done,
                        landed, before):
                v.wait_ge(loaded, loaded_by)
                for s, value in landed:
                    v.wait_ge(s, value)
                for s, value in before:
                    v.wait_ge(s, value)
                n, width = W * groups, W * P
                for c in range(n):
                    g = c // W
                    if c >= 4:
                        v.wait_ge(stepper, batch * (n + 2) + c - 3)
                    v.scalar_tensor_tensor(equal[0:P, c % 4, 0:width], rows[0:P, g * width:(g + 1) * width],
                                           K[0:P, ds(batch * n + c, 1)], order[0:P, c % W, 0:width],
                                           ALU.is_equal, ALU.mult, accum_out=weights[0:P, c:c + 1])\
                     .then_inc(stepper, 1)
                v.wait_ge(stepper, batch * (n + 2) + n)
                v.tensor_tensor(shift[0:P, 0:n], spare[0:P], K[0:P, ds(batch * n, n)], ALU.subtract).then_inc(stepper, 1)
                v.wait_ge(stepper, batch * (n + 2) + n + 1)
                v.scalar_tensor_tensor(moved[0:P, 0:n], weights[0:P], EARLIER, shift[0:P, 0:n], ALU.is_ge, ALU.mult)\
                 .then_inc(stepper, 1)
                v.wait_ge(stepper, batch * (n + 2) + n + 2)
                v.tensor_tensor(cells[0:P], moved[0:P, 0:n], K[0:P, ds(batch * n, n)], ALU.add).then_inc(done, 1)

            def compare_a(batch, slot, turn, landed, before):
                compare(batch, keyrow_a[slot], KA, order_a, spare_a, PA, GPA, row_a[slot], 16 * (turn + 1), step_a,
                        cell_a[:, slot], weight_a[:, slot], cells_a, landed, before)

            def compare_b(batch, slot, turn, landed, before):
                compare(batch, keyrow_b[:, slot], KB, order_b, spare_b, PB, GPB, row_b[slot], 16 * (turn + 1), step_b,
                        cell_b[:, slot], weight_b[:, slot], cells_b, landed, before)

            v.wait_ge(keycols_ready, 3)
            compare_a(0, 0, 0, [], [])
            compare_a(1, 1, 0, [], [(cells_a, 1)])
            v.wait_ge(x_loaded, 16)
            for t in range(NT):
                step(v.bn_stats(stats[0:T], X[0:T, t, :]))
                if t < NT - 1:
                    step(v.bn_aggr(mv[0:T, t, :], stats[0:T]))
            v.bn_aggr(mv[0:T, NT - 1, :], stats[0:T]).then_inc(rs_ready, 1)
            v.wait_ge(dev_ready, 1)
            step(v.reciprocal(rs[0:T], rs[0:T]))
            step(v.tensor_tensor(nmr[0:T], mv[0:T, :, 0], rs[0:T], ALU.mult))
            v.tensor_scalar(nmr[0:T], nmr[0:T], -1.0, None, ALU.mult).then_inc(rs_ready, 1)
            compare_b(0, 0, 0, [], [(cells_a, 2)])
            compare_b(1, 1, 0, [], [(cells_b, 1)])
            compare_b(2, 2, 0, [], [(cells_b, 2)])
            compare_a(2, 0, 1, [(landed_a[0], 2 * A_HALF)], [(cells_b, 3)])
            compare_a(3, 1, 1, [(landed_a[0], A_FIRST)], [(cells_a, 3)])

            def sent_a(batch):
                return [(landed_a[0], A_FIRST + (batch - 3) * A_HALF), (landed_a[1], (batch - 3) * A_HALF)]

            with v.Fori(2, NBA // RING_A) as i:
                for j in range(RING_A):
                    compare_a(RING_A * i + j, j, i, sent_a(RING_A * i + j), [(cells_a, RING_A * i + j)])
            compare_a(NBA - 1, 0, NBA // RING_A, sent_a(NBA - 1), [(cells_a, NBA - 1)])

            def compare_late(batch, slot, turn):
                sent = (batch - RING_B + 1) * B_HALF
                compare_b(batch, slot, turn, [(landed_b[0], sent), (landed_b[1], sent)], [(cells_b, batch)])

            def mask_of(sems, t, first):
                v.wait_ge(sems["counts_loaded"], 32 * (t + 1))
                if not first:
                    v.wait_ge(sems["lnc_ready"], t)
                v.tensor_scalar(mask[0:T], counts[0:T], 0.0, NEG, ALU.is_equal, ALU.mult).then_inc(sems["mask_ready"], 1)

            def lnc_of(sems, t):
                v.wait_ge(sems["ln_ready"], t + 1)
                v.tensor_tensor(lnc[0:T], mask[0:T], counts[0:T], ALU.add).then_inc(sems["lnc_ready"], 1)

            def row_max(sems, u, t, tile_L, h, in0, warm, close_last):
                wait_apart(v, sems["lnc_ready"], t + 1)
                v.tensor_tensor_reduce(out=tile_L[0:T].rearrange("p (s n) -> p s n", s=NSEG), in0=in0,
                                       in1=lnc[0:T].rearrange("p (s n) -> p s n", s=NSEG), scale=1.0, scalar=NEG,
                                       op0=ALU.add, op1=ALU.max, accum_out=mx[0:T, h:h + 1]).then_inc(sems["masked"], 1)
                if close_last:
                    denominators(sems, t - 1)
                v.wait_ge(sems["masked"], u + 1)
                if warm:
                    v.wait_ge(sems["exp_done"], u - H + 1)
                v.tensor_scalar(nm[0:T, h:h + 1], mx[0:T, h:h + 1], NEG_FLOOR, -1.0, ALU.max, ALU.mult)\
                 .then_inc(sems["nm_ready"], 1)

            LINKS = 8

            def divide_a(t):
                v.wait_ge(a["epi1"], t + 1)
                skip = SK[0:T, ds(t, 1), :].rearrange("p a d -> p (a d)")
                for h in range(H):
                    last = v.scalar_tensor_tensor(y[0:T, h * C:(h + 1) * C], S[0:T, 0, h * C:(h + 1) * C],
                                                  rden[0:T, h:h + 1], skip[:, h * C:(h + 1) * C], ALU.mult, ALU.add)
                last.then_inc(a["y_ready"], 1)

            def finish_a(t):
                n = [0]

                def link(ins):
                    n[0] += 1
                    ins.then_inc(a["vs"], 1)
                    wait_apart(v, a["vs"], LINKS * t + n[0])

                v.wait_ge(a["gelu_done"], t + 1)
                link(v.bn_stats(stats[0:T], y[0:T]))
                v.bn_aggr(sm[0:T, 0:2], stats[0:T]).then_inc(a["var_ready"], 1)
                v.wait_ge(a["dev_done"], 2 * t + 1)
                link(v.reciprocal(sm[0:T, 3:4], sm[0:T, 2:3]))
                link(v.tensor_scalar(z[0:T], y[0:T], sm[0:T, 0:1], sm[0:T, 3:4], ALU.subtract, ALU.mult))
                link(v.tensor_tensor(z[0:T], z[0:T], rows_ln[0:T, 0], ALU.mult))
                link(v.tensor_tensor(z[0:T], z[0:T], rows_ln[0:T, 1], ALU.add))
                xrow = X[0:T, ds(t, 1), :].rearrange("p a d -> p (a d)")
                link(v.tensor_tensor(xrow, z[0:T], xrow, ALU.add))
                link(v.bn_stats(stats[0:T], xrow))
                v.bn_aggr(sm[0:T, 4:6], stats[0:T]).then_inc(a["var_ready"], 1)
                v.wait_ge(a["dev_done"], 2 * t + 2)
                link(v.reciprocal(sm[0:T, 7:8], sm[0:T, 6:7]))
                v.tensor_copy(rs[0:T, ds(t, 1)], sm[0:T, 7:8])
                v.tensor_copy(mv[0:T, ds(t, 1), 0:1].rearrange("p a b -> p (a b)"), sm[0:T, 4:5])
                v.tensor_scalar(xn[0:T], xrow, sm[0:T, 4:5], sm[0:T, 7:8], ALU.subtract, ALU.mult)\
                 .then_inc(a["xn2_ready"], 1)
                assert n[0] == LINKS

            def keep_h(t):
                v.wait_ge(a["epi3"], t + 1)
                hrow = HV[0:T, ds(t, 1), :].rearrange("p a d -> p (a d)")
                v.tensor_copy(hrow, S[0:T, 0, 0:16])
                for i in range(2):
                    last = v.tensor_tensor(prod[0:T, i], S[0:T, 0, 0:16], att[0:T, i], ALU.mult)
                last.then_inc(b["x2_ready"], 1)
                v.wait_ge(b["x2_ready"], t + 1)
                v.tensor_reduce(s_all[0:T, :, ds(t, 1)].rearrange("p h a -> p (h a)"),
                                prod[0:T, 0].rearrange("p (h e) -> p h e", h=H), AX_X, ALU.add)
                v.tensor_reduce(t_all[0:T, ds(t, 1), :].rearrange("p a h -> p (a h)"),
                                prod[0:T, 1].rearrange("p (h e) -> p h e", h=H), AX_X, ALU.add).then_inc(a["h_kept"], 1)

            def denominators(sems, t):
                v.wait_ge(sems["exp_done"], H * t + H)
                v.tensor_scalar(rden[0:T], den[0:T], 1e-16, None, ALU.add).then_inc(sems["summed"], 1)
                v.wait_ge(sems["summed"], 2 * t + 1)
                v.reciprocal(rden[0:T], rden[0:T]).then_inc(sems["summed"], 1)
                v.wait_ge(sems["summed"], 2 * t + 2)

            PLACES = {0: 0, 1: 1, 2: None, 3: 2}

            def tile_a(t, first, last):
                for h in range(H):
                    u = H * t + h
                    if h == 1 and not first:
                        divide_a(t - 1)
                    v.wait_ge(a["qk_done"], u + 1)
                    if not (first and h < 2):
                        v.wait_ge(a["turned"], NSEG * (u - 1))
                    row_max(a, u, t, L[h % 2], h, S[0:T, :, 0:SEG], not first, h == 0 and not first)
                    if h == 2 and not last:
                        mask_of(a, t + 1, False)
                    if h == 3 and not last:
                        v.wait_ge(a["masked"], u + 1)
                        lnc_of(a, t + 1)
                    if first and h == 0:
                        for n in range(RING_B, B_EARLY):
                            compare_late(n, n - RING_B, 1)
                    j = PLACES[h]
                    if j is not None:
                        n = B_EARLY + j
                        compare_late(RING_B * t + n, n % RING_B, t + n // RING_B)
                    if h == 1 and not first:
                        finish_a(t - 1)
                if not first:
                    keep_h(t - 1)

            mask_of(a, 0, True)
            lnc_of(a, 0)
            tile_a(0, True, False)
            with v.Fori(1, NT - 1) as t:
                tile_a(t, False, False)
            tile_a(NT - 1, False, True)
            denominators(a, NT - 1)
            divide_a(NT - 1)
            finish_a(NT - 1)
            keep_h(NT - 1)

            def diagonal(t):
                v.wait_ge(b["counts_loaded"], 32 * (t + 1))
                block_t = counts[0:T, ds(t * T, T)]
                v.tensor_tensor(block_t, block_t, ident[0:T, 0:T], ALU.add).then_inc(b["y_ready"], 1)
                v.wait_ge(b["y_ready"], t + 1)

            def read_sums(t):
                v.wait_ge(b["epi1"], t + 1)
                for h in range(H):
                    last = v.tensor_scalar(agg[0:T, ds(t, 1), h * NEXP:(h + 1) * NEXP].rearrange("p a e -> p (a e)"),
                                           S[0:T, 1, h * NEXP:(h + 1) * NEXP], rden[0:T, h:h + 1], None, ALU.mult)
                last.then_inc(b["agg_read"], 1)

            def tile_b(t, first, last):
                for h in range(H):
                    u = H * t + h
                    if not first:
                        v.wait_ge(b["turned"], NSEG * (u - H + 1))
                    e = LB4[h][0:T]
                    v.tensor_scalar(e, S_all[0:T, h, :], t_all[0:T, ds(t, 1), h:h + 1].rearrange("p a b -> p (a b)"),
                                    None, ALU.add).then_inc(b["vs"], 1)
                    v.wait_ge(b["vs"], 2 * u + 1)
                    v.scalar_tensor_tensor(e, e, 0.2, e, ALU.mult, ALU.max).then_inc(b["vs"], 1)
                    v.wait_ge(b["vs"], 2 * u + 2)
                    row_max(b, u, t, LB4[h], h, e.rearrange("p (s n) -> p s n", s=NSEG), not first, h == 0 and not first)
                    if h == 2 and not last:
                        diagonal(t + 1)
                        mask_of(b, t + 1, False)
                    if h == 3 and not last:
                        v.wait_ge(b["masked"], u + 1)
                        lnc_of(b, t + 1)
                    if h == 2 and not first:
                        read_sums(t - 1)

            v.wait_ge(s_loaded, 16)
            diagonal(0)
            mask_of(b, 0, True)
            lnc_of(b, 0)
            tile_b(0, True, False)
            with v.Fori(1, NT - 1) as t:
                tile_b(t, False, False)
            tile_b(NT - 1, False, True)
            denominators(b, NT - 1)
            read_sums(NT - 1)
            v.wait_ge(b["agg_read"], NT)

            def over_tiles(row16):
                return row16.rearrange("p (a n) -> p a n", a=1).broadcast_to([T, NT, 16])

            def over_cols(col, n):
                return col.rearrange("p (t a) -> p t a", a=1).broadcast_to([T, NT, n])

            G = agg[0:T]
            big = L[0][0:T, 0:NT * 16].rearrange("p (t n) -> p t n", t=NT)
            mean = L[0][0:T, 400:400 + NT]
            step(v.tensor_tensor(G, G, over_tiles(gat_rows[0:T, 0]), ALU.add), gstep)
            step(v.tensor_reduce(mean, G, AX_X, ALU.add), gstep)
            step(v.tensor_scalar(mean, mean, 1.0 / 16, None, ALU.mult), gstep)
            step(v.tensor_tensor(G, G, over_cols(mean, 16), ALU.subtract), gstep)
            step(v.tensor_tensor(big, G, G, ALU.mult), gstep)
            var = L[0][0:T, 500:500 + NT]
            step(v.tensor_reduce(var, big, AX_X, ALU.add), gstep)
            v.tensor_scalar(nmr[0:T], var, 1.0 / 16, None, ALU.mult).then_inc(gvar, 1)
            v.wait_ge(gdev, 1)
            step(v.reciprocal(var, nmr[0:T]), gstep)
            step(v.tensor_tensor(G, G, over_cols(var, 16), ALU.mult), gstep)
            step(v.tensor_tensor(G, G, over_tiles(gat_rows[0:T, 1]), ALU.mult), gstep)
            step(v.tensor_tensor(G, G, over_tiles(gat_rows[0:T, 2]), ALU.add), gstep)
            score = L[0][0:T, 700:700 + NT * NEXP].rearrange("p (t e) -> p t e", t=NT)
            step(v.tensor_reduce(score, G.rearrange("p t (h e) -> p t e h", h=H), AX_X, ALU.add), gstep)
            step(v.tensor_scalar(score, score, 1.0 / H, None, ALU.mult), gstep)
            rank = L[0][0:T, 800:800 + NT * NEXP].rearrange("p (t e) -> p t e", t=NT)
            beats = L[0][0:T, 900:900 + NT * NEXP].rearrange("p (t e) -> p t e", t=NT)
            step(v.memset(rank, 0.0), gstep)
            for e in range(NEXP):
                other = score[:, :, e:e + 1]
                step(v.tensor_tensor(beats, other.broadcast_to([T, NT, NEXP]), score, ALU.is_gt), gstep)
                step(v.tensor_tensor(rank, rank, beats, ALU.add), gstep)
                if e + 1 < NEXP:
                    n_after = NEXP - e - 1
                    step(v.tensor_tensor(beats[:, :, 0:n_after], other.broadcast_to([T, NT, n_after]),
                                         score[:, :, e + 1:], ALU.is_equal), gstep)
                    step(v.tensor_tensor(rank[:, :, e + 1:], rank[:, :, e + 1:], beats[:, :, 0:n_after], ALU.add), gstep)
            best = L[0][0:T, 1000:1000 + NT]
            step(v.tensor_reduce(best, score, AX_X, ALU.max), gstep)
            v.tensor_tensor(gate[0:T], score, over_cols(best, NEXP), ALU.subtract).then_inc(gmax, 1)
            v.wait_ge(gexp, 1)
            step(v.tensor_scalar(rank, rank, 2.0, None, ALU.is_lt), gstep)
            step(v.tensor_tensor(gate[0:T], gate[0:T], rank, ALU.mult), gstep)
            step(v.tensor_reduce(best, gate[0:T], AX_X, ALU.add), gstep)
            step(v.reciprocal(best, best), gstep)
            step(v.tensor_tensor(gate[0:T], gate[0:T], over_cols(best, NEXP), ALU.mult), gstep)

            def norm_again(t):
                xrow = X[0:T, ds(t, 1), :].rearrange("p a d -> p (a d)")
                v.tensor_scalar(xn[0:T], xrow, mv[0:T, ds(t, 1), 0:1].rearrange("p a b -> p (a b)"),
                                rs[0:T, ds(t, 1)], ALU.subtract, ALU.mult).then_inc(e_xn, 1)

            def experts(t, first, last):
                xrow = X[0:T, ds(t, 1), :].rearrange("p a d -> p (a d)")
                for e in range(NEXP):
                    n = 2 * (NEXP * t + e)
                    if e == 1 and not last:
                        v.wait_ge(e_turned, t + 1)
                        norm_again(t + 1)
                    v.wait_ge(e_out, NEXP * t + e + 1)
                    if not (first and e == 0):
                        v.wait_ge(e_step, n)
                    if e == 0 and not first:
                        v.wait_ge(stored, 16 * t)
                    v.tensor_tensor(z[0:T], S[0:T, 3 + e % 2, 0:D], b2_sb[0:T, e], ALU.add).then_inc(e_step, 1)
                    v.wait_ge(e_step, n + 1)
                    v.scalar_tensor_tensor(y[0:T], z[0:T], gate[0:T, ds(t, 1), e:e + 1].rearrange("p a b -> p (a b)"),
                                           xrow if e == 0 else y[0:T], ALU.mult, ALU.add).then_inc(e_step, 1)

            norm_again(0)
            experts(0, True, False)
            with v.Fori(1, NT - 1) as t:
                experts(t, False, False)
            experts(NT - 1, False, True)


_ORDER = ["x", "src", "dst", "L0_gnn_Wq", "L0_gnn_bq", "L0_gnn_Wk", "L0_gnn_bk", "L0_gnn_Wv", "L0_gnn_bv",
          "L0_gnn_Wskip", "L0_gnn_bskip", "L0_gnn_gamma", "L0_gnn_beta_ln", "L0_ffn_W_gat", "L0_ffn_att_src",
          "L0_ffn_att_dst", "L0_ffn_b_gat", "L0_ffn_ln_gamma", "L0_ffn_ln_beta", "L0_ffn_W1", "L0_ffn_b1",
          "L0_ffn_W2", "L0_ffn_b2", "L0_ffn_edge_index"]


def kernel(**inputs):
    import numpy as np
    import concourse.bacc as bacc
    from concourse.bass_utils import run_bass_kernel_spmd

    nc = bacc.Bacc("TRN2", target_bir_lowering=False, num_devices=1)
    arrays, args = {}, []
    for name in _ORDER:
        arr = np.ascontiguousarray(inputs[name])
        arrays[f"in_{name}"] = arr
        args.append(nc.dram_tensor(f"in_{name}", arr.shape, mybir.dt.from_np(arr.dtype), kind="ExternalInput").ap())
    out = nc.dram_tensor("out_0", (N, D), F32, kind="ExternalOutput").ap()
    build(nc, *args, out)
    r = run_bass_kernel_spmd(nc, [arrays], core_ids=[0])
    return r.results[0]["out_0"]
```

```python
from contextlib import ExitStack

import concourse.bass as bass
from concourse import mybir
from concourse.alu_op_type import AluOpType as ALU

F32 = mybir.dt.float32
BF16 = mybir.dt.bfloat16
I32 = mybir.dt.int32
U32 = mybir.dt.uint32
ACT = mybir.ActivationFunctionType
AX_X = mybir.AxisListType.X
ds = bass.ds

N = 2500
D = 256
H = 4
C = D // H
T = 125
NT = N // T
SEG = 500
NSEG = N // SEG
TPS = SEG // T
KC = D // 128
NEXP = 4
F = 512
FC = F // 128
LN_EPS = 1e-5
NEG = -1e30
NEG_FLOOR = -1e20
QSCALE = C ** -0.5

W = 2
PA, PB = 125, 128
EA, EB = 42500, 131072
LA, LB = W * PA, W * PB
GPA, GPB = 10, 8
CA, CB = W * GPA, W * GPB
NBA, NBB = EA // (LA * GPA), EB // (LB * GPB)
EARLIER = 4096.0
DUMMY = N * N
ROWS = N + 1
IN_FLIGHT = 4
SLICES = 80
SLICE = -(-ROWS * N // (SLICES * 128))
CELLS = SLICES * 128 * SLICE
FULL = T // 16 * 16
RING_A = 2
RING_B = 3
EARLY_B = NBB - RING_B * NT
assert RING_A == 2 and NBA % 2 == 1 and RING_B <= EARLY_B and GPA % 2 == 0 and GPB % 2 == 0
SLOPE = 0.2
SHARED_HEAD = 1
SEG_ORDER = [1, 2, 3, 4, 0]


def build(nc, x, src_a, dst_a, Wq, bq, Wk, bk, Wv, bv, Wskip, bskip, gamma, beta, Wgat, att_src, att_dst,
          b_gat, g_gamma, g_beta, W1, b1, W2, b2, edge_index, out):
    ctx = ExitStack()
    with ctx:
        def sb(name, shape, dt=F32):
            return ctx.enter_context(nc.sbuf_tensor(name, shape, dt))

        def sem(name):
            return ctx.enter_context(nc.semaphore(name))

        tables_a = [nc.dram_tensor(f"table_a{i}", [CELLS, 1], F32).ap() for i in range(2)]
        tables_b = [nc.dram_tensor(f"table_b{i}", [CELLS, 1], F32).ap() for i in range(2)]
        keys_a = nc.dram_tensor("keys_a", [EA], F32).ap()
        keys_b = nc.dram_tensor("keys_b", [EB], F32).ap()
        s_rows = nc.dram_tensor("s_rows", [H, NT, T], F32).ap()

        ident = sb("ident", [128, 128])
        ones_row = sb("ones_row", [1, 128])
        spare_a = sb("spare_a", [128, CA])
        spare_b = sb("spare_b", [128, CB])
        order_a = sb("order_a", [128, W, LB], BF16)
        order_b = sb("order_b", [128, W, LB], BF16)
        eps = sb("eps", [128, 1])
        tiny = sb("tiny", [128, 1])
        KA = sb("KA", [128, NBA * CA])
        KB = sb("KB", [128, NBB * CB])
        keyrow_b = sb("keyrow_b", [128, RING_B, GPB * LB])
        weight_a = sb("weight_a", [128, RING_A, CA])
        weight_b = sb("weight_b", [128, RING_B, CB])
        cell_a = sb("cell_a", [128, RING_A, CA], U32)
        cell_b = sb("cell_b", [128, RING_B, CB], U32)
        shift = sb("shift", [128, CA])
        moved = sb("moved", [128, CA])
        X = sb("X", [128, NT, D])
        QK = sb("QK", [128, 2 * KC * N])
        VS = sb("VS", [128, 2 * NT * D])
        qT = QK[:, 0:KC * N].rearrange("p (k n) -> p k n", k=KC)
        kT = QK[:, KC * N:2 * KC * N].rearrange("p (k n) -> p k n", k=KC)
        S_all = QK[:, 0:H * N].rearrange("p (h n) -> p h n", h=H)
        V = VS[:, 0:NT * D].rearrange("p (t d) -> p t d", t=NT)
        SK = VS[:, NT * D:2 * NT * D].rearrange("p (t d) -> p t d", t=NT)
        S_slope = VS[:, 0:H * N].rearrange("p (h n) -> p h n", h=H)
        w1_sb = VS[:, 0:NEXP * KC * F].rearrange("p (e k f) -> p e k f", e=NEXP, k=KC)
        b2_sb = VS[:, 2 * NT * D - NEXP * D:2 * NT * D].rearrange("p (e d) -> p e d", e=NEXP)
        w2_sb = VS[:, NEXP * KC * F:NEXP * KC * F + NEXP * FC * D].rearrange("p (e k d) -> p e k d", e=NEXP, k=FC)
        bvs = sb("bvs", [1, 2 * D])
        bqk = sb("bqk", [128, 2, KC])
        wg_sb = sb("wg_sb", [128, KC, 16])
        rows_ln = sb("rows_ln", [128, 2, D])
        att = sb("att", [128, 2, 16])
        gat_rows = sb("gat_rows", [128, 3, 16])
        b1_sb = sb("b1_sb", [128, NEXP, FC])
        counts = sb("counts", [128, N])
        more_low = sb("more_low", [128, N // 2])
        mask = sb("mask", [128, N], BF16)
        lnc = sb("lnc", [128, N])
        L = [sb(f"L{i}", [128, N]) for i in range(2)]
        PT = sb("PT", [128, 4, SEG])
        qz = sb("qz", [128, H, T])
        oT = sb("oT", [128, H, T])
        y = sb("y", [128, D])
        z = sb("z", [128, D])
        xn = sb("xn", [128, D])
        xt = sb("xt", [128, KC, T])
        equal = sb("equal", [128, 4, LB], BF16)
        HV = sb("HV", [128, NT, 16])
        prod = sb("prod", [128, 2, 16])
        s_all = sb("s_all", [128, H, NT])
        t_all = sb("t_all", [128, NT, H])
        stats = sb("stats", [128, 6])
        mv = sb("mv", [128, NT, 2])
        rs = sb("rs", [128, NT])
        nmr = sb("nmr", [128, NT])
        sm = sb("sm", [128, 8])
        mx = sb("mx", [128, H])
        nm = sb("nm", [128, H])
        den = sb("den", [128, 2, H])
        rden = sb("rden", [128, H])
        agg = sb("agg", [128, NT, 16])
        gate = sb("gate", [128, NT, NEXP])
        sT = xn[0:H * NT, 0:T]

        S = ctx.enter_context(nc.psum_tensor("S", [128, NSEG, 512], F32))
        TP = [ctx.enter_context(nc.psum_tensor(f"TP{i}", [128, 512], F32)) for i in range(2)]
        O = ctx.enter_context(nc.psum_tensor("O", [128, 512], F32))

        wqk = L[0][:, 1024:2048].rearrange("p (w k n) -> p w k n", w=2, k=KC)
        wvs = L[1][:, 1024:2048].rearrange("p (k n) -> p k n", k=KC)
        ints = [L[0][:, 0:1024].bitcast(I32), L[1][:, 0:1024].bitcast(I32)]
        rowkey = [counts[:, 0:1024], lnc[:, 0:1024]]
        rowtmp = [counts[:, 1024:2048], lnc[:, 1024:2048]]
        dummyrow = mask[:, 0:2048].bitcast(F32)
        out_of_range = QK[:, 1024:2048]
        more = [more_low[:], mask[:].bitcast(F32)]
        hid = more_low[:, 0:2 * FC * 128].rearrange("p (a f n) -> p a f n", a=2, f=FC)
        keyrow_a = [counts, lnc]
        spare_rows = keyrow_b[:].rearrange("p s n -> p (s n)")
        LB4 = [L[0], L[1], spare_rows[:, 0:N], spare_rows[:, N:2 * N]]
        zeros = PT[:, :, :].rearrange("p a b -> p (a b)")

        QA = EA // 500

        const_ready = sem("const_ready")
        zeros_ready = sem("zeros_ready")
        ea_loaded = sem("ea_loaded")
        eb_loaded = sem("eb_loaded")
        x_loaded = sem("x_loaded")
        w_loaded = sem("w_loaded")
        zero_a = [[sem(f"zero_a{i}{j}") for j in range(IN_FLIGHT)] for i in range(2)]
        zero_b = sem("zero_b")
        keystep = sem("keystep")
        rowkeys_ready = sem("rowkeys_ready")
        keycols_done = sem("keycols_done")
        keycols_ready = sem("keycols_ready")
        keys_stored_a = sem("keys_stored_a")
        keys_stored_b = sem("keys_stored_b")
        row_a = [sem(f"row_a{j}") for j in range(RING_A)]
        row_b = [sem(f"row_b{j}") for j in range(RING_B)]
        step_a = sem("step_a")
        step_b = sem("step_b")
        cells_a = sem("cells_a")
        cells_b = sem("cells_b")
        landed_a = [sem(f"landed_a{i}") for i in range(2)]
        landed_b = [sem(f"landed_b{i}") for i in range(2)]
        vstep = sem("vstep")
        rs_ready = sem("rs_ready")
        dev_ready = sem("dev_ready")
        xn_ready = sem("xn_ready")
        xn_turned = sem("xn_turned")
        xt_ready = sem("xt_ready")
        proj_done = sem("proj_done")
        proj_kept = sem("proj_kept")
        qz_zeroed = sem("qz_zeroed")

        block = ctx.enter_context(nc.Block())
        def attention_sems(g):
            names = ["half_loaded", "counts_loaded", "added", "mask_ready", "ln_ready", "lnc_ready", "vs", "qk_done", "masked",
                     "nm_ready", "exp_done", "turned", "kept", "av_done", "o_kept", "qz_ready",
                     "epi1", "y_ready", "gelu_done", "var_ready", "dev_done", "xn2_ready", "epi2", "xt2_ready",
                     "epi3", "h_kept", "agg_read", "summed", "x2_ready"]
            return {n: sem(f"{n}_{g}") for n in names}

        a = attention_sems("a")
        b = attention_sems("b")
        PARTS = {id(a): [(0, NSEG)], id(b): [(0, 2), (2, NSEG)]}
        s_turned = sem("s_turned")
        s_kept = sem("s_kept")
        s_stored = sem("s_stored")
        s_loaded = sem("s_loaded")
        s_scaled = sem("s_scaled")
        w1_loaded = sem("w1_loaded")
        gstep = sem("gstep")
        gvar = sem("gvar")
        gdev = sem("gdev")
        gmax = sem("gmax")
        gexp = sem("gexp")
        e_xn = sem("e_xn")
        e_turned = sem("e_turned")
        e_xt = sem("e_xt")
        e_hid = sem("e_hid")
        e_act = sem("e_act")
        e_out = sem("e_out")
        e_step = sem("e_step")
        stored = sem("stored")

        CONSTANTS = 13

        passed = sem("passed")

        def wait_apart(eng, s, value):
            eng.wait_ge(s, value)
            if not isinstance(value, int):
                eng.sem_inc(passed, 1)

        def clear(eng, table, t, done):
            eng.dma_start(table[ds(t * 128 * SLICE, 128 * SLICE), :].rearrange("(p n) o -> p (n o)", p=128),
                          zeros[:, 0:SLICE]).then_inc(done, 16)

        GROUP = 16 * W
        HALF_A, HALF_B = GROUP * GPA // 2, GROUP * GPB // 2
        LANDED_A = [(NBA + 1) * HALF_A, (NBA - 1) * HALF_A]
        LANDED_B = NBB * HALF_B

        @block.sync
        def _(sp):
            sp.dma_start(ints[0][0:QA, 0:500], dst_a.rearrange("(q f) -> q f", q=QA)).then_inc(ea_loaded, 16)
            sp.dma_start(ints[0][0:QA, 512:1012], src_a.rearrange("(q f) -> q f", q=QA)).then_inc(ea_loaded, 16)
            edges_b = edge_index.rearrange("two (q f) -> two q f", q=128)
            sp.dma_start(ints[1][:, :], edges_b[1]).then_inc(eb_loaded, 16)
            sp.dma_start(QK[:, 0:1024].bitcast(I32), edges_b[0]).then_inc(eb_loaded, 16)
            def weights(dst, src_ap, slow=False):
                sp.dma_start(dst, src_ap, allow_slow_non_contiguous=slow).then_inc(w_loaded, 16)

            def spread(row, p):
                return row.rearrange("(a n) -> a n", a=1).broadcast_to([p, row.shape[0]])

            def issue_weights():
                sp.dma_start(X[0:T], x.rearrange("(t p) d -> p t d", p=T)).then_inc(x_loaded, 16)
                weights(wqk[:, 0], Wq.rearrange("(k p) n -> p k n", p=128))
                weights(wqk[:, 1], Wk.rearrange("(k p) n -> p k n", p=128))
                weights(wvs[:, :, 0:D], Wv.rearrange("(k p) n -> p k n", p=128))
                weights(wvs[:, :, D:2 * D], Wskip.rearrange("(k p) n -> p k n", p=128))
                weights(bvs[:, 0:D], bv.rearrange("(a n) -> a n", a=1))
                weights(bvs[:, D:2 * D], bskip.rearrange("(a n) -> a n", a=1))
                weights(bqk[:, 0], bq.rearrange("(k p) -> p k", p=128), True)
                weights(bqk[:, 1], bk.rearrange("(k p) -> p k", p=128), True)
                weights(wg_sb[:], Wgat.rearrange("(k p) n -> p k n", p=128))
                weights(rows_ln[:, 0], spread(gamma, 128))
                weights(rows_ln[:, 1], spread(beta, 128))
                weights(att[:, 0], spread(att_src.rearrange("h e -> (h e)"), 128))
                weights(att[:, 1], spread(att_dst.rearrange("h e -> (h e)"), 128))
                weights(gat_rows[:, 0], spread(b_gat, 128))
                weights(gat_rows[:, 1], spread(g_gamma, 128))
                weights(gat_rows[:, 2], spread(g_beta, 128))
                for e in range(NEXP):
                    weights(b1_sb[:, e], b1[e].rearrange("(k p) -> p k", p=128), True)

            sp.wait_ge(rowkeys_ready, 1)
            sp.dma_start(keys_a.rearrange("(q f) -> q f", q=QA), rowkey[0][0:QA, 0:500]).then_inc(keys_stored_a, 16)
            sp.wait_ge(rowkeys_ready, 2)
            sp.dma_start(keys_b.rearrange("(q f) -> q f", q=128), rowkey[1]).then_inc(keys_stored_b, 16)

            def load_half(keys, batch, slot, n, half, done):
                row = keys[ds(batch * n + half * n // 2, n // 2)].rearrange("(a n) -> a n", a=1).broadcast_to([128, n // 2])
                sp.dma_start(slot[:, half * n // 2:(half + 1) * n // 2], row).then_inc(done, 16)

            def rows_a(batch, slot, half):
                load_half(keys_a, batch, keyrow_a[slot], GPA * LA, half, row_a[slot])

            def rows_b(batch, slot, half):
                load_half(keys_b, batch, keyrow_b[:, slot, :], GPB * LB, half, row_b[slot])

            sp.wait_ge(keys_stored_a, 16)
            sp.wait_ge(keys_stored_b, 16)
            sp.wait_ge(keycols_done, 2)
            for j in range(2 * RING_A):
                rows_a(j // 2, j // 2, j % 2)
            for done in zero_a[1]:
                sp.wait_ge(done, 16 * SLICES // IN_FLIGHT)
            for j in range(2 * RING_B):
                rows_b(j // 2, j // 2, j % 2)
            issue_weights()

            def next_a(batch, slot):
                sp.wait_ge(cells_a, batch - RING_A + 1)
                for half in range(2):
                    sp.wait_ge(landed_a[1], HALF_A * (batch - RING_A - 1) + GROUP * (2 * half + 1))
                    rows_a(batch, slot, half)

            def next_b(batch, slot, group):
                sp.wait_ge(cells_b, batch - RING_B + 1)
                for half in range(2):
                    sp.wait_ge(landed_b[0], GROUP * (group + half))
                    rows_b(batch, slot, half)

            sp.wait_ge(cells_a, 1)
            for half in range(2):
                rows_a(2, 0, half)
            with sp.Fori(2, (NBA + 1) // RING_A) as i:
                for j in range(RING_A):
                    next_a(RING_A * i - 1 + j, 1 - j)

            def load_rows_of(dst, table, t, done, cols=slice(0, N)):
                for p0, p1 in ((0, FULL), (FULL, T)):
                    sp.dma_start(dst[p0:p1, :], table[ds(t * T * N + p0 * N, (p1 - p0) * N), :]
                                 .rearrange("(p n) o -> p (n o)", n=N)[:, cols]).then_inc(done, 16)

            def load_half_counts(t, half):
                load_rows_of(counts[:, half * N // 2:(half + 1) * N // 2], tables_a[0], t, a["counts_loaded"],
                             slice(half * N // 2, (half + 1) * N // 2))

            def load_half_more(t, half):
                load_rows_of(more[half], tables_a[1], t, a["counts_loaded"], slice(half * N // 2, (half + 1) * N // 2))

            def load_counts_a(t, held_back):
                for n in range(4):
                    if held_back is not None:
                        sp.wait_ge(landed_b[0], held_back + GROUP * (n + 1))
                    if n < 2:
                        load_half_counts(t, n)
                    else:
                        load_half_more(t, n - 2)

            def load_counts_b(t, built):
                if built is not None:
                    sp.wait_ge(b["lnc_ready"], built)
                load_rows_of(counts, tables_b[0], t, b["half_loaded"])

            for i in range(2):
                sp.wait_ge(landed_a[i], LANDED_A[i])
            load_counts_a(0, None)
            sp.wait_ge(a["lnc_ready"], 1)
            load_counts_a(1, None)

            G = GPB // 2
            for n in range(RING_B, EARLY_B):
                next_b(n, n % RING_B, G * (n - RING_B) + 1)

            def rows_late(t, j):
                n = RING_B * t + EARLY_B + j
                next_b(n, (EARLY_B + j) % RING_B, G * (n - RING_B) + G - 1)

            def tile_a(t, last):
                rows_late(t, 0)
                rows_late(t, 1)
                if not last:
                    sp.wait_ge(a["lnc_ready"], t + 1)
                    load_counts_a(t + 1, HALF_B * (RING_B * t + EARLY_B - 1))
                n = RING_B * t + EARLY_B + 2
                next_b(n, (EARLY_B + 2) % RING_B, G * (n - 2) + 1)

            for j in range(RING_B):
                rows_late(0, j)
            with sp.Fori(1, NT - 1) as t:
                tile_a(t, False)
            tile_a(NT - 1, True)
            sp.wait_ge(s_kept, 1)
            sp.dma_start(s_rows.rearrange("h t p -> (h t) p"), sT[0:H * NT, :]).then_inc(s_stored, 16)
            sp.wait_ge(s_stored, 16)
            sp.wait_ge(a["qk_done"], H * NT)
            sp.dma_start(S_all, s_rows.rearrange("h t p -> h (t p)").rearrange("(a h) n -> a h n", a=1)
                         .broadcast_to([128, H, N])).then_inc(s_loaded, 16)
            for i in range(2):
                sp.wait_ge(landed_b[i], LANDED_B)
            sp.wait_ge(a["lnc_ready"], NT)
            load_counts_b(0, None)
            load_counts_b(1, 1)
            with sp.Fori(1, NT - 1) as t:
                load_counts_b(t + 1, t + 1)
            sp.wait_ge(b["vs"], H * NT)
            sp.dma_start(w1_sb, W1.rearrange("e (k p) f -> p e k f", p=128)).then_inc(w1_loaded, 16)
            sp.dma_start(w2_sb, W2.rearrange("e (k p) d -> p e k d", p=128)).then_inc(w1_loaded, 16)
            sp.dma_start(b2_sb.rearrange("p e d -> p (e d)"), spread(b2.rearrange("e d -> (e d)"), 128)).then_inc(w1_loaded, 16)
            with sp.Fori(0, NT) as t:
                sp.wait_ge(e_step, 2 * NEXP * (t + 1))
                sp.dma_start(out[ds(t * T, T), :], y[0:T, :]).then_inc(stored, 16)
            sp.wait_ge(stored, 16 * NT)

        @block.gpsimd
        def _(pool):
            pool.memset(zeros, 0.0).then_inc(zeros_ready, 1)
            pool.iota(dummyrow[:, 0:512], pattern=[[1, 512]], base=DUMMY, channel_multiplier=0,
                      allow_small_or_imprecise_dtypes=True).then_inc(const_ready, 1)
            pool.iota(dummyrow[:, 512:1024], pattern=[[1, 512]], base=DUMMY, channel_multiplier=0,
                      allow_small_or_imprecise_dtypes=True).then_inc(const_ready, 1)
            pool.memset(ident[:], 0.0).then_inc(const_ready, 1)
            pool.memset(order_a[:], 1.0).then_inc(const_ready, 1)
            pool.memset(order_b[:], 1.0).then_inc(const_ready, 1)
            pool.iota(spare_a[:].rearrange("p (g c) -> p g c", c=W), pattern=[[0, GPA], [PA, W]], base=DUMMY, channel_multiplier=1,
                      allow_small_or_imprecise_dtypes=True).then_inc(const_ready, 1)
            pool.iota(spare_b[:].rearrange("p (g c) -> p g c", c=W), pattern=[[0, GPB], [PB, W]], base=DUMMY, channel_multiplier=1,
                      allow_small_or_imprecise_dtypes=True).then_inc(const_ready, 1)
            pool.memset(eps[:], LN_EPS).then_inc(const_ready, 1)
            pool.memset(tiny[:], 1e-18).then_inc(const_ready, 1)
            pool.memset(ones_row[:], 1.0).then_inc(const_ready, 1)
            pool.memset(qz[:], 0.0).then_inc(qz_zeroed, 1)
            pool.wait_ge(const_ready, 10)
            pool.affine_select(out=ident[:], in_=ident[:], compare_op=ALU.not_equal, fill=1.0, base=0,
                               pattern=[[-1, 128]], channel_multiplier=1).then_inc(const_ready, 1)
            for m, P in ((order_a, PA), (order_b, PB)):
                pool.affine_select(out=m[:], in_=m[:], compare_op=ALU.is_ge, fill=EARLIER, base=0,
                                   pattern=[[-P, W], [1, LB]], channel_multiplier=-1).then_inc(const_ready, 1)

            def group(table, P, cells, weights, g, landed, before):
                if before is not None:
                    wait_apart(pool, landed, before)
                for c in range(W * g, W * g + W):
                    pool.indirect_dma_start(
                        table, bass.IndirectOffsetOnAxis(ap=cells[0:P, c:c + 1], axis=0),
                        weights[0:P, c:c + 1], None, bounds_check=ROWS * N - 1, oob_is_err=True,
                        compute_op=ALU.add).then_inc(landed, 16)

            def scatter_a(batch, slot, first=False):
                wait_apart(pool, cells_a, batch + 1)
                for g in range(GPA):
                    done = (batch - 1) * HALF_A + GROUP * (g // 2)
                    if g % 2 == 0:
                        done += 2 * HALF_A
                    group(tables_a[g % 2], PA, cell_a[:, slot], weight_a[:, slot], g, landed_a[g % 2],
                          None if first and g == 1 else done)

            def scatter_b(batch, slot, first=False):
                wait_apart(pool, cells_b, batch + 1)
                for g in range(GPB):
                    group(tables_b[g % 2], PB, cell_b[:, slot], weight_b[:, slot], g, landed_b[g % 2],
                          None if first and g < 2 else batch * HALF_B + GROUP * (g // 2))

            def add_counts(tables, t, sems):
                wait_apart(pool, sems["half_loaded"], 32 * (t + 1))
                rows = tables[1][ds(t * T * N, T * N), :].rearrange("(p n) o -> p (n o)", p=T)
                for n0, n1 in ((0, N // 2), (N // 2, N)):
                    pool.dma_start(counts[0:T, n0:n1], rows[:, n0:n1], accum_op=ALU.add).then_inc(sems["counts_loaded"], 16)

            for done in zero_a[0]:
                pool.wait_ge(done, 16 * SLICES // IN_FLIGHT)
            wait_apart(pool, cells_a, 1)
            for g in range(GPA):
                group(tables_a[0], PA, cell_a[:, 0], weight_a[:, 0], g, landed_a[0], GROUP * g if g else None)
            for done in zero_a[1]:
                pool.wait_ge(done, 16 * SLICES // IN_FLIGHT)
            scatter_a(1, 1, True)
            scatter_a(2, 0)
            with pool.Fori(1, (NBA - 1) // 2) as i:
                scatter_a(2 * i + 1, 1)
                scatter_a(2 * i + 2, 0)
            pool.wait_ge(zero_b, 2 * 16 * SLICES)
            for n in range(EARLY_B):
                scatter_b(n, n % RING_B, n == 0)
            with pool.Fori(0, NT) as t:
                for j in range(RING_B):
                    scatter_b(RING_B * t + EARLY_B + j, (EARLY_B + j) % RING_B)

            with pool.Fori(0, NT) as t:
                add_counts(tables_b, t, b)

        def turn_and_sum(pe, sems, tiles, v, vpar, h, src_tile, M, first, o_free):
            parts = PARTS[id(sems)]
            n = NSEG * v

            def turn(s):
                for i, (s0, _) in enumerate(parts):
                    if s == s0:
                        pe.wait_ge(sems["exp_done"], len(parts) * v + i + 1)
                if not (first and s < 2):
                    pe.wait_ge(sems["kept"], n + s - 1)
                for j in range(TPS):
                    last = pe.transpose(TP[(vpar * NSEG + s) % 2][0:T, j * T:(j + 1) * T],
                                        tiles[vpar % len(tiles)][0:T, (TPS * s + j) * T:(TPS * s + j + 1) * T],
                                        ident[0:T, 0:T])
                last.then_inc(sems["turned"], 1)

            def sums(s):
                pe.wait_ge(sems["kept"], n + s + 1)
                if s == 0 and o_free is not None:
                    pe.wait_ge(sems["o_kept"], o_free)
                for j in range(TPS):
                    k = TPS * s + j
                    last = pe.matmul(O[0:M, h * T:(h + 1) * T], src_tile(k, h),
                                     PT[0:T, (vpar * NSEG + s) % 4, j * T:(j + 1) * T],
                                     start=(k == 0), stop=(k == NT - 1))
                last.then_inc(sems["av_done"], 1)

            turn(0)
            turn(1)
            for s in range(NSEG):
                sums(s)
                if s + 2 < NSEG:
                    turn(s + 2)

        def keep_turned(act, sems, v, vpar, first, segs=range(NSEG)):
            for s in segs:
                n = NSEG * v + s
                act.wait_ge(sems["turned"], n + 1)
                if not (first and s < 4):
                    act.wait_ge(sems["av_done"], n - 3)
                act.activation(PT[0:T, (vpar * NSEG + s) % 4, :], TP[(vpar * NSEG + s) % 2][0:T, 0:SEG],
                               ACT.Copy).then_inc(sems["kept"], 1)

        def exps(act, sems, tiles, u, h, i=0):
            s0, s1 = PARTS[id(sems)][i]
            if i == 0:
                act.wait_ge(sems["nm_ready"], u + 1)
            tile = tiles[h % len(tiles)][0:T, s0 * SEG:s1 * SEG]
            act.activation(tile, tile, ACT.Exp, bias=nm[0:T, h:h + 1],
                           accum_out=den[0:T, i, h:h + 1]).then_inc(sems["exp_done"], 1)

        @block.tensor
        def _(pe):
            pe.wait_ge(const_ready, CONSTANTS)
            pe.wait_ge(rowkeys_ready, 1)
            for c in range(4):
                last = pe.transpose(S[0:PA, 0, c * QA:(c + 1) * QA], rowkey[0][0:QA, c * PA:(c + 1) * PA],
                                    ident[0:QA, 0:QA])
            last.then_inc(keycols_done, 1)
            pe.wait_ge(rowkeys_ready, 2)
            for c in range(8):
                last = pe.transpose(S[:, 1 + c // 4, (c % 4) * 128:(c % 4 + 1) * 128],
                                    rowkey[1][:, c * 128:(c + 1) * 128], ident[:])
            last.then_inc(keycols_done, 1)

            def project(t, first):
                pe.wait_ge(xn_ready, t + 1)
                if not first:
                    pe.wait_ge(xt_ready, t)
                for k in range(KC):
                    last = pe.transpose(TP[0][:, k * T:(k + 1) * T], xn[0:T, k * 128:(k + 1) * 128],
                                        ident[0:T, 0:T])
                last.then_inc(xn_turned, 1)
                pe.wait_ge(xt_ready, t + 1)
                if not first:
                    pe.wait_ge(proj_kept, 2 * t)
                for w in range(2):
                    for m in range(KC):
                        for k in range(KC):
                            last = pe.matmul(S[:, 3, (w * KC + m) * T:(w * KC + m + 1) * T],
                                             wqk[:, w, k, m * 128:(m + 1) * 128], xt[:, k, :],
                                             start=(k == 0), stop=(k == KC - 1))
                last.then_inc(proj_done, 1)
                for k in range(KC):
                    pe.matmul(S[0:T, 4, :], xt[:, k, :], wvs[:, k, :], start=(k == 0), stop=False)
                pe.matmul(S[0:T, 4, :], ones_row[:, 0:T], bvs[:, :], start=False, stop=True).then_inc(proj_done, 1)

            pe.wait_ge(w_loaded, 16 * 20)
            project(0, True)
            with pe.Fori(1, NT) as t:
                project(t, False)

            def logits(t, h, wait_masked, lent):
                u = H * t + h
                pe.wait_ge(a["qz_ready"], u + 1)
                if wait_masked:
                    pe.wait_ge(a["masked"], u)
                for n, s in enumerate(SEG_ORDER):
                    if s == 0 and lent is not None:
                        pe.wait_ge(*lent)
                    last = pe.matmul(S[0:T, s, 0:SEG], qz[:, h, :], kT[:, h // 2, s * SEG:(s + 1) * SEG],
                                     start=True, stop=True)
                last.then_inc(a["qk_done"], 1)

            values_a = lambda k, h: V[0:T, k, h * C:(h + 1) * C]

            def epi1(t):
                wait_apart(pe, a["o_kept"], H * t + H)
                for h in range(H):
                    last = pe.transpose(S[0:T, 0, h * C:(h + 1) * C], oT[0:C, h, :], ident[0:C, 0:C])
                last.then_inc(a["epi1"], 1)

            def epi2(t):
                pe.wait_ge(a["xn2_ready"], t + 1)
                for k in range(KC):
                    last = pe.transpose(S[:, 0, k * T:(k + 1) * T], xn[0:T, k * 128:(k + 1) * 128],
                                        ident[0:T, 0:T])
                last.then_inc(a["epi2"], 1)

            def epi3(t):
                pe.wait_ge(a["xt2_ready"], t + 1)
                for k in range(KC):
                    last = pe.matmul(S[0:T, 0, 0:16], xt[:, k, :], wg_sb[:, k, :], start=(k == 0), stop=(k == KC - 1))
                last.then_inc(a["epi3"], 1)

            def tile_a(t, first, second):
                for h in range(H):
                    lent = None
                    if h in (1, 3) and not first:
                        pe.wait_ge(a["masked"], H * t + h)
                    if h == 0 and not first and not second:
                        lent = (a["h_kept"], t - 1)
                    if h == 1 and not first:
                        epi1(t - 1)
                        lent = (a["y_ready"], t)
                    if h == 3 and not first:
                        epi2(t - 1)
                        lent = (a["xt2_ready"], t)
                    logits(t, h, not (first and h == 0), lent)
                    if not (first and h == 0):
                        v = H * t + h - 1
                        turn_and_sum(pe, a, L, v, h + 3, (h + 3) % 4, values_a, C, first and h == 1,
                                     None if first or (second and h == 0) else v - 3)
                if not first:
                    pe.wait_ge(a["masked"], H * t + H)
                    epi3(t - 1)

            pe.wait_ge(proj_kept, 2 * NT)
            tile_a(0, True, False)
            tile_a(1, False, True)
            with pe.Fori(2, NT) as t:
                tile_a(t, False, False)
            turn_and_sum(pe, a, L, H * NT - 1, 3, 3, values_a, C, False, H * NT - 4)
            pe.wait_ge(a["h_kept"], NT - 1)
            epi1(NT - 1)
            epi2(NT - 1)
            epi3(NT - 1)
            pe.wait_ge(a["h_kept"], NT)
            pe.transpose(S[0:H * NT, 0, 0:T], s_all[0:T].rearrange("p h t -> p (h t)"), ident[0:T, 0:T]).then_inc(s_turned, 1)

            values_b = lambda k, h: HV[0:T, k, h * NEXP:(h + 1) * NEXP]

            def epi_b(t, first):
                if not first:
                    pe.wait_ge(b["agg_read"], t)
                wait_apart(pe, b["o_kept"], t + 1)
                for h in range(H):
                    last = pe.transpose(S[0:T, 1, h * NEXP:(h + 1) * NEXP], oT[0:NEXP, h, :], ident[0:NEXP, 0:NEXP])
                last.then_inc(b["epi1"], 1)

            def tile_b(t, first):
                for h in range(H):
                    turn_and_sum(pe, b, LB4, H * t + h, h, h, values_b, NEXP, first and h == 0,
                                 t if not first and h == 0 else None)
                epi_b(t, first)

            tile_b(0, True)
            with pe.Fori(1, NT) as t:
                tile_b(t, False)

            pe.wait_ge(w1_loaded, 48)
            pe.wait_ge(b["agg_read"], NT)

            def experts(t, first):
                pe.wait_ge(e_xn, t + 1)
                for k in range(KC):
                    last = pe.transpose(TP[0][:, k * T:(k + 1) * T], xn[0:T, k * 128:(k + 1) * 128],
                                        ident[0:T, 0:T])
                last.then_inc(e_turned, 1)
                pe.wait_ge(e_xt, t + 1)

                def hidden(e):
                    if not (first and e < 2):
                        pe.wait_ge(e_act, NEXP * t + e - 1)
                    for f in range(FC):
                        for k in range(KC):
                            last = pe.matmul(S[:, 1 + e % 2, f * T:(f + 1) * T], w1_sb[:, e, k, f * 128:(f + 1) * 128],
                                             xt[:, k, :], start=(k == 0), stop=(k == KC - 1))
                    last.then_inc(e_hid, 1)

                def output(e):
                    pe.wait_ge(e_act, NEXP * t + e + 1)
                    if not (first and e < 2):
                        pe.wait_ge(e_step, 2 * (NEXP * t + e - 2) + 1)
                    for f in range(FC):
                        last = pe.matmul(S[0:T, 3 + e % 2, 0:D], hid[:, e % 2, f, 0:T], w2_sb[:, e, f, :],
                                         start=(f == 0), stop=(f == FC - 1))
                    last.then_inc(e_out, 1)

                hidden(0)
                for e in range(NEXP):
                    if e + 1 < NEXP:
                        hidden(e + 1)
                    output(e)

            experts(0, True)
            with pe.Fori(1, NT) as t:
                experts(t, False)

        @block.scalar
        def _(act):
            def clear_paced(table, done, slices):
                for t in slices:
                    if t >= IN_FLIGHT:
                        act.wait_ge(done[t % IN_FLIGHT], 16 * (t // IN_FLIGHT))
                    clear(act, table, t, done[t % IN_FLIGHT])

            act.wait_ge(zeros_ready, 1)
            clear_paced(tables_a[0], zero_a[0], range(0, SLICES // 4))
            act.wait_ge(keycols_done, 1)
            act.activation(KA[0:PA].rearrange("p (q c) -> p c q", c=4),
                           S[0:PA, 0, 0:4 * QA].rearrange("p (c q) -> p c q", c=4), ACT.Copy).then_inc(keycols_ready, 1)
            act.wait_ge(keycols_done, 2)
            kb = KB[:].rearrange("p (q c) -> p c q", c=8)
            for i in range(2):
                act.activation(kb[:, 4 * i:4 * i + 4, :], S[:, 1 + i, :].rearrange("p (c q) -> p c q", c=4),
                               ACT.Copy).then_inc(keycols_ready, 1)
            clear_paced(tables_a[0], zero_a[0], range(SLICES // 4, SLICES))
            clear_paced(tables_a[1], zero_a[1], range(0, SLICES))
            act.wait_ge(const_ready, CONSTANTS)
            act.wait_ge(rs_ready, 1)
            act.activation(rs[0:T], mv[0:T, :, 1], ACT.Sqrt, bias=eps[0:T]).then_inc(dev_ready, 1)
            act.wait_ge(rs_ready, 2)
            act.wait_ge(w_loaded, 16 * 20)

            def project(t, first):
                def clear_part(k):
                    clear(act, tables_b[k % 2], SLICES // NT * t + k // 2, zero_b)

                clear_part(0)
                if not first:
                    act.wait_ge(xn_turned, t)
                act.activation(xn[0:T], X[0:T, ds(t, 1), :].rearrange("p a d -> p (a d)"), ACT.Identity,
                               bias=nmr[0:T, ds(t, 1)], scale=rs[0:T, ds(t, 1)]).then_inc(xn_ready, 1)
                act.wait_ge(xn_turned, t + 1)
                clear_part(1)
                if not first:
                    act.wait_ge(proj_done, 2 * t)
                act.activation(xt[:], TP[0][:, 0:KC * T].rearrange("p (k n) -> p k n", k=KC), ACT.Copy).then_inc(xt_ready, 1)
                clear_part(2)
                act.wait_ge(proj_done, 2 * t + 1)
                clear_part(3)
                for w, dst_ap, sc in ((0, qT, 1.0), (1, kT, 1.0)):
                    for m in range(KC):
                        last = act.activation(dst_ap[:, m, ds(t * T, T)], S[:, 3, (w * KC + m) * T:(w * KC + m + 1) * T],
                                              ACT.Identity, bias=bqk[:, w, m:m + 1], scale=sc)
                        if w + m < 2:
                            clear_part(4 + 2 * w + m)
                last.then_inc(proj_kept, 1)
                act.wait_ge(proj_done, 2 * t + 2)
                clear_part(7)
                act.activation(VS[0:T].rearrange("p (w t d) -> p w t d", w=2, t=NT)[:, :, ds(t, 1), :]
                               .rearrange("p w t d -> p w (t d)"),
                               S[0:T, 4, :].rearrange("p (w d) -> p w d", w=2), ACT.Copy).then_inc(proj_kept, 1)

            project(0, True)
            with act.Fori(1, NT) as t:
                project(t, False)

            def copy_q(t, h, wait):
                r = (h % 2) * C
                if wait:
                    act.wait_ge(a["qk_done"], H * (t - 1) + h + 1)
                act.activation(qz[r:r + C, h, :], qT[r:r + C, h // 2, ds(t * T, T)], ACT.Copy, scale=QSCALE)\
                   .then_inc(a["qz_ready"], 1)

            def keep_sums(v, h, wait):
                act.wait_ge(a["av_done"], NSEG * (v + 1))
                if wait is not None:
                    act.wait_ge(a["epi1"], wait)
                act.activation(oT[0:C, h, :], O[0:C, h * T:(h + 1) * T], ACT.Copy).then_inc(a["o_kept"], 1)

            def logs(sems, t):
                act.wait_ge(sems["mask_ready"], t + 1)
                act.activation(counts[0:T], counts[0:T], ACT.Ln, bias=tiny[0:T]).then_inc(sems["ln_ready"], 1)

            def turn_copy(t):
                act.wait_ge(a["epi2"], t + 1)
                act.activation(xt[:], S[:, 0, 0:KC * T].rearrange("p (k n) -> p k n", k=KC), ACT.Copy)\
                   .then_inc(a["xt2_ready"], 1)

            def gelu_of(t):
                act.wait_ge(a["y_ready"], t + 1)
                act.activation(y[0:T], y[0:T], ACT.Gelu).then_inc(a["gelu_done"], 1)
                deviation(t, 0)

            def deviation(t, i):
                act.wait_ge(a["var_ready"], 2 * t + 1 + i)
                act.activation(sm[0:T, 2 + 4 * i:3 + 4 * i], sm[0:T, 1 + 4 * i:2 + 4 * i], ACT.Sqrt, bias=eps[0:T])\
                   .then_inc(a["dev_done"], 1)

            def tile_a(t, first, last):
                for h in range(H):
                    if not (first and h == 0):
                        keep_turned(act, a, H * t + h - 1, h + 3, first and h == 1)
                    if h == 2 and not first:
                        deviation(t - 1, 1)
                    second = isinstance(t, int) and t == 1
                    if h == 0 and not first:
                        keep_sums(H * t - 1, H - 1, None if second else t - 1)
                    exps(act, a, L, H * t + h, h)
                    if h > 0:
                        keep_sums(H * t + h - 1, h - 1, None if first else t)
                    if not last:
                        copy_q(t + 1, h, True)
                    if h == 2 and not first:
                        turn_copy(t - 1)
                    if h == 2 and not last:
                        logs(a, t + 1)
                    if h == 1 and not first:
                        gelu_of(t - 1)

            act.wait_ge(qz_zeroed, 1)
            act.wait_ge(zero_b, 2 * 16 * SLICES)
            act.wait_ge(proj_kept, 2 * NT)
            for h in range(H):
                copy_q(0, h, False)
            logs(a, 0)
            tile_a(0, True, False)
            tile_a(1, False, False)
            with act.Fori(2, NT - 1) as t:
                tile_a(t, False, False)
            tile_a(NT - 1, False, True)
            keep_turned(act, a, H * NT - 1, 3, False)
            keep_sums(H * NT - 1, 3, NT - 1)
            gelu_of(NT - 1)
            deviation(NT - 1, 1)
            turn_copy(NT - 1)
            act.wait_ge(s_turned, 1)
            act.activation(sT[0:H * NT, :], S[0:H * NT, 0, 0:T], ACT.Copy).then_inc(s_kept, 1)

            def keep_sums_b(t, first):
                act.wait_ge(b["av_done"], NSEG * H * (t + 1))
                if not first:
                    act.wait_ge(b["epi1"], t)
                act.activation(oT[0:NEXP], O[0:NEXP, 0:SEG].rearrange("p (h n) -> p h n", h=H), ACT.Copy)\
                   .then_inc(b["o_kept"], 1)

            def tile_b(t, first, last):
                for h in range(H):
                    if not (first and h == 0) and h - 1 != SHARED_HEAD:
                        keep_turned(act, b, H * t + h - 1, h + 3, first and h == 1, range(0, 2))
                    exps(act, b, LB4, H * t + h, h)
                    if not (first and h == 0):
                        if h - 1 == SHARED_HEAD:
                            act.wait_ge(b["kept"], NSEG * (H * t + h - 1) + 2)
                        keep_turned(act, b, H * t + h - 1, h + 3, first and h == 1, range(2, NSEG))
                    if h == 0 and not first:
                        keep_sums_b(t - 1, isinstance(t, int) and t == 1)
                    exps(act, b, LB4, H * t + h, h, 1)
                    if h == 1 and not last:
                        logs(b, t + 1)

            act.wait_ge(a["epi1"], NT)
            act.wait_ge(s_loaded, 16)
            act.wait_ge(a["av_done"], NSEG * H * NT)
            act.wait_ge(a["y_ready"], NT)
            for h in range(2, H):
                act.activation(S_slope[0:T, h, :], S_all[0:T, h, :], ACT.Copy, scale=SLOPE).then_inc(s_scaled, 1)
            logs(b, 0)
            tile_b(0, True, False)
            tile_b(1, False, False)
            with act.Fori(2, NT - 1) as t:
                tile_b(t, False, False)
            tile_b(NT - 1, False, True)
            keep_turned(act, b, H * NT - 1, 3, False)
            keep_sums_b(NT - 1, False)

            act.wait_ge(gvar, 1)
            act.activation(nmr[0:T], nmr[0:T], ACT.Sqrt, bias=eps[0:T]).then_inc(gdev, 1)
            act.wait_ge(gmax, 1)
            act.activation(gate[0:T], gate[0:T], ACT.Exp).then_inc(gexp, 1)

            def experts(t, first):
                act.wait_ge(e_turned, t + 1)
                if not first:
                    act.wait_ge(e_hid, NEXP * t)
                act.activation(xt[:], TP[0][:, 0:KC * T].rearrange("p (k n) -> p k n", k=KC), ACT.Copy).then_inc(e_xt, 1)
                for e in range(NEXP):
                    act.wait_ge(e_hid, NEXP * t + e + 1)
                    if not (first and e < 2):
                        act.wait_ge(e_out, NEXP * t + e - 1)
                    for f in range(FC):
                        last = act.activation(hid[:, e % 2, f, 0:T], S[:, 1 + e % 2, f * T:(f + 1) * T], ACT.Gelu,
                                              bias=b1_sb[:, e, f:f + 1])
                    last.then_inc(e_act, 1)

            experts(0, True)
            with act.Fori(1, NT) as t:
                experts(t, False)

        @block.vector
        def _(v):
            steps = {}

            def step(ins, s=vstep):
                steps[id(s)] = steps.get(id(s), 0) + 1
                ins.then_inc(s, 1)
                v.wait_ge(s, steps[id(s)])

            v.wait_ge(const_ready, CONSTANTS)

            def make_keys(i, dst_i, src_i, P, width):
                key, tmp = rowkey[i][0:P, 0:width], rowtmp[i][0:P, 0:width]
                step(v.tensor_scalar(tmp, dst_i, float(N), None, ALU.min), keystep)
                step(v.tensor_scalar(key, src_i, float(N - 1), None, ALU.min), keystep)
                step(v.scalar_tensor_tensor(key, tmp, float(N), key, ALU.mult, ALU.add), keystep)
                spare = dummyrow[0:P, 0:width]
                outside = out_of_range[0:P, 0:width]
                step(v.tensor_scalar(outside, tmp, float(N), None, ALU.is_ge), keystep)
                step(v.tensor_tensor(tmp, spare, key, ALU.subtract), keystep)
                step(v.tensor_tensor(tmp, tmp, outside, ALU.mult), keystep)
                v.tensor_tensor(key, key, tmp, ALU.add).then_inc(rowkeys_ready, 1)
                v.wait_ge(rowkeys_ready, i + 1)

            v.wait_ge(ea_loaded, 32)
            make_keys(0, ints[0][0:QA, 0:500], ints[0][0:QA, 512:1012], QA, 500)
            v.wait_ge(eb_loaded, 32)
            make_keys(1, ints[1][:, :], QK[:, 0:1024].bitcast(I32), 128, 1024)

            def compare(batch, rows, K, order, spare, P, groups, loaded, loaded_by, stepper, cells, weights, done,
                        landed, before):
                v.wait_ge(loaded, loaded_by)
                for s, value in landed:
                    v.wait_ge(s, value)
                for s, value in before:
                    v.wait_ge(s, value)
                n, width = W * groups, W * P
                for c in range(n):
                    g = c // W
                    if c >= 4:
                        v.wait_ge(stepper, batch * (n + 2) + c - 3)
                    v.scalar_tensor_tensor(equal[0:P, c % 4, 0:width], rows[0:P, g * width:(g + 1) * width],
                                           K[0:P, ds(batch * n + c, 1)], order[0:P, c % W, 0:width],
                                           ALU.is_equal, ALU.mult, accum_out=weights[0:P, c:c + 1])\
                     .then_inc(stepper, 1)
                v.wait_ge(stepper, batch * (n + 2) + n)
                v.tensor_tensor(shift[0:P, 0:n], spare[0:P], K[0:P, ds(batch * n, n)], ALU.subtract).then_inc(stepper, 1)
                v.wait_ge(stepper, batch * (n + 2) + n + 1)
                v.scalar_tensor_tensor(moved[0:P, 0:n], weights[0:P], EARLIER, shift[0:P, 0:n], ALU.is_ge, ALU.mult)\
                 .then_inc(stepper, 1)
                v.wait_ge(stepper, batch * (n + 2) + n + 2)
                v.tensor_tensor(cells[0:P], moved[0:P, 0:n], K[0:P, ds(batch * n, n)], ALU.add).then_inc(done, 1)

            def compare_a(batch, slot, turn, landed, before):
                compare(batch, keyrow_a[slot], KA, order_a, spare_a, PA, GPA, row_a[slot], 32 * (turn + 1), step_a,
                        cell_a[:, slot], weight_a[:, slot], cells_a, landed, before)

            def compare_b(batch, slot, turn, landed, before):
                compare(batch, keyrow_b[:, slot], KB, order_b, spare_b, PB, GPB, row_b[slot], 32 * (turn + 1), step_b,
                        cell_b[:, slot], weight_b[:, slot], cells_b, landed, before)

            v.wait_ge(keycols_ready, 3)
            compare_a(0, 0, 0, [], [])
            compare_a(1, 1, 0, [], [(cells_a, 1)])
            compare_a(2, 0, 1, [(landed_a[0], 2 * HALF_A)], [(cells_a, 2)])
            v.wait_ge(x_loaded, 16)
            for t in range(NT):
                step(v.bn_stats(stats[0:T], X[0:T, t, :]))
                if t < NT - 1:
                    step(v.bn_aggr(mv[0:T, t, :], stats[0:T]))
            v.bn_aggr(mv[0:T, NT - 1, :], stats[0:T]).then_inc(rs_ready, 1)
            v.wait_ge(dev_ready, 1)
            step(v.reciprocal(rs[0:T], rs[0:T]))
            step(v.tensor_tensor(nmr[0:T], mv[0:T, :, 0], rs[0:T], ALU.mult))
            v.tensor_scalar(nmr[0:T], nmr[0:T], -1.0, None, ALU.mult).then_inc(rs_ready, 1)
            compare_b(0, 0, 0, [], [(cells_a, 3)])

            def sent_a(batch):
                return [(landed_a[0], batch * HALF_A), (landed_a[1], (batch - RING_A) * HALF_A)]

            with v.Fori(1, (NBA - 1) // 2) as i:
                compare_a(2 * i + 1, 1, i, sent_a(2 * i + 1), [(cells_a, 2 * i + 1), (cells_b, 1)])
                compare_a(2 * i + 2, 0, i + 1, sent_a(2 * i + 2), [(cells_a, 2 * i + 2)])

            for j in range(1, RING_B):
                compare_b(j, j, 0, [], [(cells_a, NBA) if j == 1 else (cells_b, j)])

            def compare_late(batch, slot, turn):
                done = (batch - RING_B + 1) * HALF_B
                compare_b(batch, slot, turn, [(landed_b[0], done), (landed_b[1], done)], [(cells_b, batch)])

            def mask_of(sems, t, first):
                if sems is a:
                    v.wait_ge(a["counts_loaded"], 128 * (t + 1))
                    for half in range(2):
                        part = counts[0:T, half * N // 2:(half + 1) * N // 2]
                        v.tensor_tensor(part, part, more[half][0:T], ALU.add).then_inc(a["added"], 1)
                    v.wait_ge(a["added"], 2 * t + 2)
                if not first:
                    v.wait_ge(sems["lnc_ready"], t)
                v.tensor_scalar(mask[0:T], counts[0:T], 0.0, NEG, ALU.is_equal, ALU.mult).then_inc(sems["mask_ready"], 1)

            def lnc_of(sems, t):
                v.wait_ge(sems["ln_ready"], t + 1)
                v.tensor_tensor(lnc[0:T], mask[0:T], counts[0:T], ALU.add).then_inc(sems["lnc_ready"], 1)

            def row_max(sems, u, t, tile_L, h, in0, warm, close_last):
                wait_apart(v, sems["lnc_ready"], t + 1)
                v.tensor_tensor_reduce(out=tile_L[0:T].rearrange("p (s n) -> p s n", s=NSEG), in0=in0,
                                       in1=lnc[0:T].rearrange("p (s n) -> p s n", s=NSEG), scale=1.0, scalar=NEG,
                                       op0=ALU.add, op1=ALU.max, accum_out=mx[0:T, h:h + 1]).then_inc(sems["masked"], 1)
                if close_last:
                    denominators(sems, t - 1)
                v.wait_ge(sems["masked"], u + 1)
                if warm:
                    v.wait_ge(sems["exp_done"], len(PARTS[id(sems)]) * (u - H + 1))
                v.tensor_scalar(nm[0:T, h:h + 1], mx[0:T, h:h + 1], NEG_FLOOR, -1.0, ALU.max, ALU.mult)\
                 .then_inc(sems["nm_ready"], 1)

            LINKS = 8

            def divide_a(t):
                v.wait_ge(a["epi1"], t + 1)
                skip = SK[0:T, ds(t, 1), :].rearrange("p a d -> p (a d)")
                for h in range(H):
                    last = v.scalar_tensor_tensor(y[0:T, h * C:(h + 1) * C], S[0:T, 0, h * C:(h + 1) * C],
                                                  rden[0:T, h:h + 1], skip[:, h * C:(h + 1) * C], ALU.mult, ALU.add)
                last.then_inc(a["y_ready"], 1)

            def finish_a(t):
                n = [0]

                def link(ins):
                    n[0] += 1
                    ins.then_inc(a["vs"], 1)
                    wait_apart(v, a["vs"], LINKS * t + n[0])

                v.wait_ge(a["gelu_done"], t + 1)
                link(v.bn_stats(stats[0:T], y[0:T]))
                v.bn_aggr(sm[0:T, 0:2], stats[0:T]).then_inc(a["var_ready"], 1)
                v.wait_ge(a["dev_done"], 2 * t + 1)
                link(v.reciprocal(sm[0:T, 3:4], sm[0:T, 2:3]))
                link(v.tensor_scalar(z[0:T], y[0:T], sm[0:T, 0:1], sm[0:T, 3:4], ALU.subtract, ALU.mult))
                link(v.tensor_tensor(z[0:T], z[0:T], rows_ln[0:T, 0], ALU.mult))
                link(v.tensor_tensor(z[0:T], z[0:T], rows_ln[0:T, 1], ALU.add))
                xrow = X[0:T, ds(t, 1), :].rearrange("p a d -> p (a d)")
                link(v.tensor_tensor(xrow, z[0:T], xrow, ALU.add))
                link(v.bn_stats(stats[0:T], xrow))
                v.bn_aggr(sm[0:T, 4:6], stats[0:T]).then_inc(a["var_ready"], 1)
                assert n[0] == LINKS - 1

            def norm_a(t):
                xrow = X[0:T, ds(t, 1), :].rearrange("p a d -> p (a d)")
                v.wait_ge(a["dev_done"], 2 * t + 2)
                v.reciprocal(sm[0:T, 7:8], sm[0:T, 6:7]).then_inc(a["vs"], 1)
                wait_apart(v, a["vs"], LINKS * t + LINKS)
                v.tensor_copy(rs[0:T, ds(t, 1)], sm[0:T, 7:8])
                v.tensor_copy(mv[0:T, ds(t, 1), 0:1].rearrange("p a b -> p (a b)"), sm[0:T, 4:5])
                v.tensor_scalar(xn[0:T], xrow, sm[0:T, 4:5], sm[0:T, 7:8], ALU.subtract, ALU.mult)\
                 .then_inc(a["xn2_ready"], 1)

            def keep_h(t):
                v.wait_ge(a["epi3"], t + 1)
                hrow = HV[0:T, ds(t, 1), :].rearrange("p a d -> p (a d)")
                v.tensor_copy(hrow, S[0:T, 0, 0:16])
                for i in range(2):
                    last = v.tensor_tensor(prod[0:T, i], S[0:T, 0, 0:16], att[0:T, i], ALU.mult)
                last.then_inc(b["x2_ready"], 1)
                v.wait_ge(b["x2_ready"], t + 1)
                v.tensor_reduce(s_all[0:T, :, ds(t, 1)].rearrange("p h a -> p (h a)"),
                                prod[0:T, 0].rearrange("p (h e) -> p h e", h=H), AX_X, ALU.add)
                v.tensor_reduce(t_all[0:T, ds(t, 1), :].rearrange("p a h -> p (a h)"),
                                prod[0:T, 1].rearrange("p (h e) -> p h e", h=H), AX_X, ALU.add).then_inc(a["h_kept"], 1)

            def denominators(sems, t, pair=None):
                heads, n = (slice(0, H), 2 * t) if pair is None else (slice(2 * pair, 2 * pair + 2), 4 * t + 2 * pair)
                parts = len(PARTS[id(sems)])
                v.wait_ge(sems["exp_done"], parts * (H * t + heads.stop))
                if parts == 1:
                    v.tensor_scalar(rden[0:T, heads], den[0:T, 0, heads], 1e-16, None, ALU.add).then_inc(sems["summed"], 1)
                else:
                    v.scalar_tensor_tensor(rden[0:T, heads], den[0:T, 0, heads], 1e-16, den[0:T, 1, heads],
                                           ALU.add, ALU.add).then_inc(sems["summed"], 1)
                v.wait_ge(sems["summed"], n + 1)
                v.reciprocal(rden[0:T, heads], rden[0:T, heads]).then_inc(sems["summed"], 1)
                v.wait_ge(sems["summed"], n + 2)

            PLACES = {0: (0,), 1: (1,), 2: (), 3: (2,)}

            def tile_a(t, first, last):
                for h in range(H):
                    u = H * t + h
                    if h == 1 and not first:
                        divide_a(t - 1)
                    v.wait_ge(a["qk_done"], u + 1)
                    if not (first and h < 2):
                        v.wait_ge(a["turned"], NSEG * (u - 1))
                    row_max(a, u, t, L[h % 2], h, S[0:T, :, 0:SEG], not first, h == 0 and not first)
                    if h == 2 and not first:
                        norm_a(t - 1)
                    if h == 2 and not last:
                        mask_of(a, t + 1, False)
                    if h == 3 and not last:
                        v.wait_ge(a["masked"], u + 1)
                        lnc_of(a, t + 1)
                    if first and h == 0:
                        for n in range(RING_B, EARLY_B):
                            compare_late(n, n % RING_B, n // RING_B)
                    for j in PLACES[h]:
                        m = EARLY_B + j
                        compare_late(RING_B * t + m, m % RING_B, t + m // RING_B)
                    if h == 1 and not first:
                        finish_a(t - 1)
                if not first:
                    keep_h(t - 1)

            mask_of(a, 0, True)
            lnc_of(a, 0)
            tile_a(0, True, False)
            with v.Fori(1, NT - 1) as t:
                tile_a(t, False, False)
            tile_a(NT - 1, False, True)
            denominators(a, NT - 1)
            divide_a(NT - 1)
            finish_a(NT - 1)
            norm_a(NT - 1)
            keep_h(NT - 1)

            def diagonal(t):
                v.wait_ge(b["counts_loaded"], 32 * (t + 1))
                block_t = counts[0:T, ds(t * T, T)]
                v.tensor_tensor(block_t, block_t, ident[0:T, 0:T], ALU.add).then_inc(b["y_ready"], 1)
                v.wait_ge(b["y_ready"], t + 1)

            def read_sums(t):
                v.wait_ge(b["epi1"], t + 1)
                for h in range(H):
                    last = v.tensor_scalar(agg[0:T, ds(t, 1), h * NEXP:(h + 1) * NEXP].rearrange("p a e -> p (a e)"),
                                           S[0:T, 1, h * NEXP:(h + 1) * NEXP], rden[0:T, h:h + 1], None, ALU.mult)
                last.then_inc(b["agg_read"], 1)

            def keep_first(t):
                n = NSEG * (H * t + SHARED_HEAD)
                for s in range(2):
                    v.wait_ge(b["turned"], n + s + 1)
                    v.wait_ge(b["av_done"], n + s - 3)
                    k = SHARED_HEAD * NSEG + s
                    v.tensor_copy(PT[0:T, k % 4, :], TP[k % 2][0:T, 0:SEG]).then_inc(b["kept"], 1)

            def tile_b(t, first, last):
                for h in range(H):
                    u = H * t + h
                    e = LB4[h][0:T]
                    if not first:
                        v.wait_ge(b["turned"], NSEG * (u - H + 1))
                    v.scalar_tensor_tensor(e, S_all[0:T, h, :],
                                           t_all[0:T, ds(t, 1), h:h + 1].rearrange("p a b -> p (a b)"),
                                           S_slope[0:T, h, :], ALU.add, ALU.max).then_inc(b["vs"], 1)
                    v.wait_ge(b["vs"], u + 1)
                    row_max(b, u, t, LB4[h], h, e.rearrange("p (s n) -> p s n", s=NSEG), not first, False)
                    if h == 1 and not first:
                        denominators(b, t - 1, 1)
                    if h == 1 and not last:
                        diagonal(t + 1)
                        mask_of(b, t + 1, False)
                    if h == 3:
                        keep_first(t)
                    if h == 3 and not last:
                        v.wait_ge(b["masked"], u + 1)
                        lnc_of(b, t + 1)
                    if h == 2 and not first:
                        read_sums(t - 1)
                    if h == 3:
                        denominators(b, t, 0)

            v.wait_ge(a["h_kept"], NT)
            v.tensor_scalar(t_all[0:T], t_all[0:T], 1.0 - SLOPE, None, ALU.mult).then_inc(s_scaled, 1)
            v.wait_ge(s_loaded, 16)
            v.wait_ge(a["av_done"], NSEG * H * NT)
            for h in range(2):
                v.tensor_scalar(S_slope[0:T, h, :], S_all[0:T, h, :], SLOPE, None, ALU.mult).then_inc(s_scaled, 1)
            diagonal(0)
            mask_of(b, 0, True)
            lnc_of(b, 0)
            v.wait_ge(s_scaled, H + 1)
            tile_b(0, True, False)
            with v.Fori(1, NT - 1) as t:
                tile_b(t, False, False)
            tile_b(NT - 1, False, True)
            denominators(b, NT - 1, 1)
            read_sums(NT - 1)
            v.wait_ge(b["agg_read"], NT)

            def over_tiles(row16):
                return row16.rearrange("p (a n) -> p a n", a=1).broadcast_to([T, NT, 16])

            def over_cols(col, n):
                return col.rearrange("p (t a) -> p t a", a=1).broadcast_to([T, NT, n])

            G = agg[0:T]
            big = L[0][0:T, 0:NT * 16].rearrange("p (t n) -> p t n", t=NT)
            mean = L[0][0:T, 400:400 + NT]
            step(v.tensor_tensor(G, G, over_tiles(gat_rows[0:T, 0]), ALU.add), gstep)
            step(v.tensor_reduce(mean, G, AX_X, ALU.add), gstep)
            step(v.tensor_scalar(mean, mean, 1.0 / 16, None, ALU.mult), gstep)
            step(v.tensor_tensor(G, G, over_cols(mean, 16), ALU.subtract), gstep)
            step(v.tensor_tensor(big, G, G, ALU.mult), gstep)
            var = L[0][0:T, 500:500 + NT]
            step(v.tensor_reduce(var, big, AX_X, ALU.add), gstep)
            v.tensor_scalar(nmr[0:T], var, 1.0 / 16, None, ALU.mult).then_inc(gvar, 1)
            v.wait_ge(gdev, 1)
            step(v.reciprocal(var, nmr[0:T]), gstep)
            step(v.tensor_tensor(G, G, over_cols(var, 16), ALU.mult), gstep)
            step(v.tensor_tensor(G, G, over_tiles(gat_rows[0:T, 1]), ALU.mult), gstep)
            step(v.tensor_tensor(G, G, over_tiles(gat_rows[0:T, 2]), ALU.add), gstep)
            score = L[0][0:T, 700:700 + NT * NEXP].rearrange("p (t e) -> p t e", t=NT)
            step(v.tensor_reduce(score, G.rearrange("p t (h e) -> p t e h", h=H), AX_X, ALU.add), gstep)
            step(v.tensor_scalar(score, score, 1.0 / H, None, ALU.mult), gstep)
            rank = L[0][0:T, 800:800 + NT * NEXP].rearrange("p (t e) -> p t e", t=NT)
            beats = L[0][0:T, 900:900 + NT * NEXP].rearrange("p (t e) -> p t e", t=NT)
            step(v.memset(rank, 0.0), gstep)
            for e in range(NEXP):
                other = score[:, :, e:e + 1]
                step(v.tensor_tensor(beats, other.broadcast_to([T, NT, NEXP]), score, ALU.is_gt), gstep)
                step(v.tensor_tensor(rank, rank, beats, ALU.add), gstep)
                if e + 1 < NEXP:
                    n_after = NEXP - e - 1
                    step(v.tensor_tensor(beats[:, :, 0:n_after], other.broadcast_to([T, NT, n_after]),
                                         score[:, :, e + 1:], ALU.is_equal), gstep)
                    step(v.tensor_tensor(rank[:, :, e + 1:], rank[:, :, e + 1:], beats[:, :, 0:n_after], ALU.add), gstep)
            best = L[0][0:T, 1000:1000 + NT]
            step(v.tensor_reduce(best, score, AX_X, ALU.max), gstep)
            v.tensor_tensor(gate[0:T], score, over_cols(best, NEXP), ALU.subtract).then_inc(gmax, 1)
            v.wait_ge(gexp, 1)
            step(v.tensor_scalar(rank, rank, 2.0, None, ALU.is_lt), gstep)
            step(v.tensor_tensor(gate[0:T], gate[0:T], rank, ALU.mult), gstep)
            step(v.tensor_reduce(best, gate[0:T], AX_X, ALU.add), gstep)
            step(v.reciprocal(best, best), gstep)
            step(v.tensor_tensor(gate[0:T], gate[0:T], over_cols(best, NEXP), ALU.mult), gstep)

            def norm_again(t):
                xrow = X[0:T, ds(t, 1), :].rearrange("p a d -> p (a d)")
                v.tensor_scalar(xn[0:T], xrow, mv[0:T, ds(t, 1), 0:1].rearrange("p a b -> p (a b)"),
                                rs[0:T, ds(t, 1)], ALU.subtract, ALU.mult).then_inc(e_xn, 1)

            def experts(t, first, last):
                xrow = X[0:T, ds(t, 1), :].rearrange("p a d -> p (a d)")
                for e in range(NEXP):
                    n = 2 * (NEXP * t + e)
                    if e == 1 and not last:
                        v.wait_ge(e_turned, t + 1)
                        norm_again(t + 1)
                    v.wait_ge(e_out, NEXP * t + e + 1)
                    if not (first and e == 0):
                        v.wait_ge(e_step, n)
                    if e == 0 and not first:
                        v.wait_ge(stored, 16 * t)
                    v.tensor_tensor(z[0:T], S[0:T, 3 + e % 2, 0:D], b2_sb[0:T, e], ALU.add).then_inc(e_step, 1)
                    v.wait_ge(e_step, n + 1)
                    v.scalar_tensor_tensor(y[0:T], z[0:T], gate[0:T, ds(t, 1), e:e + 1].rearrange("p a b -> p (a b)"),
                                           xrow if e == 0 else y[0:T], ALU.mult, ALU.add).then_inc(e_step, 1)

            norm_again(0)
            experts(0, True, False)
            with v.Fori(1, NT - 1) as t:
                experts(t, False, False)
            experts(NT - 1, False, True)


_ORDER = ["x", "src", "dst", "L0_gnn_Wq", "L0_gnn_bq", "L0_gnn_Wk", "L0_gnn_bk", "L0_gnn_Wv", "L0_gnn_bv",
          "L0_gnn_Wskip", "L0_gnn_bskip", "L0_gnn_gamma", "L0_gnn_beta_ln", "L0_ffn_W_gat", "L0_ffn_att_src",
          "L0_ffn_att_dst", "L0_ffn_b_gat", "L0_ffn_ln_gamma", "L0_ffn_ln_beta", "L0_ffn_W1", "L0_ffn_b1",
          "L0_ffn_W2", "L0_ffn_b2", "L0_ffn_edge_index"]


def kernel(**inputs):
    import numpy as np
    import concourse.bacc as bacc
    from concourse.bass_utils import run_bass_kernel_spmd

    nc = bacc.Bacc("TRN2", target_bir_lowering=False, num_devices=1)
    arrays, args = {}, []
    for name in _ORDER:
        arr = np.ascontiguousarray(inputs[name])
        arrays[f"in_{name}"] = arr
        args.append(nc.dram_tensor(f"in_{name}", arr.shape, mybir.dt.from_np(arr.dtype), kind="ExternalInput").ap())
    out = nc.dram_tensor("out_0", (N, D), F32, kind="ExternalOutput").ap()
    build(nc, *args, out)
    r = run_bass_kernel_spmd(nc, [arrays], core_ids=[0])
    return r.results[0]["out_0"]
```
